# Optimizing a Trainium2 kernel written in Bass

```python
import numpy as np
import jax
import jax.numpy as jnp

def _softmax(x, axis=-1):
    return jax.nn.softmax(x, axis=axis)

def _gelu(x):
    return jax.nn.gelu(x, approximate=True)

def _silu(x):
    return jax.nn.silu(x)

def _sigmoid(x):
    return jax.nn.sigmoid(x)

def _layernorm(x, axis=-1, eps=1e-05):
    m = jnp.mean(x, axis=axis, keepdims=True)
    v = jnp.var(x, axis=axis, keepdims=True)
    return (x - m) / jnp.sqrt(v + eps)

def _scatter_add(tgt, idx, src, axis=0):
    return tgt.at[idx].add(src)

def _segment_sum(src, seg, n):
    return jax.ops.segment_sum(src, seg, n)
kernel_name = 'mk_decoder_preln_d2_seqx_r4_4f2998'

def setup_inputs(seed: int=0):
    np.random.seed(seed)
    _w = jnp.asarray

    def _rec_inputs():
        import jax
        import jax.numpy as jnp
        _rk = jax.random.key(seed)
        x = -0.0002928 + 1 * jax.random.normal(jax.random.fold_in(_rk, 1), (2, 1024, 256), jnp.float32)
        _lenS = 1024 - jax.random.randint(jax.random.fold_in(_rk, 7), (2,), 0, max(1, 1024 // 4) + 1, jnp.int32)
        _lenS2 = 64 - jax.random.randint(jax.random.fold_in(_rk, 8), (2,), 0, max(1, 64 // 4) + 1, jnp.int32)
        _ctx_1024P = jax.random.normal(jax.random.fold_in(_rk, 11), (2, 16, 256), jnp.float32)
        _ctx_1024c = jax.random.dirichlet(jax.random.fold_in(_rk, 511), 0.3 * jnp.ones((16,), jnp.float32), (2, 64))
        _ctx_1024t = jnp.einsum('bsk,bkd->bsd', _ctx_1024c, _ctx_1024P)
        _ctx_1024t = _ctx_1024t * jax.lax.rsqrt(jnp.mean(jnp.square(_ctx_1024t)) + 1e-12) * 0.953939
        ctx_1024 = 0.00222621 + 0.99962 * (_ctx_1024t + 0.3 * jax.random.normal(jax.random.fold_in(_rk, 611), (2, 64, 256), jnp.float32))
        itok_BxS_0_255 = jax.random.randint(jax.random.fold_in(_rk, 12), (2, 1024), 0, 64, jnp.int32)
        return (x, ctx_1024, itok_BxS_0_255)
    x, ctx_1024, itok_BxS_0_255 = _rec_inputs()

    def _L0_attn_setup():
        import jax, jax.numpy as jnp
        import numpy as np
        MAX_DIST = 8
        GUIDANCE_WEIGHT = 0.4
        EPS_MAG = 1e-06
        EPS_COS = 1e-08
        EPS_WSUM = 1e-08
        key = jax.random.key(seed)
        k1, k2 = jax.random.split(key)
        embeddings = jax.random.normal(k1, (4, 512, 256), dtype=jnp.float32)
        guidance_trajectories = jax.random.normal(k2, (128, 256), dtype=jnp.float32)
        return {'embeddings': embeddings, 'guidance_trajectories': guidance_trajectories}
    _L0_attn_all = _L0_attn_setup()
    _L0_attn_in = {k: v for k, v in _L0_attn_all.items() if k in ('guidance_trajectories',)}
    del _L0_attn_all

    def _L0_xattn_setup():
        import jax, jax.numpy as jnp
        import numpy as np
        N_LAYERS = 4
        H = 16
        LOOKBACK = 128
        EPS = 1e-06
        ROPE_BASE = 10000.0
        NEG = jnp.float32(-1e+30)

        def rmsnorm(x, w):
            return x * jax.lax.rsqrt(jnp.mean(x * x, axis=-1, keepdims=True) + EPS) * w

        def rope_cache(L, hd):
            inv = 1.0 / ROPE_BASE ** (jnp.arange(0, hd, 2, dtype=jnp.float32) / hd)
            t = jnp.arange(L, dtype=jnp.float32)
            f = t[:, None] * inv[None, :]
            emb = jnp.concatenate([f, f], axis=-1)
            return (jnp.cos(emb), jnp.sin(emb))

        def apply_rope(x, cos, sin):
            d = x.shape[-1]
            x1, x2 = (x[..., :d // 2], x[..., d // 2:])
            rot = jnp.concatenate([-x2, x1], axis=-1)
            return x * cos + rot * sin

        def split_heads(x, n_heads):
            B, L, D = x.shape
            return x.reshape(B, L, n_heads, D // n_heads).transpose(0, 2, 1, 3)

        def merge_heads(x):
            B, h, L, d = x.shape
            return x.transpose(0, 2, 1, 3).reshape(B, L, h * d)

        def sdpa(q, k, v, bias):
            scale = q.shape[-1] ** (-0.5)
            s = jnp.einsum('bhqd,bhkd->bhqk', q, k) * scale + bias
            p = jax.nn.softmax(s, axis=-1)
            return jnp.einsum('bhqk,bhkd->bhqd', p, v)

        def forward(x, memory, seg_ids, Wqkv, bqkv, Wo, bo, Wq_c, Wkv_c, Wo_c, Wg, Wu, Wd, n1, n2, n3, nf):
            B, L, D = x.shape
            S = memory.shape[1]
            hd = D // H
            cos, sin = rope_cache(L, hd)
            i = jnp.arange(L)
            causal_bias = jnp.where(i[None, :] <= i[:, None], 0.0, NEG)[None, None]
            j = jnp.arange(S)
            allowed = (j[None, None, :] <= seg_ids[:, :, None]) & (j[None, None, :] > seg_ids[:, :, None] - LOOKBACK)
            cross_bias = jnp.where(allowed, 0.0, NEG)[:, None]
            for l in range(N_LAYERS):
                h = rmsnorm(x, n1[l])
                qkv = h @ Wqkv[l].T + bqkv[l]
                q, k, v = jnp.split(qkv, 3, axis=-1)
                q = apply_rope(split_heads(q, H), cos, sin)
                k = apply_rope(split_heads(k, H), cos, sin)
                v = split_heads(v, H)
                o = merge_heads(sdpa(q, k, v, causal_bias)) @ Wo[l].T + bo[l]
                x = x + o
                h2 = rmsnorm(x, n2[l])
                qc = split_heads(h2 @ Wq_c[l].T, H)
                kv = memory @ Wkv_c[l].T
                kc, vc = jnp.split(kv, 2, axis=-1)
                kc, vc = (split_heads(kc, H), split_heads(vc, H))
                oc = merge_heads(sdpa(qc, kc, vc, cross_bias)) @ Wo_c[l].T
                x = x + oc
                h3 = rmsnorm(x, n3[l])
                x = x + jax.nn.silu(h3 @ Wg[l].T) * (h3 @ Wu[l].T) @ Wd[l].T
            return rmsnorm(x, nf)
        key = jax.random.key(seed)
        ks = jax.random.split(key, 16)
        B, L, S, D, F = (2, 512, 64, 256, 1024)
        w = 0.02
        inp = {'x': jax.random.normal(ks[0], (B, L, D), jnp.float32), 'memory': jax.random.normal(ks[1], (B, S, D), jnp.float32), 'seg_ids': jnp.sort(jax.random.randint(ks[2], (B, L), 0, S), axis=-1), 'Wqkv': jax.random.normal(ks[3], (N_LAYERS, 3 * D, D), jnp.float32) * w, 'bqkv': jnp.zeros((N_LAYERS, 3 * D), jnp.float32), 'Wo': jax.random.normal(ks[4], (N_LAYERS, D, D), jnp.float32) * w, 'bo': jnp.zeros((N_LAYERS, D), jnp.float32), 'Wq_c': jax.random.normal(ks[5], (N_LAYERS, D, D), jnp.float32) * w, 'Wkv_c': jax.random.normal(ks[6], (N_LAYERS, 2 * D, D), jnp.float32) * w, 'Wo_c': jax.random.normal(ks[7], (N_LAYERS, D, D), jnp.float32) * w, 'Wg': jax.random.normal(ks[8], (N_LAYERS, F, D), jnp.float32) * w, 'Wu': jax.random.normal(ks[9], (N_LAYERS, F, D), jnp.float32) * w, 'Wd': jax.random.normal(ks[10], (N_LAYERS, D, F), jnp.float32) * w, 'n1': jnp.ones((N_LAYERS, D), jnp.float32), 'n2': jnp.ones((N_LAYERS, D), jnp.float32), 'n3': jnp.ones((N_LAYERS, D), jnp.float32), 'nf': jnp.ones((D,), jnp.float32)}
        return inp
    _L0_xattn_all = _L0_xattn_setup()
    _L0_xattn_in = {k: v for k, v in _L0_xattn_all.items() if k in ('Wqkv', 'bqkv', 'Wo', 'bo', 'Wq_c', 'Wkv_c', 'Wo_c', 'Wg', 'Wu', 'Wd', 'n1', 'n2', 'n3', 'nf')}
    del _L0_xattn_all

    def _L0_ffn_setup():
        import jax, jax.numpy as jnp
        import numpy as np
        HIDDEN = 256
        HEAD_DIM = 64
        N_EXPERTS = 16
        MIN_EXPERTS = 2
        B, T = (4, 512)

        def _normalize(x, axis):
            n = jnp.sqrt(jnp.sum(x * x, axis=axis, keepdims=True))
            return x / jnp.maximum(n, 1e-12)

        def _ste(x):
            hard = jax.lax.stop_gradient((x > 0).astype(x.dtype))
            return hard + x - jax.lax.stop_gradient(x)

        def _gating(hidden_states, sim_matrix, gates):
            b, t, c = hidden_states.shape
            flat = hidden_states.reshape(b * t, c)
            logits = _normalize(flat, -1) @ _normalize(sim_matrix, 0) - jax.nn.sigmoid(gates)
            gated = jax.nn.relu(logits)
            mask = _ste(gated)
            inactive = jnp.sum(mask, axis=1) == 0
            _, fb_idx = jax.lax.top_k(logits, MIN_EXPERTS)
            fb = jnp.zeros_like(mask).at[jnp.arange(b * t)[:, None], fb_idx].set(1.0)
            fb_applied = inactive[:, None] & (fb > 0)
            mask = jnp.where(fb_applied, 1.0, mask)
            masked_logits = jnp.where(mask > 0, gated, -jnp.inf)
            return jax.nn.softmax(masked_logits, axis=-1).reshape(b, t, -1)
        key = jax.random.key(seed)
        ks = jax.random.split(key, 6)
        xav_qkv = float(np.sqrt(6.0 / (HIDDEN + HEAD_DIM)))
        return {'hidden_states': jax.random.normal(ks[0], (B, T, HIDDEN), dtype=jnp.float32), 'sim_matrix': jax.random.normal(ks[1], (HIDDEN, N_EXPERTS), dtype=jnp.float32), 'gates': jnp.zeros((N_EXPERTS,), dtype=jnp.float32), 'q_proj': jax.random.uniform(ks[2], (N_EXPERTS, HIDDEN, HEAD_DIM), jnp.float32, -xav_qkv, xav_qkv), 'k_proj': jax.random.uniform(ks[3], (N_EXPERTS, HIDDEN, HEAD_DIM), jnp.float32, -xav_qkv, xav_qkv), 'v_proj': jax.random.uniform(ks[4], (N_EXPERTS, HIDDEN, HEAD_DIM), jnp.float32, -xav_qkv, xav_qkv), 'o_proj': jax.random.uniform(ks[5], (N_EXPERTS, HEAD_DIM, HIDDEN), jnp.float32, -xav_qkv, xav_qkv)}
    _L0_ffn_all = _L0_ffn_setup()
    _L0_ffn_in = {k: v for k, v in _L0_ffn_all.items() if k in ('sim_matrix', 'gates', 'q_proj', 'k_proj', 'v_proj', 'o_proj')}
    del _L0_ffn_all

    def _L1_attn_setup():
        import jax, jax.numpy as jnp
        import numpy as np
        D_MODEL = 256
        NUM_HEADS = 16
        HEAD_DIM = D_MODEL // NUM_HEADS
        key = jax.random.key(seed)
        ks = jax.random.split(key, 7)
        B, T, C = (4, 512, D_MODEL)
        s = 1.0 / np.sqrt(C)
        return {'x': jax.random.normal(ks[0], (B, T, C), dtype=jnp.float32), 'ln_gamma': jnp.ones((C,), dtype=jnp.float32), 'ln_beta': jnp.zeros((C,), dtype=jnp.float32), 'w_qkv': jax.random.normal(ks[1], (C, 3 * C), dtype=jnp.float32) * s, 'b_qkv': jnp.zeros((3 * C,), dtype=jnp.float32), 'w_out': jax.random.normal(ks[2], (C, C), dtype=jnp.float32) * s, 'b_out': jnp.zeros((C,), dtype=jnp.float32)}
    _L1_attn_all = _L1_attn_setup()
    _L1_attn_in = {k: v for k, v in _L1_attn_all.items() if k in ('ln_gamma', 'ln_beta', 'w_qkv', 'b_qkv', 'w_out', 'b_out')}
    del _L1_attn_all

    def _L1_xattn_setup():
        import jax, jax.numpy as jnp
        import numpy as np
        D = 256
        H = 16
        DH = D // H
        key = jax.random.key(seed)
        ks = jax.random.split(key, 11)
        B, T = (4, 512)
        s = 0.02
        return {'q': jax.random.normal(ks[0], (B, T, D), jnp.float32), 'k': jax.random.normal(ks[1], (B, T, D), jnp.float32), 'v': jax.random.normal(ks[2], (B, T, D), jnp.float32), 'Wq': jax.random.normal(ks[3], (D, D), jnp.float32) * s, 'b_q': jax.random.normal(ks[4], (D,), jnp.float32) * s, 'Wk': jax.random.normal(ks[5], (D, D), jnp.float32) * s, 'b_k': jax.random.normal(ks[6], (D,), jnp.float32) * s, 'Wv': jax.random.normal(ks[7], (D, D), jnp.float32) * s, 'b_v': jax.random.normal(ks[8], (D,), jnp.float32) * s, 'Wo': jax.random.normal(ks[9], (D, D), jnp.float32) * s, 'b_o': jax.random.normal(ks[10], (D,), jnp.float32) * s}
    _L1_xattn_all = _L1_xattn_setup()
    _L1_xattn_in = {k: v for k, v in _L1_xattn_all.items() if k in ('Wq', 'b_q', 'Wk', 'b_k', 'Wv', 'b_v', 'Wo', 'b_o')}
    del _L1_xattn_all

    def _L1_ffn_setup():
        import jax, jax.numpy as jnp
        import numpy as np
        EPS = 1e-05

        def _ln(x, g, b):
            mu = jnp.mean(x, axis=-1, keepdims=True)
            var = jnp.mean(jnp.square(x - mu), axis=-1, keepdims=True)
            return (x - mu) * jax.lax.rsqrt(var + EPS) * g + b

        def _forward(x, index_b, index_t, sw1, sb1, sw2, sb2, sw3, sb3, s_ln_g, s_ln_b, sg_w, sg_b, eg_w, eg_b, exp_bias, ew1, eb1, ew2, eb2, ew3, eb3, sel_ln_g, sel_ln_b):
            x1 = jnp.einsum('btd,hd->bth', x, sw1) + sb1
            x2 = jnp.einsum('btd,hd->bth', x, sw2) + sb2
            sh = _ln(jax.nn.silu(x1) * x2, s_ln_g, s_ln_b)
            shared_out = jnp.einsum('bth,dh->btd', sh, sw3) + sb3
            x_moe = x[index_b, index_t]
            shared_scores = jax.nn.sigmoid(x_moe @ sg_w.T + sg_b)
            expert_scores = jax.nn.sigmoid(x_moe @ eg_w.T + eg_b)
            top1_idx = jnp.argmax(expert_scores + exp_bias, axis=-1)
            top1_score = jnp.take_along_axis(expert_scores, top1_idx[:, None], axis=-1)
            weights = jax.nn.softmax(jnp.concatenate([shared_scores, top1_score], axis=-1), axis=-1)
            shared_w, expert_w = (weights[:, 0], weights[:, 1])
            shared_moe_out = shared_out[index_b, index_t] * shared_w[:, None]
            h1 = jnp.einsum('md,ehd->meh', x_moe, ew1) + eb1
            h2 = jnp.einsum('md,ehd->meh', x_moe, ew2) + eb2
            z = _ln(jax.nn.silu(h1) * h2, sel_ln_g, sel_ln_b)
            out_all = jnp.einsum('meh,edh->med', z, ew3) + eb3
            expert_out = jnp.take_along_axis(out_all, top1_idx[:, None, None], axis=1)[:, 0]
            expert_moe_out = expert_out * expert_w[:, None]
            final_out = shared_out.at[index_b, index_t].set(shared_moe_out + expert_moe_out)
            return final_out
        B, T, D, E, H, M = (2, 512, 256, 8, 128, 512)
        key = jax.random.key(seed)
        ks = jax.random.split(key, 24)
        s = 0.02
        inp = {}
        inp['x'] = jax.random.normal(ks[0], (B, T, D), jnp.float32)
        flat = jnp.arange(M, dtype=jnp.int32) * 2
        inp['index_b'] = flat // T
        inp['index_t'] = flat % T
        inp['sw1'] = jax.random.normal(ks[1], (H, D), jnp.float32) * s
        inp['sb1'] = jnp.zeros((H,), jnp.float32)
        inp['sw2'] = jax.random.normal(ks[2], (H, D), jnp.float32) * s
        inp['sb2'] = jnp.zeros((H,), jnp.float32)
        inp['sw3'] = jax.random.normal(ks[3], (D, H), jnp.float32) * s
        inp['sb3'] = jnp.zeros((D,), jnp.float32)
        inp['s_ln_g'] = jnp.ones((H,), jnp.float32)
        inp['s_ln_b'] = jnp.zeros((H,), jnp.float32)
        inp['sg_w'] = jax.random.normal(ks[4], (1, D), jnp.float32) * s
        inp['sg_b'] = jnp.zeros((1,), jnp.float32)
        inp['eg_w'] = jax.random.normal(ks[5], (E, D), jnp.float32) * s
        inp['eg_b'] = jnp.zeros((E,), jnp.float32)
        inp['exp_bias'] = jnp.zeros((E,), jnp.float32)
        inp['ew1'] = jax.random.normal(ks[6], (E, H, D), jnp.float32) * s
        inp['eb1'] = jnp.zeros((E, H), jnp.float32)
        inp['ew2'] = jax.random.normal(ks[7], (E, H, D), jnp.float32) * s
        inp['eb2'] = jnp.zeros((E, H), jnp.float32)
        inp['ew3'] = jax.random.normal(ks[8], (E, D, H), jnp.float32) * s
        inp['eb3'] = jnp.zeros((E, D), jnp.float32)
        inp['sel_ln_g'] = jnp.ones((H,), jnp.float32)
        inp['sel_ln_b'] = jnp.zeros((H,), jnp.float32)
        return inp
    _L1_ffn_all = _L1_ffn_setup()
    _L1_ffn_in = {k: v for k, v in _L1_ffn_all.items() if k in ('index_b', 'index_t', 'sw1', 'sb1', 'sw2', 'sb2', 'sw3', 'sb3', 's_ln_g', 's_ln_b', 'sg_w', 'sg_b', 'eg_w', 'eg_b', 'exp_bias', 'ew1', 'eb1', 'ew2', 'eb2', 'ew3', 'eb3', 'sel_ln_g', 'sel_ln_b')}
    del _L1_ffn_all
    return {'x': x, 'ctx_1024': ctx_1024, 'itok_BxS_0_255': itok_BxS_0_255, 'L0_attn_guidance_trajectories': _L0_attn_in['guidance_trajectories'], 'L0_xattn_Wqkv': _L0_xattn_in['Wqkv'], 'L0_xattn_bqkv': _L0_xattn_in['bqkv'], 'L0_xattn_Wo': _L0_xattn_in['Wo'], 'L0_xattn_bo': _L0_xattn_in['bo'], 'L0_xattn_Wq_c': _L0_xattn_in['Wq_c'], 'L0_xattn_Wkv_c': _L0_xattn_in['Wkv_c'], 'L0_xattn_Wo_c': _L0_xattn_in['Wo_c'], 'L0_xattn_Wg': _L0_xattn_in['Wg'], 'L0_xattn_Wu': _L0_xattn_in['Wu'], 'L0_xattn_Wd': _L0_xattn_in['Wd'], 'L0_xattn_n1': _L0_xattn_in['n1'], 'L0_xattn_n2': _L0_xattn_in['n2'], 'L0_xattn_n3': _L0_xattn_in['n3'], 'L0_xattn_nf': _L0_xattn_in['nf'], 'L0_ffn_sim_matrix': _L0_ffn_in['sim_matrix'], 'L0_ffn_gates': _L0_ffn_in['gates'], 'L0_ffn_q_proj': _L0_ffn_in['q_proj'], 'L0_ffn_k_proj': _L0_ffn_in['k_proj'], 'L0_ffn_v_proj': _L0_ffn_in['v_proj'], 'L0_ffn_o_proj': _L0_ffn_in['o_proj'], 'L1_attn_ln_gamma': _L1_attn_in['ln_gamma'], 'L1_attn_ln_beta': _L1_attn_in['ln_beta'], 'L1_attn_w_qkv': _L1_attn_in['w_qkv'], 'L1_attn_b_qkv': _L1_attn_in['b_qkv'], 'L1_attn_w_out': _L1_attn_in['w_out'], 'L1_attn_b_out': _L1_attn_in['b_out'], 'L1_xattn_Wq': _L1_xattn_in['Wq'], 'L1_xattn_b_q': _L1_xattn_in['b_q'], 'L1_xattn_Wk': _L1_xattn_in['Wk'], 'L1_xattn_b_k': _L1_xattn_in['b_k'], 'L1_xattn_Wv': _L1_xattn_in['Wv'], 'L1_xattn_b_v': _L1_xattn_in['b_v'], 'L1_xattn_Wo': _L1_xattn_in['Wo'], 'L1_xattn_b_o': _L1_xattn_in['b_o'], 'L1_ffn_index_b': _L1_ffn_in['index_b'], 'L1_ffn_index_t': _L1_ffn_in['index_t'], 'L1_ffn_sw1': _L1_ffn_in['sw1'], 'L1_ffn_sb1': _L1_ffn_in['sb1'], 'L1_ffn_sw2': _L1_ffn_in['sw2'], 'L1_ffn_sb2': _L1_ffn_in['sb2'], 'L1_ffn_sw3': _L1_ffn_in['sw3'], 'L1_ffn_sb3': _L1_ffn_in['sb3'], 'L1_ffn_s_ln_g': _L1_ffn_in['s_ln_g'], 'L1_ffn_s_ln_b': _L1_ffn_in['s_ln_b'], 'L1_ffn_sg_w': _L1_ffn_in['sg_w'], 'L1_ffn_sg_b': _L1_ffn_in['sg_b'], 'L1_ffn_eg_w': _L1_ffn_in['eg_w'], 'L1_ffn_eg_b': _L1_ffn_in['eg_b'], 'L1_ffn_exp_bias': _L1_ffn_in['exp_bias'], 'L1_ffn_ew1': _L1_ffn_in['ew1'], 'L1_ffn_eb1': _L1_ffn_in['eb1'], 'L1_ffn_ew2': _L1_ffn_in['ew2'], 'L1_ffn_eb2': _L1_ffn_in['eb2'], 'L1_ffn_ew3': _L1_ffn_in['ew3'], 'L1_ffn_eb3': _L1_ffn_in['eb3'], 'L1_ffn_sel_ln_g': _L1_ffn_in['sel_ln_g'], 'L1_ffn_sel_ln_b': _L1_ffn_in['sel_ln_b']}

def reference(x, ctx_1024, itok_BxS_0_255, L0_attn_guidance_trajectories, L0_xattn_Wqkv, L0_xattn_bqkv, L0_xattn_Wo, L0_xattn_bo, L0_xattn_Wq_c, L0_xattn_Wkv_c, L0_xattn_Wo_c, L0_xattn_Wg, L0_xattn_Wu, L0_xattn_Wd, L0_xattn_n1, L0_xattn_n2, L0_xattn_n3, L0_xattn_nf, L0_ffn_sim_matrix, L0_ffn_gates, L0_ffn_q_proj, L0_ffn_k_proj, L0_ffn_v_proj, L0_ffn_o_proj, L1_attn_ln_gamma, L1_attn_ln_beta, L1_attn_w_qkv, L1_attn_b_qkv, L1_attn_w_out, L1_attn_b_out, L1_xattn_Wq, L1_xattn_b_q, L1_xattn_Wk, L1_xattn_b_k, L1_xattn_Wv, L1_xattn_b_v, L1_xattn_Wo, L1_xattn_b_o, L1_ffn_index_b, L1_ffn_index_t, L1_ffn_sw1, L1_ffn_sb1, L1_ffn_sw2, L1_ffn_sb2, L1_ffn_sw3, L1_ffn_sb3, L1_ffn_s_ln_g, L1_ffn_s_ln_b, L1_ffn_sg_w, L1_ffn_sg_b, L1_ffn_eg_w, L1_ffn_eg_b, L1_ffn_exp_bias, L1_ffn_ew1, L1_ffn_eb1, L1_ffn_ew2, L1_ffn_eb2, L1_ffn_ew3, L1_ffn_eb3, L1_ffn_sel_ln_g, L1_ffn_sel_ln_b):
    import jax
    import jax.numpy as jnp

    def _L0_attn_ref(embeddings, guidance_trajectories):
        import jax, jax.numpy as jnp
        import numpy as np
        MAX_DIST = 8
        GUIDANCE_WEIGHT = 0.4
        EPS_MAG = 1e-06
        EPS_COS = 1e-08
        EPS_WSUM = 1e-08
        B, S, D = embeddings.shape
        W = min(MAX_DIST, S - 1)
        diffs = embeddings[:, 1:, :] - embeddings[:, :-1, :]
        pos = jnp.arange(S)[:, None]
        k = jnp.arange(W)[None, :]
        idx = pos - W + k
        valid = (idx >= 0) & (pos >= 1)
        windows = diffs[:, jnp.clip(idx, 0, S - 2), :]
        w = jnp.minimum(pos, W)
        j = k - (W - w)
        lin = jnp.where(w > 1, 0.1 + 0.9 * j / jnp.maximum(w - 1, 1), 0.1)
        pos_weights = jnp.where(valid, lin, 0.0).astype(embeddings.dtype)
        mag = jnp.linalg.norm(windows, axis=-1, keepdims=True)
        is_valid_mag = mag > EPS_MAG
        normed = jnp.where(is_valid_mag, windows / jnp.where(is_valid_mag, mag, 1.0), 0.0)
        mag_weights = jnp.tanh(mag * 2.0)
        combined = pos_weights[None, :, :, None] * mag_weights
        g_norm = jnp.linalg.norm(guidance_trajectories, axis=-1)
        a_norm = jnp.linalg.norm(normed, axis=-1)
        dots = jnp.einsum('bswd,gd->bswg', normed, guidance_trajectories)
        sims = dots / (jnp.maximum(a_norm, EPS_COS)[..., None] * jnp.maximum(g_norm, EPS_COS))
        g_weights = jax.nn.softmax(sims * 2.0, axis=-1)
        influence = jnp.einsum('bswg,gd->bswd', g_weights, guidance_trajectories)
        blended = (1.0 - GUIDANCE_WEIGHT) * normed + GUIDANCE_WEIGHT * influence
        weight_sum = jnp.maximum(combined.sum(axis=2), EPS_WSUM)
        trajectories = (blended * combined).sum(axis=2) / weight_sum
        return trajectories

    def _L0_xattn_ref(x, memory, seg_ids, Wqkv, bqkv, Wo, bo, Wq_c, Wkv_c, Wo_c, Wg, Wu, Wd, n1, n2, n3, nf):
        import jax, jax.numpy as jnp
        import numpy as np
        N_LAYERS = 4
        H = 16
        LOOKBACK = 128
        EPS = 1e-06
        ROPE_BASE = 10000.0
        NEG = jnp.float32(-1e+30)

        def rmsnorm(x, w):
            return x * jax.lax.rsqrt(jnp.mean(x * x, axis=-1, keepdims=True) + EPS) * w

        def rope_cache(L, hd):
            inv = 1.0 / ROPE_BASE ** (jnp.arange(0, hd, 2, dtype=jnp.float32) / hd)
            t = jnp.arange(L, dtype=jnp.float32)
            f = t[:, None] * inv[None, :]
            emb = jnp.concatenate([f, f], axis=-1)
            return (jnp.cos(emb), jnp.sin(emb))

        def apply_rope(x, cos, sin):
            d = x.shape[-1]
            x1, x2 = (x[..., :d // 2], x[..., d // 2:])
            rot = jnp.concatenate([-x2, x1], axis=-1)
            return x * cos + rot * sin

        def split_heads(x, n_heads):
            B, L, D = x.shape
            return x.reshape(B, L, n_heads, D // n_heads).transpose(0, 2, 1, 3)

        def merge_heads(x):
            B, h, L, d = x.shape
            return x.transpose(0, 2, 1, 3).reshape(B, L, h * d)

        def sdpa(q, k, v, bias):
            scale = q.shape[-1] ** (-0.5)
            s = jnp.einsum('bhqd,bhkd->bhqk', q, k) * scale + bias
            p = jax.nn.softmax(s, axis=-1)
            return jnp.einsum('bhqk,bhkd->bhqd', p, v)

        def forward(x, memory, seg_ids, Wqkv, bqkv, Wo, bo, Wq_c, Wkv_c, Wo_c, Wg, Wu, Wd, n1, n2, n3, nf):
            B, L, D = x.shape
            S = memory.shape[1]
            hd = D // H
            cos, sin = rope_cache(L, hd)
            i = jnp.arange(L)
            causal_bias = jnp.where(i[None, :] <= i[:, None], 0.0, NEG)[None, None]
            j = jnp.arange(S)
            allowed = (j[None, None, :] <= seg_ids[:, :, None]) & (j[None, None, :] > seg_ids[:, :, None] - LOOKBACK)
            cross_bias = jnp.where(allowed, 0.0, NEG)[:, None]
            for l in range(N_LAYERS):
                h = rmsnorm(x, n1[l])
                qkv = h @ Wqkv[l].T + bqkv[l]
                q, k, v = jnp.split(qkv, 3, axis=-1)
                q = apply_rope(split_heads(q, H), cos, sin)
                k = apply_rope(split_heads(k, H), cos, sin)
                v = split_heads(v, H)
                o = merge_heads(sdpa(q, k, v, causal_bias)) @ Wo[l].T + bo[l]
                x = x + o
                h2 = rmsnorm(x, n2[l])
                qc = split_heads(h2 @ Wq_c[l].T, H)
                kv = memory @ Wkv_c[l].T
                kc, vc = jnp.split(kv, 2, axis=-1)
                kc, vc = (split_heads(kc, H), split_heads(vc, H))
                oc = merge_heads(sdpa(qc, kc, vc, cross_bias)) @ Wo_c[l].T
                x = x + oc
                h3 = rmsnorm(x, n3[l])
                x = x + jax.nn.silu(h3 @ Wg[l].T) * (h3 @ Wu[l].T) @ Wd[l].T
            return rmsnorm(x, nf)
        return forward(x, memory, seg_ids, Wqkv, bqkv, Wo, bo, Wq_c, Wkv_c, Wo_c, Wg, Wu, Wd, n1, n2, n3, nf)

    def _L0_ffn_ref(hidden_states, sim_matrix, gates, q_proj, k_proj, v_proj, o_proj):
        import jax, jax.numpy as jnp
        import numpy as np
        HIDDEN = 256
        HEAD_DIM = 64
        N_EXPERTS = 16
        MIN_EXPERTS = 2
        B, T = (4, 512)

        def _normalize(x, axis):
            n = jnp.sqrt(jnp.sum(x * x, axis=axis, keepdims=True))
            return x / jnp.maximum(n, 1e-12)

        def _ste(x):
            hard = jax.lax.stop_gradient((x > 0).astype(x.dtype))
            return hard + x - jax.lax.stop_gradient(x)

        def _gating(hidden_states, sim_matrix, gates):
            b, t, c = hidden_states.shape
            flat = hidden_states.reshape(b * t, c)
            logits = _normalize(flat, -1) @ _normalize(sim_matrix, 0) - jax.nn.sigmoid(gates)
            gated = jax.nn.relu(logits)
            mask = _ste(gated)
            inactive = jnp.sum(mask, axis=1) == 0
            _, fb_idx = jax.lax.top_k(logits, MIN_EXPERTS)
            fb = jnp.zeros_like(mask).at[jnp.arange(b * t)[:, None], fb_idx].set(1.0)
            fb_applied = inactive[:, None] & (fb > 0)
            mask = jnp.where(fb_applied, 1.0, mask)
            masked_logits = jnp.where(mask > 0, gated, -jnp.inf)
            return jax.nn.softmax(masked_logits, axis=-1).reshape(b, t, -1)
        b, t, c = hidden_states.shape
        rw = _gating(hidden_states, sim_matrix, gates)
        q = jnp.einsum('bte,bted->btd', rw, jnp.einsum('btc,ecd->bted', hidden_states, q_proj))
        k = jnp.einsum('bte,bted->btd', rw, jnp.einsum('btc,ecd->bted', hidden_states, k_proj))
        v = jnp.einsum('bte,bted->btd', rw, jnp.einsum('btc,ecd->bted', hidden_states, v_proj))
        scale = 1.0 / jnp.sqrt(jnp.asarray(HEAD_DIM, dtype=q.dtype))
        scores = jnp.einsum('bqd,bkd->bqk', q, k) * scale
        causal = jnp.tril(jnp.ones((t, t), dtype=bool))
        scores = jnp.where(causal, scores, -jnp.inf)
        attn = jnp.einsum('bqk,bkd->bqd', jax.nn.softmax(scores, axis=-1), v)
        mixed = attn[:, :, None, :] * rw[..., None]
        return jnp.einsum('bted,edc->btc', mixed, o_proj)

    def _L1_attn_ref(x, ln_gamma, ln_beta, w_qkv, b_qkv, w_out, b_out):
        import jax, jax.numpy as jnp
        import numpy as np
        D_MODEL = 256
        NUM_HEADS = 16
        HEAD_DIM = D_MODEL // NUM_HEADS
        B, T, C = x.shape
        residual = x
        mu = jnp.mean(x, axis=-1, keepdims=True)
        var = jnp.var(x, axis=-1, keepdims=True)
        h = (x - mu) * jax.lax.rsqrt(var + 1e-05) * ln_gamma + ln_beta
        qkv = (h @ w_qkv + b_qkv).reshape(B, T, 3, NUM_HEADS, HEAD_DIM)
        qkv = jnp.transpose(qkv, (2, 0, 3, 1, 4))
        q, k, v = (qkv[0], qkv[1], qkv[2])
        scores = jnp.einsum('bhqd,bhkd->bhqk', q, k) / np.sqrt(HEAD_DIM)
        attn = jax.nn.softmax(scores, axis=-1)
        out = jnp.einsum('bhqk,bhkd->bhqd', attn, v)
        out = jnp.transpose(out, (0, 2, 1, 3)).reshape(B, T, C)
        out = out @ w_out + b_out
        return residual + out

    def _L1_xattn_ref(q, k, v, Wq, b_q, Wk, b_k, Wv, b_v, Wo, b_o):
        import jax, jax.numpy as jnp
        import numpy as np
        D = 256
        H = 16
        DH = D // H
        B, Tq, _ = q.shape
        Tk = k.shape[1]
        Q = (q @ Wq + b_q).reshape(B, Tq, H, DH)
        K = (k @ Wk + b_k).reshape(B, Tk, H, DH)
        V = (v @ Wv + b_v).reshape(B, Tk, H, DH)
        scores = jnp.einsum('bthd,bshd->bhts', Q, K) / jnp.sqrt(jnp.float32(DH))
        P = jax.nn.softmax(scores, axis=-1)
        out = jnp.einsum('bhts,bshd->bthd', P, V).reshape(B, Tq, D)
        return out @ Wo + b_o

    def _L1_ffn_ref(x, index_b, index_t, sw1, sb1, sw2, sb2, sw3, sb3, s_ln_g, s_ln_b, sg_w, sg_b, eg_w, eg_b, exp_bias, ew1, eb1, ew2, eb2, ew3, eb3, sel_ln_g, sel_ln_b):
        import jax, jax.numpy as jnp
        import numpy as np
        EPS = 1e-05

        def _ln(x, g, b):
            mu = jnp.mean(x, axis=-1, keepdims=True)
            var = jnp.mean(jnp.square(x - mu), axis=-1, keepdims=True)
            return (x - mu) * jax.lax.rsqrt(var + EPS) * g + b

        def _forward(x, index_b, index_t, sw1, sb1, sw2, sb2, sw3, sb3, s_ln_g, s_ln_b, sg_w, sg_b, eg_w, eg_b, exp_bias, ew1, eb1, ew2, eb2, ew3, eb3, sel_ln_g, sel_ln_b):
            x1 = jnp.einsum('btd,hd->bth', x, sw1) + sb1
            x2 = jnp.einsum('btd,hd->bth', x, sw2) + sb2
            sh = _ln(jax.nn.silu(x1) * x2, s_ln_g, s_ln_b)
            shared_out = jnp.einsum('bth,dh->btd', sh, sw3) + sb3
            x_moe = x[index_b, index_t]
            shared_scores = jax.nn.sigmoid(x_moe @ sg_w.T + sg_b)
            expert_scores = jax.nn.sigmoid(x_moe @ eg_w.T + eg_b)
            top1_idx = jnp.argmax(expert_scores + exp_bias, axis=-1)
            top1_score = jnp.take_along_axis(expert_scores, top1_idx[:, None], axis=-1)
            weights = jax.nn.softmax(jnp.concatenate([shared_scores, top1_score], axis=-1), axis=-1)
            shared_w, expert_w = (weights[:, 0], weights[:, 1])
            shared_moe_out = shared_out[index_b, index_t] * shared_w[:, None]
            h1 = jnp.einsum('md,ehd->meh', x_moe, ew1) + eb1
            h2 = jnp.einsum('md,ehd->meh', x_moe, ew2) + eb2
            z = _ln(jax.nn.silu(h1) * h2, sel_ln_g, sel_ln_b)
            out_all = jnp.einsum('meh,edh->med', z, ew3) + eb3
            expert_out = jnp.take_along_axis(out_all, top1_idx[:, None, None], axis=1)[:, 0]
            expert_moe_out = expert_out * expert_w[:, None]
            final_out = shared_out.at[index_b, index_t].set(shared_moe_out + expert_moe_out)
            return final_out
        return _forward(x, index_b, index_t, sw1, sb1, sw2, sb2, sw3, sb3, s_ln_g, s_ln_b, sg_w, sg_b, eg_w, eg_b, exp_bias, ew1, eb1, ew2, eb2, ew3, eb3, sel_ln_g, sel_ln_b)
    x = x + _L0_attn_ref(_layernorm(x, axis=-1), L0_attn_guidance_trajectories)
    x = x + _L0_xattn_ref(_layernorm(x, axis=-1), ctx_1024, itok_BxS_0_255, L0_xattn_Wqkv, L0_xattn_bqkv, L0_xattn_Wo, L0_xattn_bo, L0_xattn_Wq_c, L0_xattn_Wkv_c, L0_xattn_Wo_c, L0_xattn_Wg, L0_xattn_Wu, L0_xattn_Wd, L0_xattn_n1, L0_xattn_n2, L0_xattn_n3, L0_xattn_nf)
    x = x + _L0_ffn_ref(_layernorm(x, axis=-1), L0_ffn_sim_matrix, L0_ffn_gates, L0_ffn_q_proj, L0_ffn_k_proj, L0_ffn_v_proj, L0_ffn_o_proj)
    x = x + _L1_attn_ref(_layernorm(x, axis=-1), L1_attn_ln_gamma, L1_attn_ln_beta, L1_attn_w_qkv, L1_attn_b_qkv, L1_attn_w_out, L1_attn_b_out)
    x = x + _L1_xattn_ref(_layernorm(x, axis=-1), ctx_1024, ctx_1024, L1_xattn_Wq, L1_xattn_b_q, L1_xattn_Wk, L1_xattn_b_k, L1_xattn_Wv, L1_xattn_b_v, L1_xattn_Wo, L1_xattn_b_o)
    x = x + _L1_ffn_ref(_layernorm(x, axis=-1), L1_ffn_index_b, L1_ffn_index_t, L1_ffn_sw1, L1_ffn_sb1, L1_ffn_sw2, L1_ffn_sb2, L1_ffn_sw3, L1_ffn_sb3, L1_ffn_s_ln_g, L1_ffn_s_ln_b, L1_ffn_sg_w, L1_ffn_sg_b, L1_ffn_eg_w, L1_ffn_eg_b, L1_ffn_exp_bias, L1_ffn_ew1, L1_ffn_eb1, L1_ffn_ew2, L1_ffn_eb2, L1_ffn_ew3, L1_ffn_eb3, L1_ffn_sel_ln_g, L1_ffn_sel_ln_b)
    return x

_drawn_inputs = setup_inputs


def setup_inputs(seed=0):
    import zlib

    import numpy as np

    out = dict(_drawn_inputs(seed))
    spreads = {'L0_xattn_bqkv': (0.0, 0.1),
     'L0_xattn_bo': (0.0, 0.1),
     'L0_xattn_n1': (1.0, 0.6),
     'L0_xattn_n2': (1.0, 0.6),
     'L0_xattn_n3': (1.0, 0.6),
     'L0_xattn_nf': (1.0, 0.2),
     'L0_ffn_gates': (0.0, 0.326),
     'L1_attn_ln_gamma': (1.0, 0.6),
     'L1_attn_ln_beta': (0.0, 0.1),
     'L1_attn_b_qkv': (0.0, 0.1),
     'L1_attn_b_out': (0.0, 0.1),
     'L1_ffn_sb1': (0.0, 0.418),
     'L1_ffn_sb2': (0.0, 0.392),
     'L1_ffn_sb3': (0.0, 0.275),
     'L1_ffn_s_ln_g': (1.0, 0.6),
     'L1_ffn_s_ln_b': (0.0, 0.8),
     'L1_ffn_eg_b': (0.0, 0.8),
     'L1_ffn_exp_bias': (0.0, 0.281),
     'L1_ffn_eb1': (0.0, 0.8),
     'L1_ffn_eb2': (0.0, 0.8),
     'L1_ffn_eb3': (0.0, 0.8),
     'L1_ffn_sel_ln_g': (1.0, 0.6),
     'L1_ffn_sel_ln_b': (0.0, 0.8)}
    factors = {'L0_xattn_Wq_c': 8.0,
     'L0_ffn_q_proj': 4.236,
     'L0_ffn_k_proj': 4.24,
     'L1_xattn_Wq': 8.0,
     'L1_xattn_b_q': 8.0,
     'L1_xattn_Wk': 8.0,
     'L1_xattn_b_k': 64.0,
     'L1_xattn_Wv': 3.131,
     'L1_xattn_b_v': 8.0,
     'L1_xattn_Wo': 3.118,
     'L1_xattn_b_o': 8.0,
     'L1_ffn_sg_w': 25.985,
     'L1_ffn_eg_w': 8.0,
     'L1_ffn_ew1': 3.088,
     'L1_ffn_ew2': 3.076,
     'L1_ffn_ew3': 2.936}
    for name, (base, spread) in spreads.items():
        noise = np.random.default_rng([zlib.crc32(name.encode()), seed]).standard_normal(out[name].shape)
        drawn = base * np.exp(spread * noise) if base else spread * noise
        out[name] = jnp.asarray(drawn.astype(out[name].dtype))
    for name, factor in factors.items():
        out[name] = (out[name] * factor).astype(out[name].dtype)
    return out
```

```python
from contextlib import ExitStack, contextmanager

import numpy as np

import concourse.bass as bass
from concourse import mybir

ALU = mybir.AluOpType
ACT = mybir.ActivationFunctionType
F32 = mybir.dt.float32
BF16 = mybir.dt.bfloat16
I32 = mybir.dt.int32
AX = mybir.AxisListType

P = 128
B, S, D = 2, 1024, 256
C = D // P
TB = S // P
TT = B * TB
HALF = 512
NH = S // HALF
LAYERS, HEADS, HD = 4, 16, 16
CTX = 64
LOOKBACK = 128
FF = 1024
FT = FF // P
NEXP, MHD = 16, 64
E1, H1, M1 = 8, 128, 512
MT = M1 // P
MASKED = -4e30
WINDOW = 8
TERMS = ((0, 0), (0, 1), (0, 2), (1, 0), (1, 1), (2, 0))
TERM_DMAS = 2 * len(TERMS) * 4
ROWS = len(TERMS) * HD + 3
FIRST_SEM = 160


class Names:
    pass


class Tally:

    def __init__(self, engine, sem):
        self.engine, self.sem, self.n = engine, sem, 0

    def add(self, ins):
        ins.then_inc(self.sem, 1)
        self.n += 1

    def wait(self):
        self.engine.wait_ge(self.sem, self.n)


@contextmanager
def phase(nc, tag, names):
    with ExitStack() as ctx:
        nums = range(FIRST_SEM, FIRST_SEM + len(names.split()))
        sems = {n: ctx.enter_context(nc.semaphore(f"{tag}_{n}", num=k)) for n, k in zip(names.split(), nums)}
        nc.gpsimd.sem_clear(nums)
        nc.all_engine_barrier()
        block = ctx.enter_context(nc.Block())
        yield block, sems


class Ring:

    def __init__(self, jobs):
        self.at = {job: (n % 2, n // 2) for n, job in enumerate(jobs)}
        assert len(self.at) == len(jobs)


def attention_plan(G, steps, prep, maxima, shifts, tail):
    plan = prep(0) + maxima(0) + shifts(0)
    for g in range(G):
        side = (prep(g + 1) + maxima(g + 1) + shifts(g + 1)) if g + 1 < G else []
        lead = len(prep(g + 1)) if g + 1 < G else 0
        n = len(steps)
        spread = [[] for _ in range(n)]
        for k, job in enumerate(side):
            spread[min(n - 1, k * n // max(1, len(side)))].append(job)
        for s in range(n):
            plan += [("S", g, s)] + spread[s]
            plan += [("PV", g, s)]
            if s == n - 1 or steps[s][0] != steps[s + 1][0]:
                plan.append(("o", g, steps[s][0]))
            if s == min(n - 1, n // 2 + 2) and g >= 0 and n > 2:
                plan.append(("z", g, 0))
            if s == 0 and g > 0:
                plan += [("z", g - 1, h) for h in ((1,) if n > 2 else (0, 1))]
    plan += [("z", G - 1, h) for h in ((1,) if len(steps) > 2 else (0, 1))]
    return plan + tail


def attention(nc, tag, T, K, kind, q_in, k_in, w, H, hd, causal, lk, scale, out_rows, loads=()):
    G = HEADS // H if kind != "given" else 1
    slot = P // H
    KT = max(1, lk // P)
    KP = min(P, lk)
    masked = kind == "cross"
    stacked = kind in ("rope", "plain") and lk == S
    pair = min(2, H)
    steps = [(h, i, max(0, i * P - h * HALF) if causal else 0) for h in range(NH) for i in range(KT)
             if not causal or i * P < (h + 1) * HALF]
    last_of = {h: max(s for s, x in enumerate(steps) if x[0] == h) for h in range(NH)}

    def prep(g):
        jobs = []
        for h in range(NH):
            jobs.append(("q", g, h))
        for h in range(max(1, lk // HALF)):
            jobs.append(("k", g, h))
        if kind == "rope":
            jobs = [x for a in jobs for x in (a,)]
            folded = []
            for n, job in enumerate(jobs):
                folded.append(job)
                if n:
                    folded.append((jobs[n - 1][0] + "f",) + jobs[n - 1][1:])
            folded.append((jobs[-1][0] + "f",) + jobs[-1][1:])
            jobs = folded
        if kind != "given":
            jobs += [("v", g, n) for n in range(max(1, KT // 4))]
        return jobs

    pieces = []
    for i in range(TB):
        keys = (i + 1) * P if causal else lk
        for p in range((keys + HALF - 1) // HALF):
            pieces.append((i, p, min(HALF, keys - p * HALF), causal and p == (keys - 1) // HALF))

    def maxima(g):
        return [("m", g, j, n) for n in range(len(pieces)) for j in range(H)]

    def shifts(g):
        return [("t", g, h) for h in range(NH)]

    tail = [("y", i) for i in range(TB)] if out_rows else []
    plan = attention_plan(G, steps, prep, maxima, shifts, tail)
    ringed = [x for x in plan if x[0] not in ("S", "PV", "o")]
    ring = Ring(ringed)

    names = ("ring_full0 ring_full1 ring_free0 ring_free1 narrow_made shift_made scores_full exp_done pv_done heads_raw heads_divided cleared "
             "high_made rest_made low_made loaded terms_stacked shifts_stacked maxima_split")
    with phase(nc, tag, names) as (block, s):
        full, free = (s["ring_full0"], s["ring_full1"]), (s["ring_free0"], s["ring_free1"])

        def bank(job):
            return T.ring[ring.at[job][0]]

        def take(pe, job):
            par, use = ring.at[job]
            if use:
                pe.wait_ge(free[par], use)

        def give(ins, job):
            ins.then_inc(full[ring.at[job][0]], 1)

        def arrived(eng, job):
            par, use = ring.at[job]
            eng.wait_ge(full[par], use + 1)

        def release(ins, job):
            ins.then_inc(free[ring.at[job][0]], 1)

        def consumed(eng, job):
            par, use = ring.at[job]
            eng.wait_ge(free[par], use + 1)

        to_slots = ("qf", "kf") if kind == "rope" else ("q", "k")
        slot_jobs = [x for x in ringed if x[0] in to_slots]
        per_group = len(slot_jobs) // G
        turns = {x: n for n, x in enumerate(x for x in ringed if x[0] in ("q", "k"))}
        turn_jobs = list(turns)
        v_jobs = [x for x in ringed if x[0] == "v"]

        shift = T.shift_bf if stacked else T.shift

        def qk(g, which):
            return (T.q_slots if which == "q" else T.k_slots)[:, g % 2, :]

        def narrow(g, which):
            if stacked:
                return T.parts[:, 0 if which == "q" else 1, 0, :]
            return (T.q_narrow if which == "q" else T.k_narrow)[:, g % 2, :]

        def width(which):
            return HALF if which == "q" or lk >= HALF else lk

        @block.tensor
        def _(pe):
            for job in plan:
                what, g = job[0], job[1]
                if what in ("q", "k"):
                    h, n = job[2], width(what)
                    take(pe, job)
                    if kind == "given":
                        src = T.q_tok if what == "q" else T.k_tok
                        for i in range(4):
                            m = pe.matmul(bank(job)[:, i * P:(i + 1) * P], src[:, 4 * h + i, :], K.ident,
                                          start=True, stop=True)
                    else:
                        src = q_in if what == "q" else k_in
                        for c in range(C):
                            m = pe.matmul(bank(job)[:, 0:n], w[what][:, c, g, :], src[:, c, h * n:(h + 1) * n],
                                          start=c == 0, stop=c == C - 1)
                    give(m, job)
                elif what in ("qf", "kf"):
                    base = (what[0],) + job[1:]
                    take(pe, job)
                    consumed(pe, base)
                    m = pe.matmul(bank(job)[:, :], K.fold, T.turned[:, turns[base] % 2, :], start=True, stop=True)
                    give(m, job)
                elif what == "v":
                    take(pe, job)
                    for n in range(min(4, KT)):
                        i = 4 * job[2] + n
                        for c in range(C):
                            pe.matmul(bank(job)[0:KP, n * P:(n + 1) * P], k_in[:, c, i * KP:(i + 1) * KP],
                                      w["v"][:, c, g, :], start=c == 0, stop=False)
                        m = pe.matmul(bank(job)[0:KP, n * P:(n + 1) * P], K.ones_row[0:1, 0:KP],
                                      w["v_row"][0:1, g, :], start=False, stop=True)
                    give(m, job)
                elif what == "m":
                    j, n = job[2], job[3]
                    i, p, cols, diag = pieces[n]
                    take(pe, job)
                    if j == 0 and n == 0:
                        pe.wait_ge(s["high_made"] if stacked else s["narrow_made"], (g + 1) * per_group)
                    rows = slice(j * slot, (j + 1) * slot)
                    m = pe.matmul(bank(job)[:, 0:cols], narrow(g, "q")[rows, i * P:(i + 1) * P],
                                  narrow(g, "k")[rows, p * HALF:p * HALF + cols], start=True, stop=not (diag or masked))
                    if diag:
                        m = pe.matmul(bank(job)[:, cols - P:cols], K.ident_bf, K.mask_q, start=False, stop=True)
                    if masked:
                        m = pe.matmul(bank(job)[:, 0:cols], w["mask"][0:CTX, i * P:(i + 1) * P],
                                      K.ident_bf[0:CTX, 0:CTX], start=False, stop=True)
                    give(m, job)
                elif what == "t":
                    take(pe, job)
                    if job[2] == 0:
                        pe.wait_ge(s["shift_made"], g + 1)
                    for i in range(4):
                        m = pe.matmul(bank(job)[:, i * P:(i + 1) * P], shift[:, 4 * job[2] + i, :],
                                      K.ident_bf if stacked else K.ident, start=True, stop=True)
                    give(m, job)
                elif what == "S":
                    h, i, c0 = steps[job[2]]
                    if stacked and job[2] == 0:
                        pe.wait_ge(s["terms_stacked"], 16 * TERM_DMAS * (g + 1))
                        pe.wait_ge(s["shifts_stacked"], 16 * H * (g + 1))
                        pe.wait_ge(s["cleared"], 4)
                    elif i == 0 and not stacked:
                        consumed(pe, ("t", g, h))
                    for a in range(H // pair):
                        unit = (g * len(steps) + job[2]) * (H // pair) + a
                        if unit >= 2:
                            pe.wait_ge(s["exp_done"], unit - 1)
                        for b in range(pair):
                            rows = slice((a * pair + b) * slot, (a * pair + b + 1) * slot)
                            out = T.scores[0:KP, unit % 2, b, c0:HALF]
                            diag = causal and i * P >= h * HALF
                            keys, queries = qk(g, "k")[rows, :] if not stacked else T.stack_k[0:ROWS, g % 2, a * pair + b, :], \
                                qk(g, "q")[rows, :] if not stacked else T.stack_q[0:ROWS, g % 2, a * pair + b, :]
                            m = pe.matmul(out, keys[:, i * P:i * P + KP], queries[:, h * HALF + c0:(h + 1) * HALF],
                                          start=True, stop=not (diag or masked))
                            if diag:
                                m = pe.matmul(T.scores[:, unit % 2, b, c0:c0 + P], K.ident_bf, K.mask_k,
                                              start=False, stop=True)
                            if masked:
                                m = pe.matmul(out, K.ident_bf[0:CTX, 0:CTX], w["mask"][0:CTX, h * HALF:(h + 1) * HALF],
                                              start=False, stop=True)
                        m.then_inc(s["scores_full"], 1)
                elif what == "PV":
                    h, i, c0 = steps[job[2]]
                    n = g * len(steps) + job[2]
                    pe.wait_ge(s["exp_done"], (n + 1) * (H // pair))
                    if i == 0:
                        for x in v_jobs:
                            if x[1] == g and h == 0:
                                consumed(pe, x)
                        if g:
                            pe.wait_ge(s["heads_raw"], NH * (g - 1) + h + 1)
                    for j in range(H):
                        m = pe.matmul(T.heads_ps[j * slot:(j + 1) * slot, h, c0:HALF],
                                      T.values[0:KP, g % 2, i, j * slot:(j + 1) * slot],
                                      T.probs[0:KP, n % 2, j, c0:HALF], start=i == 0, stop=job[2] == last_of[h],
                                      skip_group_check=True)
                    m.then_inc(s["pv_done"], 1)
                elif what == "z":
                    take(pe, job)
                    pe.wait_ge(s["heads_raw"], NH * g + job[2] + 1)
                    m = pe.matmul(bank(job)[:, :], w["spread"], T.heads_sb[:, job[2], :], start=True, stop=True)
                    give(m, job)
                elif what == "y":
                    i = job[1]
                    take(pe, job)
                    if i == 0:
                        pe.wait_ge(s["heads_divided"], NH * G)
                    for gg in range(G):
                        m = pe.matmul(bank(job)[:, 0:D], T.heads_out[:, gg, i * P:(i + 1) * P], w["o"][:, gg, :],
                                      start=gg == 0, stop=gg == G - 1)
                    give(m, job)

        @block.scalar
        def _(act):
            for job in plan:
                what, g = job[0], job[1]
                if what in to_slots:
                    n = width(what[0])
                    arrived(act, job)
                    bias = w[what[0] + "_slot_bias"][:, g:g + 1]
                    if stacked:
                        if g:
                            act.wait_ge(s["terms_stacked"], 16 * TERM_DMAS * g)
                        act.activation(narrow(g, what[0])[:, job[2] * n:(job[2] + 1) * n], bank(job)[:, 0:n],
                                       ACT.Identity, bias=bias).then_inc(s["high_made"], 1)
                        continue
                    release(act.activation(qk(g, what[0])[:, job[2] * n:(job[2] + 1) * n], bank(job)[:, 0:n],
                                           ACT.Identity, bias=bias), job)
                elif what == "t" and stacked:
                    arrived(act, job)
                    if g and job[2] == 0:
                        act.wait_ge(s["shifts_stacked"], 16 * H * g)
                    release(act.activation(T.shift_rows[:, job[2] * HALF:(job[2] + 1) * HALF], bank(job)[:, :],
                                           ACT.Copy), job)
                elif what == "v":
                    arrived(act, job)
                    if g >= 2:
                        act.wait_ge(s["pv_done"], len(steps) * (g - 1))
                    n = min(4, KT)
                    release(act.activation(T.values[0:KP, g % 2, 4 * job[2]:4 * job[2] + n, :],
                                           bank(job)[0:KP, 0:n * P].rearrange("p (n c) -> p n c", c=P), ACT.Copy), job)
                elif what == "S":
                    h, i, c0 = steps[job[2]]
                    n = g * len(steps) + job[2]
                    if n >= 2:
                        act.wait_ge(s["pv_done"], n - 1)
                    for a in range(H // pair):
                        unit = n * (H // pair) + a
                        act.wait_ge(s["scores_full"], unit + 1)
                        act.activation(T.probs[0:KP, n % 2, a * pair:(a + 1) * pair, c0:HALF],
                                       T.scores[0:KP, unit % 2, 0:pair, c0:HALF], ACT.Exp,
                                       scale=scale).then_inc(s["exp_done"], 1)
                elif what == "o":
                    h = job[2]
                    act.wait_ge(s["pv_done"], g * len(steps) + last_of[h] + 1)
                    if g:
                        act.wait_ge(s["heads_divided"], NH * (g - 1) + h + 1)
                    act.activation(T.heads_sb[:, h, :], T.heads_ps[:, h, :], ACT.Copy).then_inc(s["heads_raw"], 1)

        @block.vector
        def _(dve):
            for job in plan:
                what, g = job[0], job[1]
                if what in ("q", "k") and kind == "rope":
                    arrived(dve, job)
                    u = turns[job]
                    if u >= 2:
                        old = turn_jobs[u - 2]
                        arrived(dve, (old[0] + "f",) + old[1:])
                    at = slice(job[2] * HALF, (job[2] + 1) * HALF)
                    release(dve.scalar_tensor_tensor(T.turned[:, u % 2, :], bank(job)[:, :],
                                                     w[what + "_bias"][:, g:g + 1], K.trig[:, at],
                                                     ALU.add, ALU.mult), job)
                elif what in to_slots and stacked:
                    u = slot_jobs.index(job)
                    x = 0 if what[0] == "q" else 1
                    at = slice(job[2] * HALF, (job[2] + 1) * HALF)
                    arrived(dve, job)
                    dve.wait_ge(s["high_made"], u + 1)
                    if u >= 2:
                        dve.wait_ge(s["low_made"], 2 * (u - 1))
                    ins = dve.scalar_tensor_tensor(T.rest[:, u % 2, :], bank(job)[:, :],
                                                   w[what[0] + "_slot_bias"][:, g:g + 1], T.parts[:, x, 0, at],
                                                   ALU.add, ALU.subtract)
                    release(ins, job)
                elif what == "m":
                    i, p, cols, _ = pieces[job[3]]
                    arrived(dve, job)
                    if job == maxima(0)[0]:
                        dve.wait_ge(s["cleared"], 2)
                    if g and job == maxima(g)[0]:
                        dve.wait_ge(s["shift_made"], g)
                    release(dve.tensor_reduce(T.maxima[:, p, i, job[2]:job[2] + 1], bank(job)[:, 0:cols], AX.X,
                                              ALU.max, negate=True), job)
                elif what == "t":
                    if job[2] == 0:
                        for x in maxima(g)[-2:]:
                            consumed(dve, x)
                        by_head = shift[:, :, :].rearrange("p i (j r) -> p i j r", r=slot)
                        if stacked:
                            t = Tally(dve, s["maxima_split"])
                            t.n = 5 * g
                            rest, at = T.maxima[:, 0, :, 0:H], lambda k: by_head[:, :, :, hd + k]
                            t.add(dve.tensor_tensor(rest, rest, T.maxima[:, 1, :, 0:H], ALU.min)); t.wait()
                            t.add(dve.tensor_copy(at(0), rest)); t.wait()
                            t.add(dve.tensor_tensor(rest, rest, at(0), ALU.subtract)); t.wait()
                            t.add(dve.tensor_copy(at(1), rest)); t.wait()
                            t.add(dve.tensor_tensor(rest, rest, at(1), ALU.subtract)); t.wait()
                            dve.tensor_copy(at(2), rest).then_inc(s["shift_made"], 1)
                        else:
                            dve.tensor_tensor(by_head[:, :, :, hd], T.maxima[:, 0, :, 0:H], T.maxima[:, 1, :, 0:H],
                                              ALU.min).then_inc(s["shift_made"], 1)
                    if stacked:
                        continue
                    arrived(dve, job)
                    at = qk(g, "q")[:, job[2] * HALF:(job[2] + 1) * HALF]
                    release(dve.tensor_tensor(at, bank(job)[:, :], at, ALU.add), job)
                elif what == "z":
                    h = job[2]
                    arrived(dve, job)
                    if NH * g + h:
                        dve.wait_ge(s["heads_divided"], NH * g + h)
                    release(dve.reciprocal(T.denominators[:, :], bank(job)[:, :]), job)
                    consumed(dve, job)
                    dve.tensor_tensor(T.heads_out[:, g, h * HALF:(h + 1) * HALF], T.heads_sb[:, h, :],
                                      T.denominators[:, :], ALU.mult).then_inc(s["heads_divided"], 1)
                elif what == "y":
                    arrived(dve, job)
                    rows = out_rows(job[1])
                    release(dve.tensor_tensor(rows, bank(job)[:, 0:D], rows, ALU.add), job)

        @block.gpsimd
        def _(pool):
            pool.memset(T.shift[:, :, :], 0.0).then_inc(s["cleared"], 1)
            pool.memset(T.maxima[:, :, :, :], 3e38).then_inc(s["cleared"], 1)
            if stacked:
                for par in range(2):
                    pool.wait_ge(s["cleared"], 2 + par)
                    pool.memset(T.stack_k[ROWS - 3:ROWS, par, :, :], 1.0).then_inc(s["cleared"], 1)
            pool.wait_ge(s["cleared"], 4 if stacked else 2)
            for u, job in enumerate(slot_jobs):
                what, g = job[0][0], job[1]
                n = width(what)
                consumed(pool, job)
                at = slice(job[2] * n, (job[2] + 1) * n)
                if stacked:
                    x = 0 if what == "q" else 1
                    pool.tensor_copy(T.parts[:, x, 1, at], T.rest[:, u % 2, :]).then_inc(s["low_made"], 1)
                    pool.wait_ge(s["low_made"], 2 * u + 1)
                    pool.tensor_tensor(T.parts[:, x, 2, at], T.rest[:, u % 2, :], T.parts[:, x, 1, at],
                                       ALU.subtract).then_inc(s["low_made"], 1)
                else:
                    pool.tensor_copy(narrow(g, what)[:, at], qk(g, what)[:, at]).then_inc(s["narrow_made"], 1)

        if not stacked:
            return

        @block.sync
        def _(sync):
            for to, src in loads:
                sync.dma_start(to, src).then_inc(s["loaded"], 16)
            for g in range(G):
                sync.wait_ge(s["low_made"], 2 * per_group * (g + 1))
                sync.wait_ge(s["high_made"], per_group * (g + 1))
                if g >= 2:
                    sync.wait_ge(s["scores_full"], (g - 1) * len(steps) * (H // pair))
                for j in range(H):
                    for term, parts in enumerate(TERMS):
                        for x, stack in enumerate((T.stack_q, T.stack_k)):
                            sync.dma_start(stack[term * HD:(term + 1) * HD, g % 2, j, :],
                                           T.parts[j * slot:j * slot + HD, x, parts[x], :]).then_inc(s["terms_stacked"], 16)
                for h in range(NH):
                    consumed(sync, ("t", g, h))
                for j in range(H):
                    sync.dma_start(T.stack_q[ROWS - 3:ROWS, g % 2, j, :],
                                   T.shift_rows[j * slot + HD:j * slot + HD + 3, :]).then_inc(s["shifts_stacked"], 16)
            if loads:
                sync.wait_ge(s["loaded"], 16 * len(loads))


def normalise(nc, tag, T, K, rows, count, out, eps, centred, feature_scale=None, write=None, extra=None):
    with phase(nc, tag, "stats stats_all power rstd_made normed turned0 turned1 taken0 taken1 extra") as (block, s):
        quads = count // 4

        @block.vector
        def _(dve):
            for i in range(count):
                dve.bn_stats(T.bn[:, i, :], rows(i)).then_inc(s["stats"], 1)
            for i in range(count):
                dve.wait_ge(s["stats"], i + 1)
                dve.bn_aggr(T.mv[:, i, :], T.bn[:, i, :]).then_inc(s["stats_all"], 1)
            dve.wait_ge(s["stats_all"], count)
            if centred:
                dve.tensor_scalar(T.msq[:, 0:count], T.mv[:, 0:count, 1], eps, None, ALU.add).then_inc(s["power"], 1)
            else:
                dve.tensor_tensor(T.msq[:, 0:count], T.mv[:, 0:count, 0], T.mv[:, 0:count, 0], ALU.mult).then_inc(s["power"], 1)
                dve.wait_ge(s["power"], 1)
                dve.scalar_tensor_tensor(T.msq[:, 0:count], T.mv[:, 0:count, 1], eps, T.msq[:, 0:count],
                                         ALU.add, ALU.add).then_inc(s["power"], 1)
            dve.wait_ge(s["rstd_made"], 1)
            for i in range(count):
                to = write(i) if write else T.normed[:, i, :]
                if centred:
                    dve.tensor_scalar(to, rows(i), T.mv[:, i, 0:1], T.rstd[:, i:i + 1], ALU.subtract,
                                      ALU.mult).then_inc(s["normed"], 1)
                else:
                    dve.tensor_scalar(to, rows(i), T.rstd[:, i:i + 1], None, ALU.mult).then_inc(s["normed"], 1)
            if extra:
                extra(dve, s["extra"])

        @block.gpsimd
        def _(pool):
            pool.wait_ge(s["power"], 1 if centred else 2)
            pool.tensor_tensor(T.rstd[:, 0:count], T.msq[:, 0:count], K.minus_half[:, 0:count],
                               ALU.pow).then_inc(s["rstd_made"], 1)

        if out is None:
            return
        take = [s["taken0"], s["taken1"]]
        turned = [s["turned0"], s["turned1"]]

        @block.tensor
        def _(pe):
            for q in range(quads):
                pe.wait_ge(s["normed"], 4 * q + 4)
                for c in range(C):
                    if q:
                        pe.wait_ge(take[c], q)
                    for i in range(4):
                        src = (write(4 * q + i) if write else T.normed[:, 4 * q + i, :])[:, c * P:(c + 1) * P]
                        m = pe.transpose(T.ring[c][:, i * P:(i + 1) * P], src, K.ident)
                    m.then_inc(turned[c], 1)

        @block.scalar
        def _(act):
            for q in range(quads):
                for c in range(C):
                    act.wait_ge(turned[c], q + 1)
                    to = out[:, c, q * HALF:(q + 1) * HALF]
                    if feature_scale is None:
                        ins = act.activation(to, T.ring[c][:, :], ACT.Copy)
                    else:
                        scale, bias = feature_scale
                        ins = act.activation(to, T.ring[c][:, :], ACT.Identity, scale=scale[:, c:c + 1],
                                             bias=bias[:, c:c + 1] if bias is not None else 0.0)
                    ins.then_inc(take[c], 1)


def load(nc, tag, pairs):
    with phase(nc, tag, "sync_loaded act_loaded") as (block, s):
        @block.sync
        def _(sync):
            for to, src in pairs[0::2]:
                sync.dma_start(to, src).then_inc(s["sync_loaded"], 16)
            sync.wait_ge(s["sync_loaded"], 16 * len(pairs[0::2]))

        @block.scalar
        def _(act):
            for to, src in pairs[1::2]:
                act.dma_start(to, src).then_inc(s["act_loaded"], 16)
            if pairs[1::2]:
                act.wait_ge(s["act_loaded"], 16 * len(pairs[1::2]))


def decoder_ffn(nc, tag, T, w, rows):
    with phase(nc, tag, "gate_full0 gate_full1 up_full0 up_full1 silu_done act_done down_full down_done") as (block, s):
        gate_full, up_full = (s["gate_full0"], s["gate_full1"]), (s["up_full0"], s["up_full1"])
        n_of = lambda h, f: h * FT + f

        @block.tensor
        def _(pe):
            for h in range(NH):
                for f in range(FT):
                    n = n_of(h, f)
                    for which, fullsem, bank in (("gate", gate_full, 0), ("up", up_full, 2)):
                        if n >= 2:
                            pe.wait_ge(s["silu_done"] if which == "gate" else s["act_done"], n - 1)
                        for c in range(C):
                            m = pe.matmul(T.four[:, bank + n % 2, :], w[which][:, c, f * P:(f + 1) * P],
                                          T.hT[:, c, h * HALF:(h + 1) * HALF], start=c == 0, stop=c == C - 1)
                        m.then_inc(fullsem[n % 2], 1)
                for i in range(4):
                    k = 4 * h + i
                    if i == 0:
                        pe.wait_ge(s["act_done"], n_of(h, FT - 1) + 1)
                    if k >= 2:
                        pe.wait_ge(s["down_done"], k - 1)
                    for f in range(FT):
                        m = pe.matmul(T.ring[k % 2][:, 0:D], T.ffn[:, f, i * P:(i + 1) * P], w["down"][:, f, :],
                                      start=f == 0, stop=f == FT - 1)
                    m.then_inc(s["down_full"], 1)

        @block.scalar
        def _(act):
            for n in range(NH * FT):
                act.wait_ge(gate_full[n % 2], n // 2 + 1)
                if n >= 2:
                    act.wait_ge(s["act_done"], n - 1)
                act.activation(T.silu[:, n % 2, :], T.four[:, n % 2, :], ACT.Silu).then_inc(s["silu_done"], 1)

        @block.vector
        def _(dve):
            for h in range(NH):
                for f in range(FT):
                    n = n_of(h, f)
                    dve.wait_ge(up_full[n % 2], n // 2 + 1)
                    dve.wait_ge(s["silu_done"], n + 1)
                    if f == 0 and h:
                        dve.wait_ge(s["down_full"], 4 * h)
                    dve.tensor_tensor(T.ffn[:, f, :], T.four[:, 2 + n % 2, :], T.silu[:, n % 2, :],
                                      ALU.mult).then_inc(s["act_done"], 1)
                for i in range(4):
                    k = 4 * h + i
                    dve.wait_ge(s["down_full"], k + 1)
                    dve.tensor_tensor(rows(k), T.ring[k % 2][:, 0:D], rows(k), ALU.add).then_inc(s["down_done"], 1)


def constants(nc, enter, a):
    K = Names()

    def sb(name, shape, dt=F32):
        return enter(nc.sbuf_tensor(name, shape, dt))

    ident, fold, trig = sb("ident", [P, P]), sb("fold", [P, P]), sb("trig", [P, S])
    spread, spread_wide = sb("spread", [P, P]), sb("spread_wide", [P, P])
    table, ones = sb("mask_table", [P, 2, P]), sb("ones", [P, P])
    cols, powers = sb("const_cols", [P, 16]), sb("powers", [P, 2, TT])
    ident_bf, mask_bf = sb("ident_bf", [P, P], BF16), sb("mask_bf", [P, 2, P], BF16)
    load(nc, "constants", [(ident[:, :], a["c_ident"]), (fold[:, :], a["c_fold"]), (trig[:, :], a["c_trig"]),
                           (spread[:, :], a["c_spread"]), (spread_wide[:, :], a["c_spread_wide"]),
                           (table[:, :, :], a["c_mask"]), (cols[:, :], a["c_cols"])])
    with phase(nc, "constants_made", "made") as (block, s):
        @block.vector
        def _(dve):
            dve.tensor_copy(ident_bf[:, :], ident[:, :]).then_inc(s["made"], 1)
            dve.tensor_copy(mask_bf[:, :, :], table[:, :, :]).then_inc(s["made"], 1)
            dve.memset(ones[:, :], 1.0).then_inc(s["made"], 1)
            dve.memset(powers[:, 0, :], -0.5).then_inc(s["made"], 1)
            dve.memset(powers[:, 1, :], 0.5).then_inc(s["made"], 1)
    K.ident, K.fold, K.trig = ident[:, :], fold[:, :], trig[:, :]
    K.spread, K.spread_wide = spread[:, :], spread_wide[:, :]
    K.ident_bf, K.mask_q, K.mask_k = ident_bf[:, :], mask_bf[:, 0, :], mask_bf[:, 1, :]
    K.minus_half, K.half = powers[:, 0, :], powers[:, 1, :]
    K.ones, K.ones_row = ones[:, :], ones[0:1, :]
    K.zero4, K.one4, K.one_wide = cols[:, 0:4], cols[:, 4:8], cols[:, 8:12]
    K.key = cols[:, 12:13]
    K.key_back = cols[:, 13:14]
    return K


def tensors(nc, enter):
    T = Names()

    def sb(name, shape, dt=F32):
        return enter(nc.sbuf_tensor(name, shape, dt))

    T.X = sb("main_rows", [P, TT, D])
    T.Y = sb("inner_rows", [P, TT, D])
    T.hT = sb("normed_T", [P, C, S])
    T.bn, T.mv = sb("bn_stats", [P, TT, 6]), sb("mean_var", [P, TT, 2])
    T.msq, T.rstd = sb("mean_square", [P, TT]), sb("rstd", [P, TT])
    banks = [enter(nc.psum_tensor(n, [P, HALF], F32)) for n in ("ring0", "ring1")]
    T.ring = banks
    T.scores = enter(nc.psum_tensor("scores", [P, 2, 2, HALF], F32))
    T.heads_ps = enter(nc.psum_tensor("heads_ps", [P, NH, HALF], F32))
    T.four = T.scores[:, :, :, :].rearrange("p a b c -> p (a b) c")
    return T


def attention_tensors(nc, enter, T, tag):
    def sb(name, shape, dt=F32):
        return enter(nc.sbuf_tensor(tag + "_" + name, shape, dt))

    T.stack_q, T.stack_k = sb("stack_q", [P, 2, 4, S], BF16), sb("stack_k", [P, 2, 4, S], BF16)
    T.q_slots, T.k_slots = (x[:, 0, :, :].rearrange("p j s -> p (j s)").bitcast(F32).rearrange("p (u s) -> p u s", u=2)
                            for x in (T.stack_q, T.stack_k))
    T.q_narrow, T.k_narrow = T.stack_q[:, 1, 0:2, :], T.stack_k[:, 1, 0:2, :]
    T.parts = sb("parts", [P, 2, 3, S], BF16)
    T.rest = sb("rest", [P, 2, HALF])
    T.shift_rows = sb("shift_rows", [P, S], BF16)
    T.values = sb("values", [P, 2, TB, P])
    T.probs = sb("probs", [P, 2, 4, HALF])
    T.heads_sb = sb("heads_sb", [P, NH, HALF])
    T.normed = T.probs[:, 0, :, :].rearrange("p a b -> p (a b)").rearrange("p (t d) -> p t d", d=D)
    T.denominators = sb("denominators", [P, HALF])
    T.heads_out = sb("heads_out", [P, 4, S])
    T.turned = sb("turned", [P, 2, HALF])
    T.shift = sb("shift", [P, TB, P])
    T.shift_bf = T.shift[:, :, :].rearrange("p i r -> p (i r)").bitcast(BF16)[:, 0:S].rearrange("p (i r) -> p i r", r=P)
    T.maxima = sb("maxima", [P, 2, TB, 4])


def decoder(nc, a, T, K):
    with ExitStack() as stage:
        enter = stage.enter_context

        def sb(name, shape, dt=F32):
            return enter(nc.sbuf_tensor("dec_" + name, shape, dt))

        attention_tensors(nc, enter, T, "dec")
        T.silu = T.turned
        T.ffn = T.probs[:, :, :, :].rearrange("p a b c -> p (a b) c")
        slots = sb("w_slots", [P, 5, C, 4, P])
        slots_v = sb("w_cross_v", [P, C, 4, P])
        outs = sb("w_outs", [P, 2, 4, D])
        rows_flat = T.X[:, :, :].rearrange("p t d -> p (t d)")
        gate, up = (rows_flat[:, n * C * FF:(n + 1) * C * FF].rearrange("p (c f) -> p c f", c=C) for n in range(2))
        down = sb("w_down", [P, FT, D])
        v_row = sb("v_row", [1, 2, 4, P])
        qk_bias = sb("qk_bias", [P, 2, 4])
        norms = sb("norm_scales", [P, 3, C])
        ctxT, ctxb = sb("ctxT", [P, B, C, CTX]), sb("ctxT_b", [P, C, CTX])
        seg_i = T.heads_sb[0:CTX, :, :].rearrange("p h s -> p (h s)").bitcast(I32)
        mask = sb("mask_b", [CTX, S], BF16)
        mask_f, mask_g = T.heads_out[0:CTX, 0, :], T.heads_out[0:CTX, 1, :]

        load(nc, "decoder_in", [(ctxT[:, :, :, :], a["ctxT"]),
                                ])
        normalise(nc, "decoder_start", T, K, lambda i: T.X[:, i, :], TT, None, 1e-5, True,
                  write=lambda i: T.Y[:, i, :])
        load(nc, "park", [(a["parked"], rows_flat)])
        with nc.Fori(0, LAYERS) as layer:
            at = lambda name: a[name][bass.ds(layer, 1)].rearrange("o p x -> (o p) x")
            load(nc, "layer_weights", [
                (slots[:, 0:3].rearrange("p a c g s -> p (a c g s)"), at("w_slots")[:, 0:3 * C * 4 * P]),
                (outs[:, :, :, :].rearrange("p c g s -> p (c g s)"), at("w_outs")),
                (v_row[:, :, :, :].rearrange("p c g s -> p (c g s)"), at("v_row")),
                (qk_bias[:, :, :].rearrange("p c g -> p (c g)"), at("qk_bias")),
                (norms[:, :, :].rearrange("p c g -> p (c g)"), at("norm_scales")),
            ])
            later = [
                (slots[:, 3:5].rearrange("p a c g s -> p (a c g s)"), at("w_slots")[:, 3 * C * 4 * P:]),
                (slots_v[:, :, :, :].rearrange("p c g s -> p (c g s)"), at("w_cross_v")),
                (gate.rearrange("p c f -> p (c f)"), at("w_gate")),
                (up.rearrange("p c f -> p (c f)"), at("w_up")),
                (down[:, :, :].rearrange("p c f -> p (c f)"), at("w_down"))]
            w_self = {"q": slots[:, 0], "k": slots[:, 1], "v": slots[:, 2], "v_row": v_row[:, 0], "o": outs[:, 0],
                      "q_bias": qk_bias[:, 0], "k_bias": qk_bias[:, 1], "q_slot_bias": K.zero4, "k_slot_bias": K.one4,
                      "spread": K.spread}
            w_cross = {"q": slots[:, 3], "k": slots[:, 4], "v": slots_v[:, :, :, :], "v_row": v_row[:, 1],
                       "o": outs[:, 1], "q_slot_bias": K.zero4, "k_slot_bias": K.one4, "spread": K.spread,
                       "mask": mask}
            with nc.Fori(0, B) as b:
                def rows(i):
                    return T.Y[:, bass.ds(b * TB + i, 1), :].rearrange("p o d -> p (o d)")

                def cross_inputs(dve, sem):
                    seg = seg_i
                    dve.tensor_copy(ctxb[:, :, :], ctxT[:, bass.ds(b, 1), :, :].rearrange("p o c s -> p (o c) s")).then_inc(sem, 1)
                    dve.tensor_scalar(mask_f, seg, K.key[0:CTX, :], MASKED, ALU.is_lt, ALU.mult).then_inc(sem, 1)
                    dve.tensor_scalar(mask_g, seg, K.key_back[0:CTX, :], MASKED, ALU.is_ge, ALU.mult).then_inc(sem, 1)
                    dve.wait_ge(sem, 3)
                    dve.tensor_tensor(mask[:, :], mask_f, mask_g, ALU.min).then_inc(sem, 1)

                normalise(nc, "norm1", T, K, rows, TB, T.hT, 1e-6, False, (norms[:, 0, :], None))
                attention(nc, "self", T, K, "rope", T.hT, T.hT, w_self, 4, HD, True, S, 0.25, rows, later)
                load(nc, "segments", [(seg_i, a["seg"][bass.ds(b * S, S)].partition_broadcast(CTX))])
                normalise(nc, "norm2", T, K, rows, TB, T.hT, 1e-6, False, (norms[:, 1, :], None), extra=cross_inputs)
                attention(nc, "cross", T, K, "cross", T.hT, ctxb, w_cross, 4, HD, False, CTX, 0.25, rows)
                normalise(nc, "norm3", T, K, rows, TB, T.hT, 1e-6, False, (norms[:, 2, :], None))
                decoder_ffn(nc, "ffn", T, {"gate": gate, "up": up, "down": down}, rows)
        nf = T.hT[:, 0, 0:D]
        load(nc, "unpark", [(rows_flat, a["parked"])])
        load(nc, "last_scale", [(nf, a["nf"].partition_broadcast(P))])
        normalise(nc, "decoder_end", T, K, lambda i: T.Y[:, i, :], TT, None, 1e-6, False,
                  write=lambda i: T.Y[:, i, :])
        with phase(nc, "decoder_add", "scaled") as (block, s):
            @block.vector
            def _(dve):
                for i in range(TT):
                    dve.tensor_tensor(T.Y[:, i, :], T.Y[:, i, :], nf, ALU.mult).then_inc(s["scaled"], 1)
                for i in range(TT):
                    dve.wait_ge(s["scaled"], i + 1)
                    dve.tensor_tensor(T.X[:, i, :], T.X[:, i, :], T.Y[:, i, :], ALU.add)


def trajectories(nc, a, T, K):
    G = 128
    with ExitStack() as stage:
        enter = stage.enter_context

        def sb(name, shape, dt=F32):
            return enter(nc.sbuf_tensor("traj_" + name, shape, dt))

        diffs, weighted = sb("diffs", [P, TT, D]), sb("weighted", [P, TT, D + 1])
        guide, guide_n, guide_T = sb("guide", [P, D + 1]), sb("guide_n", [P, D]), sb("guide_T", [P, C, P])
        square = sb("square", [P, 2, D])
        likeness = sb("likeness", [P, 2, HALF])
        unit, unit_T = sb("unit", [P, 2, D]), sb("unit_T", [P, C, HALF])
        base = sb("base", [P, 2, D])
        band = sb("band", [P, 3, P])
        m = {n: sb("mag_" + n, [P, TT]) for n in "sq norm valid safe inv a ra inv2 tanh c06 c04 share".split()}
        g = {n: sb("g_" + n, [P, 1]) for n in "sq norm floor inv".split()}
        winv = sb("weight_inv", [P, TT])

        normalise(nc, "traj_norm", T, K, lambda i: T.X[:, i, :], TT, None, 1e-5, True, write=lambda i: T.Y[:, i, :])
        load(nc, "shifted", [
            (diffs[0:P - 1, :, :], T.Y[1:P, :, :]), (diffs[P - 1:P, 0:TT - 1, :], T.Y[0:1, 1:TT, :]),
            (diffs[P - 1:P, TT - 1, :], T.Y[P - 1:P, TT - 1, :]),
            (guide[:, 0:D], a["guide"]), (band[:, :, :], a["c_band"])])
        with phase(nc, "diffs", "diff squared root root_g chain tanh ones gn gt gtaken") as (block, s):
            @block.scalar
            def _(act):
                act.activation(square[:, 0, :], guide[:, 0:D], ACT.Square, accum_out=g["sq"][:, :]).then_inc(s["squared"], 1)
                for i in range(TT):
                    act.wait_ge(s["diff"], i + 1)
                    act.wait_ge(s["squared"], i + 1)
                    act.activation(square[:, 0, :], diffs[:, i, :], ACT.Square,
                                   accum_out=m["sq"][:, i:i + 1]).then_inc(s["squared"], 1)
                act.wait_ge(s["root"], 1)
                act.activation(m["tanh"][:, :], m["norm"][:, :], ACT.Tanh, scale=2.0).then_inc(s["tanh"], 1)
                for c in range(C):
                    act.wait_ge(s["gt"], c + 1)
                    act.activation(guide_T[:, c, :], T.ring[c][:, 0:P], ACT.Copy).then_inc(s["gtaken"], 1)

            @block.gpsimd
            def _(pool):
                pool.memset(guide[:, D:D + 1], 1.0).then_inc(s["ones"], 1)
                pool.wait_ge(s["squared"], 1)
                pool.tensor_tensor(g["norm"][:, :], g["sq"][:, :], K.half[:, 0:1], ALU.pow).then_inc(s["root_g"], 1)
                pool.wait_ge(s["squared"], TT + 1)
                pool.tensor_tensor(m["norm"][:, :], m["sq"][:, :], K.half, ALU.pow).then_inc(s["root"], 1)

            @block.tensor
            def _(pe):
                pe.wait_ge(s["gn"], 1)
                for c in range(C):
                    pe.transpose(T.ring[c][:, 0:P], guide_n[:, c * P:(c + 1) * P], K.ident).then_inc(s["gt"], 1)

            @block.vector
            def _(dve):
                for i in range(TT):
                    dve.tensor_tensor(diffs[:, i, :], diffs[:, i, :], T.Y[:, i, :], ALU.subtract).then_inc(s["diff"], 1)
                t = Tally(dve, s["chain"])
                dve.wait_ge(s["root_g"], 1)
                t.add(dve.tensor_scalar(g["floor"][:, :], g["norm"][:, :], 1e-8, None, ALU.max)); t.wait()
                t.add(dve.reciprocal(g["inv"][:, :], g["floor"][:, :])); t.wait()
                dve.tensor_scalar(guide_n[:, :], guide[:, 0:D], g["inv"][:, :], None, ALU.mult).then_inc(s["gn"], 1)
                dve.wait_ge(s["root"], 1)
                v = lambda n: m[n][:, :]
                t.add(dve.tensor_scalar(v("valid"), v("norm"), 1e-6, None, ALU.is_gt)); t.wait()
                t.add(dve.tensor_tensor(v("safe"), v("norm"), v("valid"), ALU.mult)); t.wait()
                t.add(dve.scalar_tensor_tensor(v("safe"), v("safe"), 1.0, v("valid"), ALU.add, ALU.subtract)); t.wait()
                t.add(dve.reciprocal(v("inv"), v("safe"))); t.wait()
                t.add(dve.tensor_tensor(v("inv"), v("inv"), v("valid"), ALU.mult)); t.wait()
                t.add(dve.tensor_tensor(v("a"), v("norm"), v("inv"), ALU.mult)); t.wait()
                t.add(dve.tensor_scalar(v("a"), v("a"), 1e-8, None, ALU.max)); t.wait()
                t.add(dve.reciprocal(v("ra"), v("a"))); t.wait()
                t.add(dve.tensor_tensor(v("inv2"), v("inv"), v("ra"), ALU.mult)); t.wait()
                dve.wait_ge(s["tanh"], 1)
                t.add(dve.scalar_tensor_tensor(v("c06"), v("inv"), 0.6, v("tanh"), ALU.mult, ALU.mult)); t.wait()
                t.add(dve.tensor_scalar(v("c04"), v("tanh"), 0.4, None, ALU.mult)); t.wait()
                t.add(dve.tensor_copy(weighted[:, :, D], v("tanh")))

        with phase(nc, "guided", "unit turned0 turned1 taken0 taken1 dots exp infl0 infl1 based share done") as (block, s):
            turned, taken, infl = (s["turned0"], s["turned1"]), (s["taken0"], s["taken1"]), (s["infl0"], s["infl1"])
            QUADS = TT // 4
            spot = lambda n: T.four[:, 2 + n % 2, 0:D + 1]

            @block.tensor
            def _(pe):
                for q in range(QUADS):
                    for i in range(4):
                        n = 4 * q + i
                        pe.wait_ge(s["unit"], n + 1)
                        for c in range(C):
                            if q and i == 0:
                                pe.wait_ge(taken[c], q)
                            t = pe.transpose(T.ring[c][:, i * P:(i + 1) * P], unit[:, n % 2, c * P:(c + 1) * P], K.ident)
                            t.then_inc(turned[c], 1)
                    if q >= 2:
                        pe.wait_ge(s["exp"], q - 1)
                    for c in range(C):
                        pe.wait_ge(taken[c], q + 1)
                    for c in range(C):
                        t = pe.matmul(T.four[:, q % 2, :], guide_T[:, c, :], unit_T[:, c, :], start=c == 0, stop=c == C - 1)
                    t.then_inc(s["dots"], 1)
                    pe.wait_ge(s["exp"], q + 1)
                    for i in range(4):
                        n = 4 * q + i
                        if n >= 2:
                            pe.wait_ge(s["done"], n - 1)
                        pe.matmul(spot(n), likeness[:, q % 2, i * P:(i + 1) * P], guide[:, :],
                                  start=True, stop=True).then_inc(infl[n % 2], 1)

            @block.scalar
            def _(act):
                for q in range(QUADS):
                    for c in range(C):
                        act.wait_ge(turned[c], 4 * q + 4)
                        if q:
                            act.wait_ge(s["dots"], q)
                        act.activation(unit_T[:, c, :], T.ring[c][:, :], ACT.Copy).then_inc(taken[c], 1)
                    act.wait_ge(s["dots"], q + 1)
                    if q >= 2:
                        act.wait_ge(infl[1], 2 * (q - 1))
                    act.activation(likeness[:, q % 2, :], T.four[:, q % 2, :], ACT.Exp, scale=2.0).then_inc(s["exp"], 1)

            @block.vector
            def _(dve):
                for q in range(QUADS):
                    for i in range(4):
                        n = 4 * q + i
                        if n >= 2:
                            dve.wait_ge(turned[1], n - 1)
                        dve.tensor_scalar(unit[:, n % 2, :], diffs[:, n, :], m["inv2"][:, n:n + 1], None,
                                          ALU.mult).then_inc(s["unit"], 1)
                    for i in range(4):
                        n = 4 * q + i
                        if n >= 2:
                            dve.wait_ge(s["done"], n - 1)
                        dve.tensor_scalar(base[:, n % 2, :], diffs[:, n, :], m["c06"][:, n:n + 1], None,
                                          ALU.mult).then_inc(s["based"], 1)
                        dve.wait_ge(infl[n % 2], n // 2 + 1)
                        dve.reciprocal(m["share"][:, n:n + 1], spot(n)[:, D:D + 1]).then_inc(s["share"], 1)
                        dve.wait_ge(s["share"], 2 * n + 1)
                        dve.tensor_tensor(m["share"][:, n:n + 1], m["share"][:, n:n + 1], m["c04"][:, n:n + 1],
                                          ALU.mult).then_inc(s["share"], 1)
                        dve.wait_ge(s["share"], 2 * n + 2)
                        dve.wait_ge(s["based"], n + 1)
                        dve.scalar_tensor_tensor(weighted[:, n, 0:D], spot(n)[:, 0:D], m["share"][:, n:n + 1],
                                                 base[:, n % 2, :], ALU.mult, ALU.add).then_inc(s["done"], 1)

        with phase(nc, "windows", "sum0 sum1 floor inverse added") as (block, s):
            full = (s["sum0"], s["sum1"])

            @block.tensor
            def _(pe):
                for n in range(TT):
                    if n >= 2:
                        pe.wait_ge(s["added"], n - 1)
                    first = n % TB == 0
                    t = pe.matmul(T.ring[n % 2][:, 0:D + 1], band[:, 0 if first else 1, :], weighted[:, n, :],
                                  start=True, stop=first)
                    if not first:
                        t = pe.matmul(T.ring[n % 2][:, 0:D + 1], band[:, 2, :], weighted[:, n - 1, :],
                                      start=False, stop=True)
                    t.then_inc(full[n % 2], 1)

            @block.vector
            def _(dve):
                for n in range(TT):
                    dve.wait_ge(full[n % 2], n // 2 + 1)
                    dve.tensor_scalar(winv[:, n:n + 1], T.ring[n % 2][:, D:D + 1], 1e-8, None,
                                      ALU.max).then_inc(s["floor"], 1)
                    dve.wait_ge(s["floor"], n + 1)
                    dve.reciprocal(winv[:, n:n + 1], winv[:, n:n + 1]).then_inc(s["inverse"], 1)
                    dve.wait_ge(s["inverse"], n + 1)
                    dve.scalar_tensor_tensor(T.X[:, n, :], T.ring[n % 2][:, 0:D], winv[:, n:n + 1], T.X[:, n, :],
                                             ALU.mult, ALU.add).then_inc(s["added"], 1)


def mixture_attention(nc, a, T, K):
    QC = NEXP * MHD
    with ExitStack() as stage:
        enter = stage.enter_context

        def sb(name, shape, dt=F32):
            return enter(nc.sbuf_tensor("mix_" + name, shape, dt))

        attention_tensors(nc, enter, T, "mix")
        T.q_tok, T.k_tok = T.heads_out[:, 1, :].rearrange("p (i c) -> p i c", c=P), T.heads_out[:, 2, :].rearrange("p (i c) -> p i c", c=P)
        sim, sim_n = sb("sim", [P, C, NEXP]), sb("sim_n", [P, C, NEXP])
        sim_inv = sb("sim_inv", [P, NEXP])
        gates = sb("gates", [P, NEXP])
        proj = sb("w_mix_qkv", [P, 3, C, QC])
        w_o = sb("w_mix_o", [P, 8, D])
        mixed = T.probs[:, :, :, :].rearrange("p a b c -> p (a b c)")[:, 0:2 * QC].rearrange("p (u c) -> p u c", u=2)
        mixed_T = T.values[:, :, :, :].rearrange("p a i c -> p a (i c)")
        n_sq, n_inv = sb("norm_sq", [P, TB]), sb("norm_inv", [P, TB])
        big = [sb(f"gate_{n}", [P, TB, NEXP]) for n in ("logits", "mask", "work", "sel", "left", "weights", "expd")]
        logits, mask, work, sel, left, weights, expd = big
        few = [sb(f"gate1_{n}", [P, TB]) for n in ("any", "max", "sum")]
        anyone, most, total = few
        order = sb("order", [P, TB, NEXP])
        share = sb("share", [P, D])

        load(nc, "mixture_in", [(sim[:, :, :].rearrange("p c e -> p (c e)"), a["sim"]), (gates[:, :], a["gates"].partition_broadcast(P)),
                                (proj[:, :, :, :].rearrange("p a c e -> p (a c e)"), a["mix_qkv"]),
                                (w_o[:, :, :].rearrange("p c e -> p (c e)"), a["mix_o"]),
                                (order[:, :, :].rearrange("p c e -> p (c e)"), a["c_order"])])
        with phase(nc, "experts_norm", "squared summed root inverse chain") as (block, s):
            @block.vector
            def _(dve):
                t = Tally(dve, s["chain"])
                dve.tensor_tensor(work[:, 0:C, :], sim[:, :, :], sim[:, :, :], ALU.mult).then_inc(s["squared"], 1)
                dve.wait_ge(s["summed"], 1)
                t.add(dve.tensor_copy(sel[:, 0, :], T.ring[0][:, 0:NEXP])); t.wait()
                dve.wait_ge(s["root"], 1)
                t.add(dve.tensor_scalar(sim_inv[:, :], sim_inv[:, :], 1e-12, None, ALU.max)); t.wait()
                t.add(dve.reciprocal(sim_inv[:, :], sim_inv[:, :])); t.wait()
                for c in range(C):
                    dve.tensor_tensor(sim_n[:, c, :], sim[:, c, :], sim_inv[:, :], ALU.mult)

            @block.tensor
            def _(pe):
                pe.wait_ge(s["squared"], 1)
                for c in range(C):
                    t = pe.matmul(T.ring[0][:, 0:NEXP], K.ones, work[:, c, :], start=c == 0, stop=c == C - 1)
                t.then_inc(s["summed"], 1)

            @block.gpsimd
            def _(pool):
                pool.wait_ge(s["chain"], 1)
                pool.tensor_tensor(sim_inv[:, :], sel[:, 0, :], K.half[:, 0:NEXP], ALU.pow).then_inc(s["root"], 1)

            @block.scalar
            def _(act):
                act.activation(gates[:, :], gates[:, :], ACT.Sigmoid)

        with nc.Fori(0, B) as b:
            def rows(i):
                return T.X[:, bass.ds(b * TB + i, 1), :].rearrange("p o d -> p (o d)")

            normalise(nc, "mix_norm", T, K, rows, TB, T.hT, 1e-5, True)
            with phase(nc, "gate", "squared root inverse dots0 dots1 scaled chain exp gated") as (block, s):
                dots = (s["dots0"], s["dots1"])

                @block.scalar
                def _(act):
                    for i in range(TB):
                        if i:
                            act.wait_ge(s["squared"], i)
                        act.activation(share[:, :], T.normed[:, i, :], ACT.Square,
                                       accum_out=n_sq[:, i:i + 1]).then_inc(s["squared"], 1)
                    act.wait_ge(s["gated"], 1)
                    act.activation(expd[:, :, :], work[:, :, :], ACT.Exp).then_inc(s["exp"], 1)

                @block.gpsimd
                def _(pool):
                    pool.wait_ge(s["squared"], TB)
                    pool.tensor_tensor(n_inv[:, :], n_sq[:, :], K.half[:, 0:TB], ALU.pow).then_inc(s["root"], 1)

                @block.tensor
                def _(pe):
                    for i in range(TB):
                        if i >= 2:
                            pe.wait_ge(s["scaled"], i - 1)
                        for c in range(C):
                            t = pe.matmul(T.ring[i % 2][:, 0:NEXP], T.hT[:, c, i * P:(i + 1) * P], sim_n[:, c, :],
                                          start=c == 0, stop=c == C - 1)
                        t.then_inc(dots[i % 2], 1)

                @block.vector
                def _(dve):
                    t = Tally(dve, s["chain"])
                    step = lambda ins: (t.add(ins), t.wait())
                    across = lambda x: x[:, :].unsqueeze(2).to_broadcast([P, TB, NEXP])
                    f = lambda x: x[:, :, :]
                    dve.wait_ge(s["root"], 1)
                    step(dve.tensor_scalar(n_inv[:, :], n_inv[:, :], 1e-12, None, ALU.max))
                    step(dve.reciprocal(n_inv[:, :], n_inv[:, :]))
                    for i in range(TB):
                        dve.wait_ge(dots[i % 2], i // 2 + 1)
                        dve.scalar_tensor_tensor(logits[:, i, :], T.ring[i % 2][:, 0:NEXP], n_inv[:, i:i + 1],
                                                 gates[:, :], ALU.mult, ALU.subtract).then_inc(s["scaled"], 1)
                    dve.wait_ge(s["scaled"], TB)
                    step(dve.tensor_scalar(f(mask), f(logits), 0.0, None, ALU.is_gt))
                    step(dve.tensor_reduce(anyone[:, :], f(mask), AX.X, ALU.max))
                    step(dve.tensor_scalar(anyone[:, :], anyone[:, :], -1.0, 1.0, ALU.mult, ALU.add))
                    step(dve.tensor_copy(f(left), f(logits)))
                    for k in range(2):
                        step(dve.tensor_reduce(most[:, :], f(left), AX.X, ALU.max))
                        step(dve.tensor_tensor(f(sel), f(left), across(most), ALU.is_equal))
                        step(dve.tensor_tensor(f(sel), f(sel), f(order), ALU.mult))
                        step(dve.tensor_reduce(most[:, :], f(sel), AX.X, ALU.max))
                        step(dve.tensor_tensor(f(sel), f(order), across(most), ALU.is_equal))
                        step(dve.scalar_tensor_tensor(f(left), f(sel), -1e9, f(left), ALU.mult, ALU.add))
                        step(dve.tensor_tensor(f(sel), f(sel), across(anyone), ALU.mult))
                        step(dve.tensor_tensor(f(mask), f(mask), f(sel), ALU.add))
                    dve.tensor_scalar(f(work), f(logits), 0.0, None, ALU.max).then_inc(s["gated"], 1)
                    dve.wait_ge(s["exp"], 1)
                    step(dve.tensor_tensor(f(weights), f(expd), f(mask), ALU.mult))
                    step(dve.tensor_reduce(total[:, :], f(weights), AX.X, ALU.add))
                    step(dve.reciprocal(total[:, :], total[:, :]))
                    step(dve.tensor_tensor(f(weights), f(weights), across(total), ALU.mult))

            with phase(nc, "mix_project", "cleared full scaled0 scaled1 summed") as (block, s):
                @block.gpsimd
                def _(pool):
                    pool.memset(T.heads_out[:, 1:3, :], 0.0).then_inc(s["cleared"], 1)
                    pool.memset(T.values[:, 0, :, MHD:P], 0.0).then_inc(s["cleared"], 1)
                    pool.wait_ge(s["cleared"], 2)
                    pool.memset(T.values[:, 0, :, MHD:MHD + 1], 1.0).then_inc(s["cleared"], 1)

                jobs = [(i, x) for i in range(TB) for x in range(3)]

                @block.tensor
                def _(pe):
                    for n, (i, x) in enumerate(jobs):
                        if n >= 2:
                            pe.wait_ge(s["scaled0"], n - 1)
                        for h in range(2):
                            for c in range(C):
                                t = pe.matmul(T.scores[:, n % 2, h, :], T.hT[:, c, i * P:(i + 1) * P],
                                              proj[:, x, c, h * HALF:(h + 1) * HALF], start=c == 0, stop=c == C - 1)
                        t.then_inc(s["full"], 1)

                @block.vector
                def _(dve):
                    dve.wait_ge(s["cleared"], 3)
                    for n, (i, x) in enumerate(jobs):
                        dve.wait_ge(s["full"], n + 1)
                        if n >= 2:
                            dve.wait_ge(s["summed"], n - 1)
                        by = weights[:, i, :].unsqueeze(2).to_broadcast([P, NEXP, MHD])
                        dve.tensor_tensor(mixed[:, n % 2, :].rearrange("p (e d) -> p e d", d=MHD),
                                          T.scores[:, n % 2, :, :].rearrange("p h (e d) -> p (h e) d", d=MHD),
                                          by, ALU.mult).then_inc(s["scaled0"], 1)
                        dve.wait_ge(s["scaled0"], n + 1)
                        to = (T.q_tok[:, i, 0:MHD], T.k_tok[:, i, 0:MHD], T.values[:, 0, i, 0:MHD])[x]
                        dve.tensor_reduce(to, mixed[:, n % 2, :].rearrange("p (e d) -> p d e", d=MHD), AX.X,
                                          ALU.add).then_inc(s["summed"], 1)

            w = {"q_slot_bias": K.zero4, "k_slot_bias": K.one_wide, "spread": K.spread_wide}
            attention(nc, "mix", T, K, "given", None, None, w, 1, MHD, True, S, 0.125, None)

            with phase(nc, "mix_out", "turned0 turned1 mixed spread0 spread1 copied out0 out1 added") as (block, s):
                turned, out = (s["turned0"], s["turned1"]), (s["out0"], s["out1"])

                @block.tensor
                def _(pe):
                    for i in range(TB):
                        if i >= 2:
                            pe.wait_ge(s["mixed"], i - 1)
                        pe.matmul(T.ring[i % 2][:, 0:P], T.heads_out[:, 0, i * P:(i + 1) * P], K.ident, start=True,
                                  stop=True).then_inc(turned[i % 2], 1)
                        pe.wait_ge(s["mixed"], i + 1)
                        if i >= 2:
                            pe.wait_ge(s["copied"], i - 1)
                        for e in range(8):
                            t = pe.transpose(T.scores[:, i % 2, e // 4, (e % 4) * P:(e % 4 + 1) * P],
                                             mixed[:, i % 2, e * P:(e + 1) * P], K.ident)
                        t.then_inc(s["spread0"], 1)
                        pe.wait_ge(s["copied"], i + 1)
                        if i >= 2:
                            pe.wait_ge(s["added"], i - 1)
                        for e in range(8):
                            t = pe.matmul(T.heads_ps[:, i % 2, 0:D], mixed_T[:, i % 2, e * P:(e + 1) * P], w_o[:, e, :],
                                          start=e == 0, stop=e == 7)
                        t.then_inc(out[i % 2], 1)

                @block.scalar
                def _(act):
                    for i in range(TB):
                        act.wait_ge(s["spread0"], i + 1)
                        if i >= 2:
                            act.wait_ge(out[i % 2], i // 2)
                        act.activation(mixed_T[:, i % 2, :], T.scores[:, i % 2, :, :].rearrange("p a b -> p (a b)"),
                                       ACT.Copy).then_inc(s["copied"], 1)

                @block.vector
                def _(dve):
                    for i in range(TB + 1):
                        if i < TB:
                            dve.wait_ge(turned[i % 2], i // 2 + 1)
                            if i >= 2:
                                dve.wait_ge(s["spread0"], i - 1)
                            dve.tensor_tensor(mixed[:, i % 2, :].rearrange("p (e d) -> p e d", d=MHD),
                                              T.ring[i % 2][:, 0:MHD].unsqueeze(1).to_broadcast([P, NEXP, MHD]),
                                              weights[:, i, :].unsqueeze(2).to_broadcast([P, NEXP, MHD]),
                                              ALU.mult).then_inc(s["mixed"], 1)
                        if i:
                            k = i - 1
                            dve.wait_ge(out[k % 2], k // 2 + 1)
                            dve.tensor_tensor(rows(k), T.heads_ps[:, k % 2, 0:D], rows(k), ALU.add).then_inc(s["added"], 1)


def level_one_attention(nc, a, T, K, cross):
    tag = "x1" if cross else "s1"
    with ExitStack() as stage:
        enter = stage.enter_context

        def sb(name, shape, dt=F32):
            return enter(nc.sbuf_tensor(tag + "_" + name, shape, dt))

        attention_tensors(nc, enter, T, tag)
        wq, wk, wv = (sb("w1_" + n, [P, C, 4, P]) for n in "qkv")
        wo = sb("w1_o", [P, 4, D])
        v_row, bias = sb("v1_row", [1, 4, P]), sb("qk1_bias", [P, 2, 4])
        affine = sb("affine", [P, 2, C])
        ctxT, ctxb = sb("ctxT", [P, B, C, CTX]), sb("ctxT_b", [P, C, CTX])
        flat = lambda t: t[:, :, :, :].rearrange("p c g s -> p (c g s)")
        load(nc, tag + "_in", [
            (flat(wq), a[tag + "_q"]), (flat(wk), a[tag + "_k"]), (flat(wv), a[tag + "_v"]),
            (wo[:, :, :].rearrange("p g d -> p (g d)"), a[tag + "_o"]),
            (v_row[:, :, :].rearrange("p g d -> p (g d)"), a[tag + "_v_row"]),
            (bias[:, :, :].rearrange("p g d -> p (g d)"), a[tag + "_bias"]),
            (affine[:, :, :].rearrange("p g d -> p (g d)"), a["s1_affine"]),
            (ctxT[:, :, :, :], a["ctxT"])])
        w = {"q": wq[:, :, :, :], "k": wk[:, :, :, :], "v": wv[:, :, :, :], "o": wo[:, :, :], "v_row": v_row[:, :, :],
             "q_slot_bias": bias[:, 0, :], "k_slot_bias": bias[:, 1, :], "spread": K.spread}
        if not cross:
            normalise(nc, "s1_outer", T, K, lambda i: T.X[:, i, :], TT, None, 1e-5, True, write=lambda i: T.Y[:, i, :])
        with nc.Fori(0, B) as b:
            stream = T.X if cross else T.Y

            def rows(i):
                return stream[:, bass.ds(b * TB + i, 1), :].rearrange("p o d -> p (o d)")

            def context(dve, sem):
                dve.tensor_copy(ctxb[:, :, :], ctxT[:, bass.ds(b, 1), :, :].rearrange("p o c s -> p (o c) s")).then_inc(sem, 1)

            normalise(nc, tag + "_norm", T, K, rows, TB, T.hT, 1e-5, True,
                      None if cross else (affine[:, 0, :], affine[:, 1, :]), extra=context if cross else None)
            attention(nc, tag, T, K, "plain", T.hT, ctxb if cross else T.hT, w, 4, HD, False, CTX if cross else S,
                      0.25, rows)
        if not cross:
            with phase(nc, "s1_add", "added") as (block, s):
                @block.vector
                def _(dve):
                    for i in range(TT):
                        dve.tensor_tensor(T.X[:, i, :], T.X[:, i, :], T.Y[:, i, :], ALU.add)


def self_attention(nc, a, T, K):
    level_one_attention(nc, a, T, K, False)


def cross_attention(nc, a, T, K):
    level_one_attention(nc, a, T, K, True)


def gated_units(nc, tag, T, K, batches):
    names = "in0 in1 silu gated stats aggr floor rstd normed turned copied out0 out1 finished"
    with phase(nc, tag, names) as (block, s):
        full, out = (s["in0"], s["in1"]), (s["out0"], s["out1"])
        starts = [sum(len(x) for x in batches[:k]) for k in range(len(batches) + 1)]

        @block.tensor
        def _(pe):
            for k, batch in enumerate(batches):
                for n, u in enumerate(batch):
                    at = starts[k] + n
                    if at >= 2:
                        pe.wait_ge(s["gated"], at - 1)
                    for c in range(C):
                        pe.matmul(T.ring[at % 2][:, 0:2 * H1], u["x"][:, c, :], u["w12"][:, c, :], start=c == 0, stop=False)
                    pe.matmul(T.ring[at % 2][:, 0:2 * H1], K.ones_row, u["b12"], start=False,
                              stop=True).then_inc(full[at % 2], 1)
                for n, u in enumerate(batch):
                    at = starts[k] + n
                    pe.wait_ge(s["normed"], at + 1)
                    if at >= 4:
                        pe.wait_ge(s["copied"], at - 3)
                    pe.transpose(T.four[:, at % 4, 0:P], T.unit_rows[:, k % 2, n, :], K.ident).then_inc(s["turned"], 1)
                for n, u in enumerate(batch):
                    at = starts[k] + n
                    pe.wait_ge(s["copied"], at + 1)
                    if at >= 2:
                        pe.wait_ge(s["finished"], at - 1)
                    pe.matmul(T.heads_ps[:, at % 2, 0:D], T.unit_T[:, at % 4, :], u["w3"], start=True, stop=False)
                    pe.matmul(T.heads_ps[:, at % 2, 0:D], K.ones_row, u["b3"], start=False,
                              stop=True).then_inc(out[at % 2], 1)

        @block.scalar
        def _(act):
            for k, batch in enumerate(batches):
                for n, u in enumerate(batch):
                    at = starts[k] + n
                    act.wait_ge(full[at % 2], at // 2 + 1)
                    if at >= 2:
                        act.wait_ge(s["gated"], at - 1)
                    act.activation(T.unit_silu[:, at % 2, :], T.ring[at % 2][:, 0:H1], ACT.Silu).then_inc(s["silu"], 1)
                for n, u in enumerate(batch):
                    at = starts[k] + n
                    act.wait_ge(s["turned"], at + 1)
                    if at >= 4:
                        act.wait_ge(out[at % 2], (at - 4) // 2 + 1)
                    act.activation(T.unit_T[:, at % 4, :], T.four[:, at % 4, 0:P], ACT.Identity, scale=u["scale"],
                                   bias=u["shift"]).then_inc(s["copied"], 1)

        @block.gpsimd
        def _(pool):
            for k, batch in enumerate(batches):
                pool.wait_ge(s["floor"], k + 1)
                pool.tensor_tensor(T.rstd[:, 0:len(batch)], T.msq[:, 0:len(batch)], K.minus_half[:, 0:len(batch)],
                                   ALU.pow).then_inc(s["rstd"], 1)

        @block.vector
        def _(dve):
            for k, batch in enumerate(batches):
                for n, u in enumerate(batch):
                    at = starts[k] + n
                    dve.wait_ge(s["silu"], at + 1)
                    if k >= 2 and n == 0:
                        dve.wait_ge(s["turned"], starts[k - 1])
                    dve.tensor_tensor(T.unit_rows[:, k % 2, n, :], T.ring[at % 2][:, H1:2 * H1], T.unit_silu[:, at % 2, :],
                                      ALU.mult).then_inc(s["gated"], 1)
                for n, u in enumerate(batch):
                    dve.wait_ge(s["gated"], starts[k] + n + 1)
                    dve.bn_stats(T.bn[:, n, :], T.unit_rows[:, k % 2, n, :]).then_inc(s["stats"], 1)
                if k:
                    dve.wait_ge(s["normed"], starts[k])
                for n, u in enumerate(batch):
                    dve.wait_ge(s["stats"], starts[k] + n + 1)
                    dve.bn_aggr(T.mv[:, n, :], T.bn[:, n, :]).then_inc(s["aggr"], 1)
                dve.wait_ge(s["aggr"], starts[k + 1])
                dve.tensor_scalar(T.msq[:, 0:len(batch)], T.mv[:, 0:len(batch), 1], 1e-5, None, ALU.add).then_inc(s["floor"], 1)
                dve.wait_ge(s["rstd"], k + 1)
                for n, u in enumerate(batch):
                    dve.tensor_scalar(T.unit_rows[:, k % 2, n, :], T.unit_rows[:, k % 2, n, :], T.mv[:, n, 0:1],
                                      T.rstd[:, n:n + 1], ALU.subtract, ALU.mult).then_inc(s["normed"], 1)
                for n, u in enumerate(batch):
                    at = starts[k] + n
                    dve.wait_ge(out[at % 2], at // 2 + 1)
                    if at:
                        dve.wait_ge(s["finished"], at)
                    u["finish"](dve, T.heads_ps[:, at % 2, 0:D]).then_inc(s["finished"], 1)


def expert_ffn(nc, a, T, K):
    with ExitStack() as stage:
        enter = stage.enter_context

        def sb(name, shape, dt=F32):
            return enter(nc.sbuf_tensor("moe_" + name, shape, dt))

        w12, b12 = sb("e_w12", [P, C, E1 + 1, 2 * H1]), sb("e_b12", [1, E1 + 1, 2 * H1])
        w3, b3 = sb("e_w3", [P, E1 + 1, D]), sb("e_b3", [1, E1 + 1, D])
        norms = sb("e_norms", [P, 4])
        wg, bg = sb("e_gate", [P, C, E1 + 1]), sb("e_gate_bias", [1, E1 + 1])
        exp_bias, order = sb("exp_bias", [P, E1]), sb("e_order", [P, NEXP])
        at_i, at_f = sb("at_int", [P, 2, M1], I32), sb("at_float", [P, 2, M1])
        col_i, col_f = sb("col_int", [P, 2, MT], I32), sb("col_float", [P, 2, MT])
        place = sb("token_number", [P, B * S])
        one_hot = sb("one_hot", [P, 2, B * S // 2])
        shared = sb("shared_rows", [P, TT, D])
        picked = sb("picked_T", [P, C, M1])
        values = sb("picked_values", [P, MT, D + 1])
        T.normed = sb("normed", [P, TB, D])
        T.unit_rows, T.unit_T, T.unit_silu = sb("unit_rows", [P, 2, 8, H1]), sb("unit_T", [P, 4, P]), sb("unit_silu", [P, 2, H1])
        score = sb("e_score", [P, MT, E1 + 1])
        names = "biased pick tmp mix expd".split()
        e = {n: sb("e_" + n, [P, MT, E1 + 1]) for n in names}
        one = {n: sb("e1_" + n, [P, MT]) for n in ("top", "sum")}
        count, keep = sb("count", [P, TT]), sb("keep", [P, TT])
        number = sb("number_by_tile", [P, TT])
        flat4 = lambda t: t[:, :, :, :].rearrange("p c e h -> p (c e h)")
        flat3 = lambda t: t[:, :, :].rearrange("p e h -> p (e h)")

        load(nc, "experts_in", [
            (flat4(w12), a["e_w12"]), (flat3(w3), a["e_w3"]), (flat3(b12), a["e_b12"]), (flat3(b3), a["e_b3"]),
            (norms[:, :], a["e_norms"]), (flat3(wg), a["e_gate"]), (bg[:, :], a["e_gate_bias"]),
            (exp_bias[:, :], a["e_bias"].partition_broadcast(P)), (order[:, :], a["c_order"][:, 0:NEXP]),
            (at_i[:, 0, :], a["index_b"].partition_broadcast(P)), (at_i[:, 1, :], a["index_t"].partition_broadcast(P)),
            (col_i[:, :, :], a["index_cols"]),
            (place[:, :], a["c_place"].partition_broadcast(P)), (number[:, :], a["c_number"])])
        normalise(nc, "experts_norm_all", T, K, lambda i: T.X[:, i, :], TT, None, 1e-5, True,
                  write=lambda i: T.Y[:, i, :])
        with phase(nc, "experts_gather", "chain hot gathered taken gates scored sig exped onecol") as (block, s):
            @block.vector
            def _(dve):
                t = Tally(dve, s["chain"])
                step = lambda ins: (t.add(ins), t.wait())
                for i, f in ((at_i, at_f), (col_i, col_f)):
                    step(dve.tensor_copy(f[:, :, :], i[:, :, :]))
                    step(dve.scalar_tensor_tensor(f[:, 0, :], f[:, 0, :], float(S), f[:, 1, :], ALU.mult, ALU.add))
                for n in range(TT):
                    if n >= 2:
                        dve.wait_ge(s["gathered"], n - 1)
                    dve.tensor_scalar(one_hot[:, n % 2, 0:M1], at_f[:, 0, :], number[:, n:n + 1], None,
                                      ALU.is_equal).then_inc(s["hot"], 1)
                dve.wait_ge(s["sig"], MT)
                f = lambda n: e[n][:, :, 0:E1]
                across = lambda x: x[:, :].unsqueeze(2).to_broadcast([P, MT, E1])
                order_all = order[:, 0:E1].unsqueeze(1).to_broadcast([P, MT, E1])
                step(dve.tensor_tensor(f("biased"), score[:, :, 0:E1], exp_bias[:, :].unsqueeze(1).to_broadcast([P, MT, E1]), ALU.add))
                step(dve.tensor_reduce(one["top"][:, :], f("biased"), AX.X, ALU.max))
                step(dve.tensor_tensor(f("pick"), f("biased"), across(one["top"]), ALU.is_equal))
                step(dve.tensor_tensor(f("pick"), f("pick"), order_all, ALU.mult))
                step(dve.tensor_reduce(one["top"][:, :], f("pick"), AX.X, ALU.max))
                step(dve.tensor_tensor(f("pick"), order_all, across(one["top"]), ALU.is_equal))
                step(dve.tensor_tensor(f("tmp"), f("pick"), score[:, :, 0:E1], ALU.mult))
                step(dve.tensor_reduce(e["mix"][:, :, 0], f("tmp"), AX.X, ALU.add))
                step(dve.tensor_copy(e["mix"][:, :, 1], score[:, :, E1]))
                dve.wait_ge(s["exped"], 1)
                step(dve.tensor_reduce(one["sum"][:, :], e["expd"][:, :, 0:2], AX.X, ALU.add))
                step(dve.reciprocal(one["sum"][:, :], one["sum"][:, :]))
                step(dve.tensor_tensor(e["mix"][:, :, 0:2], e["expd"][:, :, 0:2],
                                       one["sum"][:, :].unsqueeze(2).to_broadcast([P, MT, 2]), ALU.mult))
                step(dve.tensor_tensor(f("pick"), f("pick"), e["mix"][:, :, 0:1].to_broadcast([P, MT, E1]), ALU.mult))

            @block.tensor
            def _(pe):
                for n in range(TT):
                    pe.wait_ge(s["hot"], n + 1)
                    for c in range(C):
                        m = pe.matmul(T.four[:, c, :], T.Y[:, n, c * P:(c + 1) * P], one_hot[:, n % 2, 0:M1],
                                      start=n == 0, stop=n == TT - 1)
                    m.then_inc(s["gathered"], 1)
                pe.wait_ge(s["taken"], C)
                for n in range(MT):
                    for c in range(C):
                        pe.matmul(T.ring[0][:, n * 16:n * 16 + E1 + 1], picked[:, c, n * P:(n + 1) * P], wg[:, c, :],
                                  start=c == 0, stop=False)
                    pe.matmul(T.ring[0][:, n * 16:n * 16 + E1 + 1], K.ones_row, bg[:, :], start=False,
                              stop=True).then_inc(s["scored"], 1)

            @block.scalar
            def _(act):
                act.wait_ge(s["gathered"], TT)
                for c in range(C):
                    act.activation(picked[:, c, :], T.four[:, c, :], ACT.Copy).then_inc(s["taken"], 1)
                act.wait_ge(s["scored"], MT)
                for n in range(MT):
                    act.activation(score[:, n, :], T.ring[0][:, n * 16:n * 16 + E1 + 1], ACT.Sigmoid).then_inc(s["sig"], 1)
                act.wait_ge(s["chain"], 4 + 9)
                act.activation(e["expd"][:, :, 0:2], e["mix"][:, :, 0:2], ACT.Exp).then_inc(s["exped"], 1)

            @block.gpsimd
            def _(pool):
                pool.memset(values[:, :, D:D + 1], 1.0)

        def unit(k, x, finish):
            n = 0 if k == E1 else 2
            return {"x": x, "w12": w12[:, :, k, :], "b12": b12[:, k, :], "scale": norms[:, n:n + 1],
                    "shift": norms[:, n + 1:n + 2], "w3": w3[:, k, :], "b3": b3[:, k, :], "finish": finish}

        with nc.Fori(0, B) as b:
            def rows(i):
                return T.Y[:, bass.ds(b * TB + i, 1), :].rearrange("p o d -> p (o d)")

            def keep_shared(i):
                return lambda dve, ps: dve.tensor_copy(
                    shared[:, bass.ds(b * TB + i, 1), :].rearrange("p o d -> p (o d)"), ps)

            transposed(nc, "experts_turn", T, K, rows)
            gated_units(nc, "shared_net", T, K, [[unit(E1, T.hT[:, :, i * P:(i + 1) * P], keep_shared(i)) for i in range(TB)]])

        def first(n):
            return lambda dve, ps: dve.tensor_scalar(values[:, n, 0:D], ps, e["mix"][:, n, 1:2], None, ALU.mult)

        def more(n, k):
            return lambda dve, ps: dve.scalar_tensor_tensor(values[:, n, 0:D], ps, e["pick"][:, n, k:k + 1],
                                                            values[:, n, 0:D], ALU.mult, ALU.add)

        x_of = lambda n: picked[:, :, n * P:(n + 1) * P]
        gated_units(nc, "expert_nets", T, K, [[unit(E1, x_of(n), first(n)) for n in range(MT)]] +
                    [[unit(k, x_of(n), more(n, k)) for k in range(E1)] for n in range(MT)])
        with phase(nc, "experts_back", "hot back0 back1 counted kept scaled done") as (block, s):
            back = (s["back0"], s["back1"])

            def finish(dve, n):
                dve.wait_ge(back[n % 2], n // 2 + 1)
                ps = T.ring[n % 2]
                dve.tensor_scalar(count[:, n:n + 1], ps[:, D:D + 1], 1.0, None, ALU.max).then_inc(s["counted"], 1)
                dve.tensor_scalar(keep[:, n:n + 1], ps[:, D:D + 1], 1.0, -1.0, ALU.min, ALU.mult).then_inc(s["counted"], 1)
                dve.wait_ge(s["counted"], 2 * n + 2)
                dve.reciprocal(count[:, n:n + 1], count[:, n:n + 1]).then_inc(s["kept"], 1)
                dve.scalar_tensor_tensor(shared[:, n, :], shared[:, n, :], keep[:, n:n + 1], shared[:, n, :],
                                         ALU.mult, ALU.add).then_inc(s["kept"], 1)
                dve.wait_ge(s["kept"], 2 * n + 2)
                dve.scalar_tensor_tensor(shared[:, n, :], ps[:, 0:D], count[:, n:n + 1], shared[:, n, :], ALU.mult,
                                         ALU.add).then_inc(s["scaled"], 1)
                dve.wait_ge(s["scaled"], n + 1)
                dve.tensor_tensor(T.X[:, n, :], T.X[:, n, :], shared[:, n, :], ALU.add).then_inc(s["done"], 1)

            @block.vector
            def _(dve):
                for n in range(TT):
                    if n >= 2:
                        dve.wait_ge(back[n % 2], n // 2)
                    for m in range(MT):
                        dve.tensor_scalar(one_hot[:, n % 2, m * P:(m + 1) * P], place[:, n * P:(n + 1) * P],
                                          col_f[:, 0, m:m + 1], None, ALU.is_equal).then_inc(s["hot"], 1)
                    if n:
                        finish(dve, n - 1)
                finish(dve, TT - 1)

            @block.tensor
            def _(pe):
                for n in range(TT):
                    pe.wait_ge(s["hot"], MT * (n + 1))
                    if n >= 2:
                        pe.wait_ge(s["scaled"], n - 1)
                    for m in range(MT):
                        t = pe.matmul(T.ring[n % 2][:, 0:D + 1], one_hot[:, n % 2, m * P:(m + 1) * P], values[:, m, :],
                                      start=m == 0, stop=m == MT - 1)
                    t.then_inc(back[n % 2], 1)


def transposed(nc, tag, T, K, rows):
    with phase(nc, tag, "staged turned0 turned1 taken0 taken1") as (block, s):
        turned, taken = (s["turned0"], s["turned1"]), (s["taken0"], s["taken1"])

        @block.vector
        def _(dve):
            for i in range(TB):
                dve.tensor_copy(T.normed[:, i, :], rows(i)).then_inc(s["staged"], 1)

        @block.tensor
        def _(pe):
            for q in range(NH):
                pe.wait_ge(s["staged"], 4 * q + 4)
                for c in range(C):
                    if q:
                        pe.wait_ge(taken[c], q)
                    for i in range(4):
                        m = pe.transpose(T.ring[c][:, i * P:(i + 1) * P], T.normed[:, 4 * q + i, c * P:(c + 1) * P], K.ident)
                    m.then_inc(turned[c], 1)

        @block.scalar
        def _(act):
            for q in range(NH):
                for c in range(C):
                    act.wait_ge(turned[c], q + 1)
                    act.activation(T.hT[:, c, q * HALF:(q + 1) * HALF], T.ring[c][:, :], ACT.Copy).then_inc(taken[c], 1)


def program(nc, a, out, stages):
    with ExitStack() as ctx:
        K = constants(nc, ctx.enter_context, a)
        T = tensors(nc, ctx.enter_context)
        load(nc, "x_in", [(T.X[:, b * TB:(b + 1) * TB, :], a["x"][b].rearrange("(t p) d -> p t d", p=P)) for b in range(B)])
        if "traj" in stages:
            trajectories(nc, a, T, K)
        if "decoder" in stages:
            decoder(nc, a, T, K)
        if "mixture" in stages:
            mixture_attention(nc, a, T, K)
        if "self" in stages:
            self_attention(nc, a, T, K)
        if "cross" in stages:
            cross_attention(nc, a, T, K)
        if "moe" in stages:
            expert_ffn(nc, a, T, K)
        with phase(nc, "x_out", "stored") as (block, s):
            @block.sync
            def _(sync):
                for b in range(B):
                    sync.dma_start(out[b].rearrange("(t p) d -> p t d", p=P),
                                   T.X[:, b * TB:(b + 1) * TB, :]).then_inc(s["stored"], 16)
                sync.wait_ge(s["stored"], 16 * B)


def _chunks(w):
    return np.ascontiguousarray(w.reshape(-1, P, w.shape[1]).transpose(1, 0, 2).reshape(P, -1))


def _slots(w, turned=False):
    o = np.zeros((HEADS, 32) + w.shape[1:], w.dtype)
    r = w.reshape((HEADS, HD) + w.shape[1:])
    o[:, 0:HD] = r
    if turned:
        o[:, HD:HD + 8], o[:, HD + 8:2 * HD] = r[:, 8:16], r[:, 0:8]
    return o.reshape((4 * P,) + w.shape[1:])


def _w_slots(w, turned=False):
    return _chunks(_slots(w, turned).T)


def _out_slots(w, bias=None):
    o = _slots(w)
    if bias is not None:
        o[HD] = bias
    return np.ascontiguousarray(o.reshape(4, P, D).transpose(1, 0, 2).reshape(P, 4 * D))


def _v_row(bias):
    o = _slots(bias).reshape(HEADS, 32)
    o[:, HD] = 1
    return o.reshape(1, -1)


def _columns(bias, turned=False):
    return np.ascontiguousarray(_slots(bias, turned).reshape(4, P).T)


def _by_feature(v):
    return np.ascontiguousarray(v.reshape(C, P).T)


def _tables():
    f = np.float32
    ident = np.eye(P, dtype=f)
    fold, spread, spread_wide = np.zeros((P, P), f), np.zeros((P, P), f), np.zeros((P, P), f)
    trig, cols = np.zeros((P, S), f), np.zeros((P, 16), f)
    inv = (1.0 / f(10000.0) ** (np.arange(0, HD, 2, dtype=f) / f(HD))).astype(f)
    angle = np.arange(S, dtype=f)[:, None] * inv[None, :]
    cos, sin = np.cos(angle), np.sin(angle)
    for j in range(4):
        for d in range(HD):
            fold[32 * j + d, 32 * j + d] = fold[32 * j + HD + d, 32 * j + d] = 1
            trig[32 * j + d] = cos[:, d % 8]
            trig[32 * j + HD + d] = sin[:, d % 8] * (-1 if d < 8 else 1)
        spread[32 * j + HD, 32 * j:32 * j + 32] = 1
        cols[32 * j + HD, 4:8] = 1
    spread_wide[MHD, :] = 1
    cols[MHD, 8:12] = 1
    cols[:, 12], cols[:, 13] = np.arange(P), np.arange(P) + LOOKBACK
    q, k = np.arange(P)[:, None], np.arange(P)[None, :]
    mask = np.stack([np.where(k > q, f(MASKED), f(0)), np.where(q > k, f(MASKED), f(0))], 1).astype(f)
    band = np.zeros((P, 3, P), f)
    for pos in range(2 * P):
        n = min(pos, WINDOW)
        for j in range(n):
            idx = pos - n + j
            v = f(0.1) + f(0.9) * f(j) / f(max(n - 1, 1)) if n > 1 else f(0.1)
            if pos < P:
                band[idx, 0, pos] = v
            elif idx >= P:
                band[idx - P, 1, pos - P] = v
            else:
                band[idx, 2, pos - P] = v
    order = np.tile(np.arange(NEXP, 0, -1, dtype=f), (P, TB))
    place = np.arange(B * S, dtype=f)
    return {"c_place": place, "c_number": np.ascontiguousarray(place.reshape(TT, P).T), "c_band": band, "c_order": order, "c_ident": ident, "c_fold": fold, "c_trig": trig, "c_spread": spread, "c_spread_wide": spread_wide,
            "c_mask": mask, "c_cols": cols}


def layouts(i):
    g = {k: np.asarray(v) for k, v in i.items()}
    a = dict(_tables())
    a["x"] = g["x"]
    a["ctxT"] = np.ascontiguousarray(g["ctx_1024"].reshape(B, CTX, C, P).transpose(3, 0, 2, 1))
    a["seg"] = g["itok_BxS_0_255"].reshape(B * S)
    n = "L0_xattn_"
    qkv, bqkv = g[n + "Wqkv"], g[n + "bqkv"]
    kv = g[n + "Wkv_c"]
    a["nf"] = g[n + "nf"]
    a["w_slots"] = np.stack([np.concatenate([
        _w_slots(qkv[l, 0:D], True), _w_slots(qkv[l, D:2 * D], True), _w_slots(qkv[l, 2 * D:]),
        _w_slots(g[n + "Wq_c"][l]), _w_slots(kv[l, 0:D])], 1) for l in range(LAYERS)])
    a["w_cross_v"] = np.stack([_w_slots(kv[l, D:]) for l in range(LAYERS)])
    a["w_outs"] = np.stack([np.concatenate([_out_slots(g[n + "Wo"][l].T, g[n + "bo"][l]),
                                            _out_slots(g[n + "Wo_c"][l].T)], 1) for l in range(LAYERS)])
    a["v_row"] = np.stack([np.concatenate([_v_row(bqkv[l, 2 * D:]), _v_row(np.zeros(D, np.float32))], 1)
                           for l in range(LAYERS)])
    a["qk_bias"] = np.stack([np.concatenate([_columns(bqkv[l, 0:D], True), _columns(bqkv[l, D:2 * D], True)], 1)
                             for l in range(LAYERS)])
    a["norm_scales"] = np.stack([np.concatenate([_by_feature(g[n + m][l]) for m in ("n1", "n2", "n3")], 1)
                                 for l in range(LAYERS)])
    a["w_gate"] = np.stack([_chunks(g[n + "Wg"][l].T) for l in range(LAYERS)])
    a["w_up"] = np.stack([_chunks(g[n + "Wu"][l].T) for l in range(LAYERS)])
    a["w_down"] = np.stack([_chunks(g[n + "Wd"][l].T) for l in range(LAYERS)])
    a["guide"] = g["L0_attn_guidance_trajectories"]
    n = "L0_ffn_"
    a["sim"], a["gates"] = _chunks(g[n + "sim_matrix"]), g[n + "gates"]
    wide = lambda w: _chunks(w.transpose(1, 0, 2).reshape(D, NEXP * MHD))
    a["mix_qkv"] = np.concatenate([wide(g[n + m]) for m in ("q_proj", "k_proj", "v_proj")], 1)
    a["mix_o"] = _chunks(g[n + "o_proj"].reshape(NEXP * MHD, D))
    n = "L1_attn_"
    wt, bias = g[n + "w_qkv"].T, g[n + "b_qkv"]
    parts = {"s1": (wt[0:D], wt[D:2 * D], wt[2 * D:], g[n + "w_out"], bias[0:D], bias[D:2 * D], bias[2 * D:], g[n + "b_out"])}
    a["s1_affine"] = np.concatenate([_by_feature(g[n + "ln_gamma"]), _by_feature(g[n + "ln_beta"])], 1)
    n = "L1_xattn_"
    parts["x1"] = (g[n + "Wq"].T, g[n + "Wk"].T, g[n + "Wv"].T, g[n + "Wo"], g[n + "b_q"], g[n + "b_k"], g[n + "b_v"],
                   g[n + "b_o"])
    for tag, (q, k, v, o, bq, bk, bv, bo) in parts.items():
        a[tag + "_q"], a[tag + "_k"], a[tag + "_v"] = _w_slots(q), _w_slots(k), _w_slots(v)
        a[tag + "_o"], a[tag + "_v_row"] = _out_slots(o, bo), _v_row(bv)
        k_cols = _columns(bk)
        k_cols[HD::32] = 1
        a[tag + "_bias"] = np.concatenate([_columns(bq), k_cols], 1)
    n = "L1_ffn_"
    both = lambda w1, w2: np.concatenate([w1, w2], -2).transpose(0, 2, 1)
    w12 = np.concatenate([both(g[n + "ew1"], g[n + "ew2"]), both(g[n + "sw1"][None], g[n + "sw2"][None])], 0)
    a["e_w12"] = w12.reshape(E1 + 1, C, P, 2 * H1).transpose(2, 1, 0, 3).reshape(P, -1)
    a["e_b12"] = np.concatenate([np.concatenate([g[n + "eb1"], g[n + "eb2"]], 1).reshape(-1), g[n + "sb1"], g[n + "sb2"]])[None]
    a["e_w3"] = np.concatenate([g[n + "ew3"], g[n + "sw3"][None]], 0).transpose(2, 0, 1).reshape(P, -1)
    a["e_b3"] = np.concatenate([g[n + "eb3"].reshape(-1), g[n + "sb3"]])[None]
    a["e_norms"] = np.stack([g[n + m] for m in ("s_ln_g", "s_ln_b", "sel_ln_g", "sel_ln_b")], 1)
    a["e_gate"] = _chunks(np.concatenate([g[n + "eg_w"], g[n + "sg_w"]], 0).T)
    a["e_gate_bias"] = np.concatenate([g[n + "eg_b"], g[n + "sg_b"]])[None]
    a["e_bias"] = g[n + "exp_bias"]
    a["index_b"], a["index_t"] = g[n + "index_b"], g[n + "index_t"]
    a["index_cols"] = np.stack([g[n + m].reshape(MT, P).T for m in ("index_b", "index_t")], 1)
    return a


STAGES = ("traj", "decoder", "mixture", "self", "cross", "moe")


def declare(nc, arrays, stages=STAGES):
    args = {k: nc.dram_tensor(f"in_{k}", v.shape, mybir.dt.from_np(v.dtype), kind="ExternalInput").ap()
            for k, v in arrays.items()}
    args["parked"] = nc.dram_tensor("parked", (P, TT * D), F32, kind="Internal").ap()
    out = nc.dram_tensor("out", (B, S, D), F32, kind="ExternalOutput").ap()
    program(nc, args, out, stages)


def kernel(**inputs):
    import concourse.bacc as bacc
    from concourse.bass_utils import run_bass_kernel_spmd

    arrays = {k: np.ascontiguousarray(v) for k, v in layouts(inputs).items()}
    nc = bacc.Bacc("TRN2", target_bir_lowering=False, num_devices=1)
    declare(nc, arrays)
    r = run_bass_kernel_spmd(nc, [{f"in_{k}": v for k, v in arrays.items()}], core_ids=[0])
    return r.results[0]["out"]
```

```python
from contextlib import ExitStack, contextmanager

import numpy as np

import concourse.bass as bass
from concourse import mybir

ALU = mybir.AluOpType
ACT = mybir.ActivationFunctionType
F32 = mybir.dt.float32
BF16 = mybir.dt.bfloat16
I32 = mybir.dt.int32
AX = mybir.AxisListType

P = 128
B, S, D = 2, 1024, 256
C = D // P
TB = S // P
TT = B * TB
HALF = 512
NH = S // HALF
LAYERS, HEADS, HD = 4, 16, 16
CTX = 64
LOOKBACK = 128
FF = 1024
FT = FF // P
NEXP, MHD = 16, 64
E1, H1, M1 = 8, 128, 512
MT = M1 // P
MASKED = -4e30
WINDOW = 8
RING = 3
LAG = 1
ROOM = 0.85
TERMS = ((0, 0), (0, 1), (0, 2), (1, 0), (1, 1), (2, 0))
TERM_DMAS = 2 * len(TERMS) * 4
ROWS = len(TERMS) * HD + 3
FIRST_SEM = 160


class Names:
    pass


class Tally:

    def __init__(self, engine, sem):
        self.engine, self.sem, self.n = engine, sem, 0

    def add(self, ins):
        ins.then_inc(self.sem, 1)
        self.n += 1

    def wait(self):
        self.engine.wait_ge(self.sem, self.n)


@contextmanager
def phase(nc, tag, names):
    with ExitStack() as ctx:
        nums = range(FIRST_SEM, FIRST_SEM + len(names.split()))
        sems = {n: ctx.enter_context(nc.semaphore(f"{tag}_{n}", num=k)) for n, k in zip(names.split(), nums)}
        nc.gpsimd.sem_clear(nums)
        nc.all_engine_barrier()
        block = ctx.enter_context(nc.Block())
        yield block, sems


class Ring:

    def __init__(self, jobs):
        self.at = {job: (n % RING, n // RING) for n, job in enumerate(jobs)}
        assert len(self.at) == len(jobs)


def attention_plan(G, GB, steps, units, prep, maxima, shifts, out_jobs):
    n = len(steps)
    plan = prep(0) + maxima(0) + shifts(0)
    late = []
    after = []
    parts = 1 if n > 2 else 3
    for g in range(G):
        side = prep(g + 1) + maxima(g + 1) + shifts(g + 1) if g + 1 < G else []
        fills = n * (units + 1) * parts
        room = max(1, int(ROOM * fills))
        spread = [[] for _ in range(fills)]
        for k, job in enumerate(side):
            spread[k * room // len(side)].append(job)
        out = out_jobs(g // GB - 1) if g and g % GB == 0 else []
        old = ("z", g - 1, 1)
        k = 0
        for s in range(n):
            for a in range(units + 1):
                if a < units:
                    plan.append(("S", g, s, a))
                if a == units - (n <= 2):
                    plan += late
                    after += finish_heads(late)
                    late = []
                for _ in range(parts):
                    plan += spread[k]
                    if out and old in plan:
                        plan.append(out.pop(0))
                    if after:
                        assert not (after[0][0:2] == ("z", g) and out and out[0][2] < 4 * (after[0][2] + 1))
                        plan.append(after.pop(0))
                    k += 1
            late = [("PV", g, s)]
            if s == n - 1 or steps[s][0] != steps[s + 1][0]:
                late.append(("o", g, steps[s][0]))
    plan += late + after + finish_heads(late) + out_jobs((G - 1) // GB)
    return [job for job in plan if job]


def finish_heads(late):
    return [x for what, g, h in late if what == "o" for x in (("d", g, h), ()) + ((),) * LAG + (("z", g, h),)]


def attention(nc, tag, T, K, kind, q_in, k_in, w, H, hd, causal, lk, scale, out_rows, NB, loads=()):
    GB = HEADS // H if kind != "given" else 1
    G = NB * GB
    short = lk < P
    slot = P // H
    KT = max(1, lk // P)
    KP = min(P, lk)
    masked = "mask" in w
    stacked = kind in ("rope", "plain") and lk == S
    pair = 4 if short else min(2, H)
    steps = [(h, i, max(0, i * P - h * HALF) if causal else 0) for h in range(NH) for i in range(KT)
             if not causal or i * P < (h + 1) * HALF]
    last_of = {h: max(s for s, x in enumerate(steps) if x[0] == h) for h in range(NH)}

    def prep(g):
        jobs = []
        for h in range(max(1, lk // HALF)):
            jobs.append(("k", g, h))
        for h in range(NH):
            jobs.append(("q", g, h))
        if kind == "rope":
            folded = []
            for n, job in enumerate(jobs):
                folded.append(job)
                if n:
                    folded.append((jobs[n - 1][0] + "f",) + jobs[n - 1][1:])
            folded.append((jobs[-1][0] + "f",) + jobs[-1][1:])
            jobs = folded
        if kind != "given" and g % GB == 0:
            jobs += [("v", g, n) for n in range(max(1, KT // 2))]
        return jobs

    pieces = []
    for i in range(TB):
        keys = (i + 1) * P if causal else lk
        for p in range((keys + HALF - 1) // HALF):
            pieces.append((i, p, min(HALF, keys - p * HALF), causal and p == (keys - 1) // HALF))

    def maxima(g):
        return [("m", g, j, n) for n in range(len(pieces)) for j in ((0,) if short else range(H))]

    def shifts(g):
        return [("t", g, h) for h in range(NH)]

    def out_jobs(b):
        return [("y", b, i) for i in range(TB)] if out_rows else []

    plan = attention_plan(G, GB, steps, H // pair, prep, maxima, shifts, out_jobs)
    ringed = [x for x in plan if x[0] not in ("S", "PV", "o")]
    ring = Ring(ringed)

    names = ("ring_full0 ring_full1 ring_full2 ring_free0 ring_free1 ring_free2 narrow_made shift_made scores_full exp_done pv_done heads_raw inverses_spread cleared heads_cleared "
             "high_made rest_made low_made loaded terms_stacked shifts_stacked maxima_split blocks blocks_v")
    with phase(nc, tag, names) as (block, s):
        full = (s["ring_full0"], s["ring_full1"], s["ring_full2"])
        free = (s["ring_free0"], s["ring_free1"], s["ring_free2"])

        def bank(job):
            return T.ring[ring.at[job][0]]

        def take(pe, job):
            par, use = ring.at[job]
            if use:
                pe.wait_ge(free[par], use)

        def give(ins, job):
            ins.then_inc(full[ring.at[job][0]], 1)

        def arrived(eng, job):
            par, use = ring.at[job]
            eng.wait_ge(full[par], use + 1)

        def release(ins, job):
            ins.then_inc(free[ring.at[job][0]], 1)

        def consumed(eng, job):
            par, use = ring.at[job]
            eng.wait_ge(free[par], use + 1)

        to_slots = ("qf", "kf") if kind == "rope" else ("q", "k")
        slot_jobs = [x for x in ringed if x[0] in to_slots]
        per_group = len(slot_jobs) // G
        turns = {x: n for n, x in enumerate(x for x in ringed if x[0] in ("q", "k"))}
        turn_jobs = list(turns)
        v_jobs = [x for x in ringed if x[0] == "v"]
        zs = [x for x in ringed if x[0] == "z"]

        shift = T.shift_bf if stacked else T.shift
        cleared = 5 if stacked else 7 if short else 3 if kind != "given" else 2

        def qk(g, which):
            return (T.q_slots if which == "q" else T.k_slots)[:, g % 2, :]

        def narrow(g, which):
            if stacked:
                return T.parts[:, 0 if which == "q" else 1, 0, :]
            return (T.q_narrow if which == "q" else T.k_narrow)[:, g % 2, :]

        def width(which):
            return HALF if which == "q" or lk >= HALF else lk

        @block.tensor
        def _(pe):
            for job in plan:
                what, g = job[0], job[1]
                if what in ("q", "k"):
                    h, n = job[2], width(what)
                    take(pe, job)
                    if kind == "given":
                        src = T.q_tok if what == "q" else T.k_tok
                        for i in range(4):
                            m = pe.matmul(bank(job)[:, i * P:(i + 1) * P], src[:, 4 * h + i, :], K.ident,
                                          start=True, stop=True)
                    else:
                        src = (q_in if what == "q" else k_in)(g // GB)
                        for c in range(C):
                            m = pe.matmul(bank(job)[:, 0:n], w[what][:, c, g % GB, :], src[:, c, h * n:(h + 1) * n],
                                          start=c == 0, stop=c == C - 1)
                    give(m, job)
                elif what in ("qf", "kf"):
                    base = (what[0],) + job[1:]
                    take(pe, job)
                    consumed(pe, base)
                    m = pe.matmul(bank(job)[:, :], K.fold, T.turned[:, turns[base] % 2, :], start=True, stop=True)
                    give(m, job)
                elif what == "v":
                    take(pe, job)
                    for n in range(min(2, KT)):
                        i = 2 * job[2] + n
                        for c in range(C):
                            m = pe.matmul(bank(job)[:, n * D:(n + 1) * D], k_in(g // GB)[:, c, i * P:(i + 1) * P],
                                          w["v"][:, c, :], start=c == 0, stop=c == C - 1)
                    give(m, job)
                elif what == "m":
                    j, n = job[2], job[3]
                    i, p, cols, diag = pieces[n]
                    take(pe, job)
                    if j == 0 and n == 0:
                        if stacked:
                            pe.wait_ge(s["high_made"], (g + 1) * per_group)
                        else:
                            pe.wait_ge(s["narrow_made"], (g + 1) * (per_group + (H - 1 if short else 0)))
                    rows = slice(j * slot, (j + 1) * slot)
                    if short:
                        if masked:
                            m = pe.matmul(bank(job)[:, 0:H * lk], w["mask"][:, g // GB, i * P:(i + 1) * P],
                                          K.ident_rows, start=True, stop=False)
                        m = pe.matmul(bank(job)[:, 0:H * lk], narrow(g, "q")[:, i * P:(i + 1) * P],
                                      narrow(g, "k")[:, 0:H * lk], start=not masked, stop=True)
                        give(m, job)
                        continue
                    m = pe.matmul(bank(job)[:, 0:cols], narrow(g, "q")[rows, i * P:(i + 1) * P],
                                  narrow(g, "k")[rows, p * HALF:p * HALF + cols], start=True, stop=not diag)
                    if diag:
                        m = pe.matmul(bank(job)[:, cols - P:cols], K.ident_bf, K.mask_q, start=False, stop=True)
                    give(m, job)
                elif what == "t":
                    take(pe, job)
                    if job[2] == 0:
                        pe.wait_ge(s["shift_made"], g + 1)
                    for i in range(4):
                        m = pe.matmul(bank(job)[:, i * P:(i + 1) * P], shift[:, 4 * job[2] + i, :],
                                      K.ident_bf if stacked else K.ident, start=True, stop=True)
                    give(m, job)
                elif what == "S":
                    h, i, c0 = steps[job[2]]
                    a = job[3]
                    if stacked and job[2] == 0 and a == 0:
                        pe.wait_ge(s["terms_stacked"], 16 * TERM_DMAS * (g + 1))
                        pe.wait_ge(s["shifts_stacked"], 16 * H * (g + 1))
                        pe.wait_ge(s["cleared"], cleared)
                    elif i == 0 and a == 0 and not stacked:
                        consumed(pe, ("t", g, h))
                    unit = (g * len(steps) + job[2]) * (H // pair) + a
                    if unit >= 2:
                        pe.wait_ge(s["exp_done"], unit - 1)
                    if short:
                        at = slice(h * HALF, (h + 1) * HALF)
                        for two in range(H // 2):
                            if masked:
                                pe.matmul(T.scores[:, unit % 2, two, :], K.ident_two, w["mask"][:, g // GB, at],
                                          start=True, stop=False)
                            m = pe.matmul(T.scores[:, unit % 2, two, :], qk(g, "k")[:, 2 * two * lk:2 * (two + 1) * lk],
                                          qk(g, "q")[:, at], start=not masked, stop=True)
                        m.then_inc(s["scores_full"], 1)
                        continue
                    diag = causal and i * P >= h * HALF
                    for b in range(pair):
                        rows = slice((a * pair + b) * slot, (a * pair + b + 1) * slot)
                        keys, queries = qk(g, "k")[rows, :] if not stacked else T.stack_k[0:ROWS, g % 2, a * pair + b, :], \
                            qk(g, "q")[rows, :] if not stacked else T.stack_q[0:ROWS, g % 2, a * pair + b, :]
                        m = pe.matmul(T.scores[:, unit % 2, b, c0:HALF], keys[:, i * P:(i + 1) * P],
                                      queries[:, h * HALF + c0:(h + 1) * HALF], start=True, stop=not diag)
                        if diag:
                            m = pe.matmul(T.scores[:, unit % 2, b, c0:c0 + P], K.ident_bf, K.mask_k,
                                          start=False, stop=True)
                    m.then_inc(s["scores_full"], 1)
                elif what == "PV":
                    h, i, c0 = steps[job[2]]
                    n = g * len(steps) + job[2]
                    pe.wait_ge(s["exp_done"], (n + 1) * (H // pair))
                    if i == 0:
                        if kind != "given" and h == 0 and g % GB == 0:
                            for x in [x for x in v_jobs if x[1] == g][-RING:]:
                                consumed(pe, x)
                        if n == 0:
                            pe.wait_ge(s["cleared"], cleared)
                            pe.wait_ge(s["heads_cleared"], 1)
                        if NH * g + h:
                            pe.wait_ge(s["heads_raw"], NH * g + h)
                    first = dict(start=i == 0, stop=job[2] == last_of[h], skip_group_check=True)
                    for two in range(H // 2 if short else 0):
                        e = H * (g % GB) + 2 * two
                        m = pe.matmul(T.heads_ps[2 * two * slot:2 * (two + 1) * slot, :],
                                      T.values_short[:, g // GB, e:e + 2, :].rearrange("p e d -> p (e d)"),
                                      T.probs[:, n % 2, two, :], **first)
                    for j in range(0 if short else H):
                        if kind == "given":
                            m = pe.matmul(T.heads_ps[:, c0:HALF], T.values_wide[:, 0, i, :],
                                          T.probs[:, n % 2, j, c0:HALF], **first)
                            continue
                        m = pe.matmul(T.heads_ps[j * slot:j * slot + HD + 1, c0:HALF],
                                      T.values[:, g // GB, i, H * (g % GB) + j, :],
                                      T.probs[:, n % 2, j, c0:HALF], **first)
                    m.then_inc(s["pv_done"], 1)
                elif what == "d":
                    take(pe, job)
                    pe.wait_ge(s["heads_raw"], NH * g + job[2] + 1)
                    for i in range(4):
                        m = pe.matmul(bank(job)[:, i * H:(i + 1) * H], T.heads_sb[:, job[2], i * P:(i + 1) * P],
                                      w["pick"], start=True, stop=True)
                    give(m, job)
                elif what == "z":
                    take(pe, job)
                    pe.wait_ge(s["inverses_spread"], NH * g + job[2] + 1)
                    for i in range(4):
                        m = pe.matmul(bank(job)[:, i * P:(i + 1) * P], T.denominators[:, i * P:(i + 1) * P], K.ident,
                                      start=True, stop=True)
                    give(m, job)
                elif what == "y":
                    b, i = job[1:]
                    take(pe, job)
                    if i == 0:
                        for x in {ring.at[z][0]: z for z in ringed if z[0] == "z" and z[1] // GB == b}.values():
                            consumed(pe, x)
                    for gg in range(GB):
                        m = pe.matmul(bank(job)[:, 0:D], T.heads_out[:, gg, i * P:(i + 1) * P], w["o"][:, gg, :],
                                      start=gg == 0, stop=gg == GB - 1)
                    give(m, job)

        @block.scalar
        def _(act):
            for job in plan:
                what, g = job[0], job[1]
                if what in to_slots:
                    n = width(what[0])
                    arrived(act, job)
                    bias = w[what[0] + "_slot_bias"][:, g % GB:g % GB + 1]
                    if stacked:
                        if g:
                            act.wait_ge(s["terms_stacked"], 16 * TERM_DMAS * g)
                        act.activation(narrow(g, what[0])[:, job[2] * n:(job[2] + 1) * n], bank(job)[:, 0:n],
                                       ACT.Identity, bias=bias).then_inc(s["high_made"], 1)
                        continue
                    if short and what == "k":
                        act.wait_ge(s["cleared"], cleared)
                        for j in range(H):
                            rows = slice(j * slot, (j + 1) * slot)
                            act.activation(narrow(g, "k")[rows, j * n:(j + 1) * n], bank(job)[rows, 0:n],
                                           ACT.Identity, bias=bias[rows, :]).then_inc(s["narrow_made"], 1)
                        for j in range(H):
                            rows = slice(j * slot, (j + 1) * slot)
                            ins = act.activation(qk(g, "k")[rows, j * n:(j + 1) * n], bank(job)[rows, 0:n],
                                                 ACT.Identity, bias=bias[rows, :])
                            if j + 1 < H:
                                ins.then_inc(s["blocks"], 1)
                        act.wait_ge(s["blocks"], (H - 1) * (g + 1))
                        release(ins, job)
                        continue
                    at = slice(job[2] * n, (job[2] + 1) * n)
                    act.activation(narrow(g, what[0])[:, at], bank(job)[:, 0:n], ACT.Identity,
                                   bias=bias).then_inc(s["narrow_made"], 1)
                    release(act.activation(qk(g, what[0])[:, at], bank(job)[:, 0:n], ACT.Identity, bias=bias), job)
                elif what == "t" and stacked:
                    arrived(act, job)
                    if g and job[2] == 0:
                        act.wait_ge(s["shifts_stacked"], 16 * H * g)
                    release(act.activation(T.shift_rows[:, job[2] * HALF:(job[2] + 1) * HALF], bank(job)[:, :],
                                           ACT.Copy), job)
                elif what == "S":
                    h, i, c0 = steps[job[2]]
                    n = g * len(steps) + job[2]
                    a = job[3]
                    if n >= 2 and a == 0:
                        act.wait_ge(s["pv_done"], n - 1)
                    unit = n * (H // pair) + a
                    act.wait_ge(s["scores_full"], unit + 1)
                    banks = min(2, pair)
                    act.activation(T.probs[:, n % 2, a * banks:(a + 1) * banks, c0:HALF],
                                   T.scores[:, unit % 2, 0:banks, c0:HALF], ACT.Exp,
                                   scale=scale).then_inc(s["exp_done"], 1)
                elif what == "z":
                    n = NH * g + job[2]
                    consumed(act, ("d", g, job[2]))
                    if n:
                        arrived(act, zs[n - 1])
                    act.activation(T.denominators[:, :].rearrange("p (i j r) -> p i j r", i=4, j=H),
                                   T.inverses[:, n % 2, 0:4 * H].rearrange("p (i j) -> p i j", j=H).unsqueeze(3)
                                   .to_broadcast([P, 4, H, slot]), ACT.Copy).then_inc(s["inverses_spread"], 1)
                elif what == "o":
                    h = job[2]
                    act.wait_ge(s["pv_done"], g * len(steps) + last_of[h] + 1)
                    if g:
                        consumed(act, ("z", g - 1, h))
                    act.activation(T.heads_sb[:, h, :], T.heads_ps[:, :], ACT.Copy).then_inc(s["heads_raw"], 1)

        @block.vector
        def _(dve):
            dve.memset(T.heads_ps[:, :], 0.0).then_inc(s["heads_cleared"], 1)
            for job in plan:
                what, g = job[0], job[1]
                if what == "v":
                    arrived(dve, job)
                    n = min(2, KT)
                    b = g // GB
                    if short:
                        dve.wait_ge(s["cleared"], cleared)
                        for half in range(2):
                            keys = slice(half * lk, (half + 1) * lk)
                            pairs = lambda x: x.rearrange("p (e u) d -> p e u d", u=2)[:, :, half, :]
                            ins = dve.tensor_tensor(
                                pairs(T.values_short[keys, b, :, 0:HD]),
                                pairs(bank(job)[keys, 0:D].rearrange("p (e d) -> p e d", d=HD)),
                                pairs(w["v_bias"][keys, :].rearrange("p (e d) -> p e d", d=HD)), ALU.add)
                            if not half:
                                ins.then_inc(s["blocks_v"], 1)
                        dve.wait_ge(s["blocks_v"], b + 1)
                        release(ins, job)
                        continue
                    release(dve.tensor_tensor(
                        T.values[:, b, 2 * job[2]:2 * job[2] + n, :, 0:HD],
                        bank(job)[:, 0:n * D].rearrange("p (n e d) -> p n e d", n=n, d=HD),
                        w["v_bias"].rearrange("p (e d) -> p e d", d=HD).unsqueeze(1).to_broadcast([P, n, HEADS, HD]),
                        ALU.add), job)
                elif what in ("q", "k") and kind == "rope":
                    arrived(dve, job)
                    u = turns[job]
                    if u >= 2:
                        old = turn_jobs[u - 2]
                        arrived(dve, (old[0] + "f",) + old[1:])
                    at = slice(job[2] * HALF, (job[2] + 1) * HALF)
                    release(dve.scalar_tensor_tensor(T.turned[:, u % 2, :], bank(job)[:, :],
                                                     w[what + "_bias"][:, g % GB:g % GB + 1], K.trig[:, at],
                                                     ALU.add, ALU.mult), job)
                elif what in to_slots and stacked:
                    u = slot_jobs.index(job)
                    x = 0 if what[0] == "q" else 1
                    at = slice(job[2] * HALF, (job[2] + 1) * HALF)
                    arrived(dve, job)
                    dve.wait_ge(s["high_made"], u + 1)
                    if u >= 2:
                        dve.wait_ge(s["low_made"], 2 * (u - 1))
                    ins = dve.scalar_tensor_tensor(T.rest[:, u % 2, :], bank(job)[:, :],
                                                   w[what[0] + "_slot_bias"][:, g % GB:g % GB + 1], T.parts[:, x, 0, at],
                                                   ALU.add, ALU.subtract)
                    release(ins, job)
                elif what == "m":
                    i, p, cols, _ = pieces[job[3]]
                    arrived(dve, job)
                    if job == maxima(0)[0]:
                        dve.wait_ge(s["cleared"], 2)
                    if g and job == maxima(g)[0]:
                        dve.wait_ge(s["shift_made"], g)
                    if short:
                        release(dve.tensor_reduce(T.maxima[:, 0, i, 0:H], bank(job)[:, 0:H * lk].rearrange(
                            "p (j k) -> p j k", k=lk), AX.X, ALU.max, negate=True), job)
                        continue
                    release(dve.tensor_reduce(T.maxima[:, p, i, job[2]:job[2] + 1], bank(job)[:, 0:cols], AX.X,
                                              ALU.max, negate=True), job)
                elif what == "t":
                    if job[2] == 0:
                        for x in maxima(g)[-RING:]:
                            consumed(dve, x)
                        by_head = shift[:, :, :].rearrange("p i (j r) -> p i j r", r=slot)
                        if stacked:
                            t = Tally(dve, s["maxima_split"])
                            t.n = 5 * g
                            rest, at = T.maxima[:, 0, :, 0:H], lambda k: by_head[:, :, :, hd + k]
                            t.add(dve.tensor_tensor(rest, rest, T.maxima[:, 1, :, 0:H], ALU.min)); t.wait()
                            t.add(dve.tensor_copy(at(0), rest)); t.wait()
                            t.add(dve.tensor_tensor(rest, rest, at(0), ALU.subtract)); t.wait()
                            t.add(dve.tensor_copy(at(1), rest)); t.wait()
                            t.add(dve.tensor_tensor(rest, rest, at(1), ALU.subtract)); t.wait()
                            dve.tensor_copy(at(2), rest).then_inc(s["shift_made"], 1)
                        else:
                            dve.tensor_tensor(by_head[:, :, :, hd], T.maxima[:, 0, :, 0:H], T.maxima[:, 1, :, 0:H],
                                              ALU.min).then_inc(s["shift_made"], 1)
                    if stacked:
                        continue
                    arrived(dve, job)
                    at = qk(g, "q")[:, job[2] * HALF:(job[2] + 1) * HALF]
                    release(dve.tensor_tensor(at, bank(job)[:, :], at, ALU.add), job)
                elif what == "d":
                    n = NH * g + job[2]
                    arrived(dve, job)
                    if n >= 2:
                        dve.wait_ge(s["inverses_spread"], n - 1)
                    release(dve.reciprocal(T.inverses[:, n % 2, 0:4 * H], bank(job)[:, 0:4 * H]), job)
                elif what == "z":
                    h = job[2]
                    arrived(dve, job)
                    dve.wait_ge(s["heads_raw"], NH * g + h + 1)
                    release(dve.tensor_tensor(T.heads_out[:, g % GB, h * HALF:(h + 1) * HALF], T.heads_sb[:, h, :],
                                              bank(job)[:, :], ALU.mult), job)
                elif what == "y":
                    arrived(dve, job)
                    rows = out_rows(job[1], job[2])
                    release(dve.tensor_tensor(rows, bank(job)[:, 0:D], rows, ALU.add), job)

        @block.gpsimd
        def _(pool):
            pool.memset(T.shift[:, :, :], 0.0).then_inc(s["cleared"], 1)
            pool.memset(T.maxima[:, :, :, :], 3e38).then_inc(s["cleared"], 1)
            if short:
                pool.memset(T.values_short[:, :, :, :], 0.0).then_inc(s["cleared"], 1)
                pool.memset(T.k_slots[:, :, 0:H * lk], 0.0).then_inc(s["cleared"], 1)
                pool.memset(T.k_narrow[:, :, 0:H * lk], 0.0).then_inc(s["cleared"], 1)
                for half in range(2):
                    pool.wait_ge(s["cleared"], 5 + half)
                    keys = slice(half * lk, (half + 1) * lk)
                    pool.memset(T.values_short[keys, :, :, HD].rearrange("p b (e u) -> p b e u", u=2)[:, :, :, half],
                                1.0).then_inc(s["cleared"], 1)
            elif kind != "given":
                pool.memset(T.values[:, :, :, :, HD], 1.0).then_inc(s["cleared"], 1)
            if stacked:
                for par in range(2):
                    pool.wait_ge(s["cleared"], 3 + par)
                    pool.memset(T.stack_k[ROWS - 3:ROWS, par, :, :], 1.0).then_inc(s["cleared"], 1)
            pool.wait_ge(s["cleared"], cleared)
            for u, job in enumerate(slot_jobs if stacked else []):
                what, g = job[0][0], job[1]
                n = width(what)
                consumed(pool, job)
                at = slice(job[2] * n, (job[2] + 1) * n)
                x = 0 if what == "q" else 1
                pool.tensor_copy(T.parts[:, x, 1, at], T.rest[:, u % 2, :]).then_inc(s["low_made"], 1)
                pool.wait_ge(s["low_made"], 2 * u + 1)
                pool.tensor_tensor(T.parts[:, x, 2, at], T.rest[:, u % 2, :], T.parts[:, x, 1, at],
                                   ALU.subtract).then_inc(s["low_made"], 1)

        @block.sync
        def _(sync):
            for to, src in loads:
                sync.dma_start(to, src).then_inc(s["loaded"], 16)
            for g in range(G if stacked else 0):
                sync.wait_ge(s["low_made"], 2 * per_group * (g + 1))
                sync.wait_ge(s["high_made"], per_group * (g + 1))
                if g >= 2:
                    sync.wait_ge(s["scores_full"], (g - 1) * len(steps) * (H // pair))
                for j in range(H):
                    for term, parts in enumerate(TERMS):
                        for x, stack in enumerate((T.stack_q, T.stack_k)):
                            sync.dma_start(stack[term * HD:(term + 1) * HD, g % 2, j, :],
                                           T.parts[j * slot:j * slot + HD, x, parts[x], :]).then_inc(s["terms_stacked"], 16)
                for h in range(NH):
                    consumed(sync, ("t", g, h))
                for j in range(H):
                    sync.dma_start(T.stack_q[ROWS - 3:ROWS, g % 2, j, :],
                                   T.shift_rows[j * slot + HD:j * slot + HD + 3, :]).then_inc(s["shifts_stacked"], 16)
            if loads:
                sync.wait_ge(s["loaded"], 16 * len(loads))


def normalise(nc, tag, T, K, rows, count, out, eps, centred, feature_scale=None, write=None, extra=None):
    with phase(nc, tag, "stats stats_all power rstd_made normed normed_act turned0 turned1 taken0 taken1 extra") as (block, s):
        quads = count // 4
        half = count // 2
        shared = not centred and out is not None
        to = lambda i: write(i) if write else T.normed[:, i, :]

        @block.vector
        def _(dve):
            for part in range(2):
                tiles, at = range(part * half, (part + 1) * half), slice(part * half, (part + 1) * half)
                for i in tiles:
                    dve.bn_stats(T.bn[:, i, :], rows(i)).then_inc(s["stats"], 1)
                for i in tiles:
                    dve.wait_ge(s["stats"], i + 1)
                    dve.bn_aggr(T.mv[:, i, :], T.bn[:, i, :]).then_inc(s["stats_all"], 1)
                dve.wait_ge(s["stats_all"], (part + 1) * half)
                if centred:
                    dve.tensor_scalar(T.msq[:, at], T.mv[:, at, 1], eps, None, ALU.add).then_inc(s["power"], 1)
                else:
                    dve.tensor_tensor(T.msq[:, at], T.mv[:, at, 0], T.mv[:, at, 0], ALU.mult).then_inc(s["power"], 1)
                    dve.wait_ge(s["power"], 2 * part + 1)
                    dve.scalar_tensor_tensor(T.msq[:, at], T.mv[:, at, 1], eps, T.msq[:, at],
                                             ALU.add, ALU.add).then_inc(s["power"], 1)
            for i in range(count):
                if i % half == 0:
                    dve.wait_ge(s["rstd_made"], i // half + 1)
                if centred:
                    dve.tensor_scalar(to(i), rows(i), T.mv[:, i, 0:1], T.rstd[:, i:i + 1], ALU.subtract,
                                      ALU.mult).then_inc(s["normed"], 1)
                elif not shared or i % 2 == 0:
                    dve.tensor_scalar(to(i), rows(i), T.rstd[:, i:i + 1], None, ALU.mult).then_inc(s["normed"], 1)
            if extra:
                extra(dve, s["extra"])

        @block.gpsimd
        def _(pool):
            for part in range(2):
                at = slice(part * half, (part + 1) * half)
                pool.wait_ge(s["power"], (part + 1) * (1 if centred else 2))
                pool.tensor_tensor(T.rstd[:, at], T.msq[:, at], K.minus_half[:, at], ALU.pow).then_inc(s["rstd_made"], 1)

        if out is None:
            return
        take = [s["taken0"], s["taken1"]]
        turned = [s["turned0"], s["turned1"]]

        @block.tensor
        def _(pe):
            for q in range(quads):
                pe.wait_ge(s["normed"], 2 * q + 2 if shared else 4 * q + 4)
                if shared:
                    pe.wait_ge(s["normed_act"], 2 * q + 2)
                for c in range(C):
                    if q:
                        pe.wait_ge(take[c], q)
                    for i in range(4):
                        src = (write(4 * q + i) if write else T.normed[:, 4 * q + i, :])[:, c * P:(c + 1) * P]
                        m = pe.transpose(T.ring[c][:, i * P:(i + 1) * P], src, K.ident)
                    m.then_inc(turned[c], 1)

        @block.scalar
        def _(act):
            def scale_tiles(q):
                for i in (4 * q + 1, 4 * q + 3):
                    if i % half == 1:
                        act.wait_ge(s["rstd_made"], i // half + 1)
                    act.activation(to(i), rows(i), ACT.Copy, scale=T.rstd[:, i:i + 1]).then_inc(s["normed_act"], 1)

            if shared:
                scale_tiles(0)
            for q in range(quads):
                if shared and q + 1 < quads:
                    scale_tiles(q + 1)
                for c in range(C):
                    act.wait_ge(turned[c], q + 1)
                    at = out[:, c, q * HALF:(q + 1) * HALF]
                    if feature_scale is None:
                        ins = act.activation(at, T.ring[c][:, :], ACT.Copy)
                    else:
                        scale, bias = feature_scale
                        ins = act.activation(at, T.ring[c][:, :], ACT.Identity, scale=scale[:, c:c + 1],
                                             bias=bias[:, c:c + 1] if bias is not None else 0.0)
                    ins.then_inc(take[c], 1)


def load(nc, tag, pairs):
    with phase(nc, tag, "sync_loaded act_loaded") as (block, s):
        @block.sync
        def _(sync):
            for to, src in pairs[0::2]:
                sync.dma_start(to, src).then_inc(s["sync_loaded"], 16)
            sync.wait_ge(s["sync_loaded"], 16 * len(pairs[0::2]))

        @block.scalar
        def _(act):
            for to, src in pairs[1::2]:
                act.dma_start(to, src).then_inc(s["act_loaded"], 16)
            if pairs[1::2]:
                act.wait_ge(s["act_loaded"], 16 * len(pairs[1::2]))


def decoder_ffn(nc, tag, T, w, rows, loads):
    with phase(nc, tag, "loaded gate_full0 gate_full1 up_full0 up_full1 silu_done act_done down_full down_done") as (block, s):
        gate_full, up_full = (s["gate_full0"], s["gate_full1"]), (s["up_full0"], s["up_full1"])
        n_of = lambda h, f: h * FT + f

        @block.sync
        def _(sync):
            for to, src in loads:
                sync.dma_start(to, src).then_inc(s["loaded"], 16)
            sync.wait_ge(s["loaded"], 16 * len(loads))

        @block.tensor
        def _(pe):
            for h in range(B * NH):
                for f in range(FT):
                    n = n_of(h, f)
                    for which, fullsem, bank in (("gate", gate_full, 0), ("up", up_full, 2)):
                        if n >= 2:
                            pe.wait_ge(s["silu_done"] if which == "gate" else s["act_done"], n - 1)
                        for c in range(C):
                            m = pe.matmul(T.four[:, bank + n % 2, :], w[which][:, c, f * P:(f + 1) * P],
                                          T.hT[:, c, h * HALF:(h + 1) * HALF], start=c == 0, stop=c == C - 1)
                        m.then_inc(fullsem[n % 2], 1)
                for i in range(4):
                    k = 4 * h + i
                    if i == 0:
                        pe.wait_ge(s["act_done"], n_of(h, FT - 1) + 1)
                    if k >= 2:
                        pe.wait_ge(s["down_done"], k - 1)
                    for f in range(FT):
                        m = pe.matmul(T.ring[k % 2][:, 0:D], T.ffn[:, f, i * P:(i + 1) * P], w["down"][:, f, :],
                                      start=f == 0, stop=f == FT - 1)
                    m.then_inc(s["down_full"], 1)

        @block.scalar
        def _(act):
            for n in range(B * NH * FT):
                act.wait_ge(gate_full[n % 2], n // 2 + 1)
                if n >= 2:
                    act.wait_ge(s["act_done"], n - 1)
                act.activation(T.silu[:, n % 2, :], T.four[:, n % 2, :], ACT.Silu).then_inc(s["silu_done"], 1)

        @block.vector
        def _(dve):
            for h in range(B * NH):
                for f in range(FT):
                    n = n_of(h, f)
                    dve.wait_ge(up_full[n % 2], n // 2 + 1)
                    dve.wait_ge(s["silu_done"], n + 1)
                    if f == 0 and h:
                        dve.wait_ge(s["down_full"], 4 * h)
                    dve.tensor_tensor(T.ffn[:, f, :], T.four[:, 2 + n % 2, :], T.silu[:, n % 2, :],
                                      ALU.mult).then_inc(s["act_done"], 1)
                for i in range(4):
                    k = 4 * h + i
                    dve.wait_ge(s["down_full"], k + 1)
                    dve.tensor_tensor(rows(k), T.ring[k % 2][:, 0:D], rows(k), ALU.add).then_inc(s["down_done"], 1)


def constants(nc, enter, a):
    K = Names()

    def sb(name, shape, dt=F32):
        return enter(nc.sbuf_tensor(name, shape, dt))

    ident, fold, trig = sb("ident", [P, P]), sb("fold", [P, P]), sb("trig", [P, S])
    table, ones = sb("mask_table", [P, 2, P]), sb("ones", [P, P])
    cols, powers = sb("const_cols", [P, 18]), sb("powers", [P, 2, TT])
    ident_rows, ident_two = sb("ident_rows", [CTX, 4, CTX], BF16), sb("ident_two", [CTX, 2, CTX], BF16)
    ident_bf, mask_bf = sb("ident_bf", [P, P], BF16), sb("mask_bf", [P, 2, P], BF16)
    load(nc, "constants", [(ident[:, :], a["c_ident"]), (fold[:, :], a["c_fold"]), (trig[:, :], a["c_trig"]),
                           (table[:, :, :], a["c_mask"]), (cols[:, :], a["c_cols"])])
    with phase(nc, "constants_made", "made") as (block, s):
        @block.vector
        def _(dve):
            dve.tensor_copy(ident_bf[:, :], ident[:, :]).then_inc(s["made"], 1)
            dve.tensor_copy(mask_bf[:, :, :], table[:, :, :]).then_inc(s["made"], 1)
            dve.memset(ones[:, :], 1.0).then_inc(s["made"], 1)
            for t, n in ((ident_rows, 4), (ident_two, 2)):
                for k in range(n):
                    dve.tensor_copy(t[:, k, :], ident[0:CTX, 0:CTX]).then_inc(s["made"], 1)
            dve.memset(powers[:, 0, :], -0.5).then_inc(s["made"], 1)
            dve.memset(powers[:, 1, :], 0.5).then_inc(s["made"], 1)
    K.ident, K.fold, K.trig = ident[:, :], fold[:, :], trig[:, :]
    K.ident_bf, K.mask_q, K.mask_k = ident_bf[:, :], mask_bf[:, 0, :], mask_bf[:, 1, :]
    K.ident_rows, K.ident_two = (t[:, :, :].rearrange("p a b -> p (a b)") for t in (ident_rows, ident_two))
    K.minus_half, K.half = powers[:, 0, :], powers[:, 1, :]
    K.ones, K.ones_row = ones[:, :], ones[0:1, :]
    K.zero4, K.one4, K.one_wide = cols[:, 0:4], cols[:, 4:8], cols[:, 8:12]
    K.pick = cols[:, 14:18]
    K.key = cols[:, 12:13]
    K.key_back = cols[:, 13:14]
    return K


def tensors(nc, enter):
    T = Names()

    def sb(name, shape, dt=F32):
        return enter(nc.sbuf_tensor(name, shape, dt))

    T.X = sb("main_rows", [P, TT, D])
    T.Y = sb("inner_rows", [P, TT, D])
    T.hT = sb("normed_T", [P, C, B * S])
    T.bn, T.mv = sb("bn_stats", [P, TT, 6]), sb("mean_var", [P, TT, 2])
    T.msq, T.rstd = sb("mean_square", [P, TT]), sb("rstd", [P, TT])
    banks = [enter(nc.psum_tensor(n, [P, HALF], F32)) for n in ("ring0", "ring1", "ring2")]
    T.ring = banks
    T.scores = enter(nc.psum_tensor("scores", [P, 2, 2, HALF], F32))
    T.heads_ps = enter(nc.psum_tensor("heads_ps", [P, HALF], F32))
    T.four = T.scores[:, :, :, :].rearrange("p a b c -> p (a b) c")
    return T


def attention_tensors(nc, enter, T, tag):
    def sb(name, shape, dt=F32):
        return enter(nc.sbuf_tensor(tag + "_" + name, shape, dt))

    T.stack_q, T.stack_k = sb("stack_q", [P, 2, 4, S], BF16), sb("stack_k", [P, 2, 4, S], BF16)
    T.q_slots, T.k_slots = (x[:, 0, :, :].rearrange("p j s -> p (j s)").bitcast(F32).rearrange("p (u s) -> p u s", u=2)
                            for x in (T.stack_q, T.stack_k))
    T.q_narrow, T.k_narrow = T.stack_q[:, 1, 0:2, :], T.stack_k[:, 1, 0:2, :]
    T.parts = sb("parts", [P, 2, 3, S], BF16)
    T.rest = sb("rest", [P, 2, HALF])
    T.shift_rows = sb("shift_rows", [P, S], BF16)
    T.values = sb("values", [P, B, TB, HEADS, HD + 1])
    T.values_short = T.values[:, :, :, :, :].rearrange("p b i e d -> p (b i e d)")[:, 0:B * HEADS * 32].rearrange(
        "p (b e d) -> p b e d", b=B, d=32)
    T.probs = sb("probs", [P, 2, 4, HALF])
    T.heads_sb = sb("heads_sb", [P, NH, HALF])
    T.normed = T.probs[:, :, :, :].rearrange("p u a b -> p (u a b)").rearrange("p (t d) -> p t d", d=D)
    T.denominators = sb("denominators", [P, HALF])
    T.inverses = sb("inverses", [P, 2, 16])
    T.heads_out = sb("heads_out", [P, 4, S])
    T.turned = sb("turned", [P, 2, HALF])
    T.shift = sb("shift", [P, TB, P])
    T.shift_bf = T.shift[:, :, :].rearrange("p i r -> p (i r)").bitcast(BF16)[:, 0:S].rearrange("p (i r) -> p i r", r=P)
    T.maxima = sb("maxima", [P, 2, TB, 4])


def decoder(nc, a, T, K):
    with ExitStack() as stage:
        enter = stage.enter_context

        def sb(name, shape, dt=F32):
            return enter(nc.sbuf_tensor("dec_" + name, shape, dt))

        attention_tensors(nc, enter, T, "dec")
        T.silu = T.turned
        T.ffn = T.probs[:, :, :, :].rearrange("p a b c -> p (a b) c")
        slots = sb("w_slots", [P, 4, C, 4, P])
        wv = sb("w_v", [P, 2, C, D])
        outs = sb("w_outs", [P, 2, 4, D])
        rows_flat = T.X[:, :, :].rearrange("p t d -> p (t d)")
        gate, up = (rows_flat[:, n * C * FF:(n + 1) * C * FF].rearrange("p (c f) -> p c f", c=C) for n in range(2))
        down = T.parts[:, :, :, :].rearrange("p x k s -> p (x k s)")[:, 0:2 * FT * D].bitcast(F32)
        v_bias = sb("v_bias", [P, 2, D])
        qk_bias = sb("qk_bias", [P, 2, 4])
        norms = sb("norm_scales", [P, 3, C])
        ctxT = sb("ctxT", [P, B, C, 2 * CTX])
        mask = sb("mask", [CTX, B, S], BF16)

        seg_i = T.heads_out[0:CTX, 0:2, :].bitcast(I32)
        load(nc, "decoder_in", [(ctxT[:, :, :, :], a["ctxT"]), (seg_i.rearrange("p b s -> p (b s)"), a["seg"].partition_broadcast(CTX))])
        with phase(nc, "masks", "made") as (block, s):
            @block.vector
            def _(dve):
                behind, missed = T.hT[0:CTX, 0, :], T.hT[0:CTX, 1, :]
                seg = seg_i.rearrange("p b s -> p (b s)")
                dve.tensor_scalar(behind, seg, K.key[0:CTX, :], MASKED, ALU.is_lt, ALU.mult).then_inc(s["made"], 1)
                dve.tensor_scalar(missed, seg, K.key_back[0:CTX, :], MASKED, ALU.is_ge, ALU.mult).then_inc(s["made"], 1)
                dve.wait_ge(s["made"], 2)
                dve.tensor_tensor(mask[:, :, :].rearrange("p b s -> p (b s)"), behind, missed, ALU.min)

        normalise(nc, "decoder_start", T, K, lambda i: T.X[:, i, :], TT, None, 1e-5, True,
                  write=lambda i: T.Y[:, i, :])
        with phase(nc, "no_bias", "made") as (block, s):
            @block.vector
            def _(dve):
                dve.memset(v_bias[:, 1, :], 0.0).then_inc(s["made"], 1)
        load(nc, "park", [(a["parked"], rows_flat)])

        def first_weights(at):
            return [
                (slots[:, 0:2].rearrange("p a c g s -> p (a c g s)"), at("w_slots")[:, 0:2 * C * 4 * P]),
                (wv[:, :, :, :].rearrange("p c g s -> p (c g s)"), at("w_v")),
                (outs[:, :, :, :].rearrange("p c g s -> p (c g s)"), at("w_outs")),
                (v_bias[:, 0, :], at("v_bias").partition_broadcast(P)),
                (qk_bias[:, :, :].rearrange("p c g -> p (c g)"), at("qk_bias")),
                (norms[:, :, :].rearrange("p c g -> p (c g)"), at("norm_scales"))]

        def of_layer(which):
            def at(name):
                one = a[name][which]
                return one.rearrange("o d -> (o d)") if name == "v_bias" else one.rearrange("o p x -> (o p) x")
            return at

        load(nc, "first_layer", first_weights(of_layer(slice(0, 1))))
        with nc.Fori(0, LAYERS) as layer:
            at = of_layer(bass.ds(layer, 1))
            later = [
                (slots[:, 2:4].rearrange("p a c g s -> p (a c g s)"), at("w_slots")[:, 2 * C * 4 * P:]),
                (gate.rearrange("p c f -> p (c f)"), at("w_gate")),
                (up.rearrange("p c f -> p (c f)"), at("w_up"))]
            last = [(down, at("w_down"))]
            w_self = {"q": slots[:, 0], "k": slots[:, 1], "v": wv[:, 0], "v_bias": v_bias[:, 0, :], "o": outs[:, 0],
                      "q_bias": qk_bias[:, 0], "k_bias": qk_bias[:, 1], "q_slot_bias": K.zero4, "k_slot_bias": K.zero4,
                      "pick": K.pick}
            w_cross = {"q": slots[:, 2], "k": slots[:, 3], "v": wv[:, 1], "v_bias": v_bias[:, 1, :], "o": outs[:, 1],
                       "q_slot_bias": K.zero4, "k_slot_bias": K.one4, "pick": K.pick, "mask": mask}

            def tile(i):
                return T.Y[:, i, :]

            def rows(b, i):
                return T.Y[:, b * TB + i, :]

            def tokens(b):
                return T.hT[:, :, b * S:(b + 1) * S]

            normalise(nc, "norm1", T, K, tile, TT, T.hT, 1e-6, False, (norms[:, 0, :], None))
            attention(nc, "self", T, K, "rope", tokens, tokens, w_self, 4, HD, True, S, 0.25, rows, B, later)
            normalise(nc, "norm2", T, K, tile, TT, T.hT, 1e-6, False, (norms[:, 1, :], None))
            attention(nc, "cross", T, K, "plain", tokens, lambda b: ctxT[:, b, :, :], w_cross, 4, HD, False, CTX, 0.25,
                      rows, B, last)
            normalise(nc, "norm3", T, K, tile, TT, T.hT, 1e-6, False, (norms[:, 2, :], None))
            decoder_ffn(nc, "ffn", T, {"gate": gate, "up": up, "down": down.rearrange("p (f d) -> p f d", f=FT)}, tile,
                        first_weights(of_layer(bass.ds(layer + 1, 1))))
        nf = T.hT[:, 0, 0:D]
        load(nc, "unpark", [(rows_flat, a["parked"])])
        load(nc, "last_scale", [(nf, a["nf"].partition_broadcast(P))])
        normalise(nc, "decoder_end", T, K, lambda i: T.Y[:, i, :], TT, None, 1e-6, False,
                  write=lambda i: T.Y[:, i, :])
        with phase(nc, "decoder_add", "scaled") as (block, s):
            @block.vector
            def _(dve):
                for i in range(TT):
                    dve.tensor_tensor(T.Y[:, i, :], T.Y[:, i, :], nf, ALU.mult).then_inc(s["scaled"], 1)
                for i in range(TT):
                    dve.wait_ge(s["scaled"], i + 1)
                    dve.tensor_tensor(T.X[:, i, :], T.X[:, i, :], T.Y[:, i, :], ALU.add)


def trajectories(nc, a, T, K):
    G = 128
    with ExitStack() as stage:
        enter = stage.enter_context

        def sb(name, shape, dt=F32):
            return enter(nc.sbuf_tensor("traj_" + name, shape, dt))

        diffs, weighted = sb("diffs", [P, TT, D]), sb("weighted", [P, TT, D + 1])
        guide, guide_n, guide_T = sb("guide", [P, D + 1]), sb("guide_n", [P, D]), sb("guide_T", [P, C, P])
        square = sb("square", [P, 2, D])
        likeness = sb("likeness", [P, 2, HALF])
        unit, unit_T = sb("unit", [P, 2, D]), sb("unit_T", [P, C, HALF])
        base = sb("base", [P, 2, D])
        band = sb("band", [P, 3, P])
        m = {n: sb("mag_" + n, [P, TT]) for n in "sq norm valid safe inv a ra inv2 tanh c06 c04 share".split()}
        g = {n: sb("g_" + n, [P, 1]) for n in "sq norm floor inv".split()}
        winv = sb("weight_inv", [P, TT])

        normalise(nc, "traj_norm", T, K, lambda i: T.X[:, i, :], TT, None, 1e-5, True, write=lambda i: T.Y[:, i, :])
        load(nc, "shifted", [
            (diffs[0:P - 1, :, :], T.Y[1:P, :, :]), (diffs[P - 1:P, 0:TT - 1, :], T.Y[0:1, 1:TT, :]),
            (diffs[P - 1:P, TT - 1, :], T.Y[P - 1:P, TT - 1, :]),
            (guide[:, 0:D], a["guide"]), (band[:, :, :], a["c_band"])])
        with phase(nc, "diffs", "diff squared root root_g chain tanh ones gn gt gtaken") as (block, s):
            @block.scalar
            def _(act):
                act.activation(square[:, 0, :], guide[:, 0:D], ACT.Square, accum_out=g["sq"][:, :]).then_inc(s["squared"], 1)
                for i in range(TT):
                    act.wait_ge(s["diff"], i + 1)
                    act.wait_ge(s["squared"], i + 1)
                    act.activation(square[:, 0, :], diffs[:, i, :], ACT.Square,
                                   accum_out=m["sq"][:, i:i + 1]).then_inc(s["squared"], 1)
                act.wait_ge(s["root"], 1)
                act.activation(m["tanh"][:, :], m["norm"][:, :], ACT.Tanh, scale=2.0).then_inc(s["tanh"], 1)
                for c in range(C):
                    act.wait_ge(s["gt"], c + 1)
                    act.activation(guide_T[:, c, :], T.ring[c][:, 0:P], ACT.Copy).then_inc(s["gtaken"], 1)

            @block.gpsimd
            def _(pool):
                pool.memset(guide[:, D:D + 1], 1.0).then_inc(s["ones"], 1)
                pool.wait_ge(s["squared"], 1)
                pool.tensor_tensor(g["norm"][:, :], g["sq"][:, :], K.half[:, 0:1], ALU.pow).then_inc(s["root_g"], 1)
                pool.wait_ge(s["squared"], TT + 1)
                pool.tensor_tensor(m["norm"][:, :], m["sq"][:, :], K.half, ALU.pow).then_inc(s["root"], 1)

            @block.tensor
            def _(pe):
                pe.wait_ge(s["gn"], 1)
                for c in range(C):
                    pe.transpose(T.ring[c][:, 0:P], guide_n[:, c * P:(c + 1) * P], K.ident).then_inc(s["gt"], 1)

            @block.vector
            def _(dve):
                for i in range(TT):
                    dve.tensor_tensor(diffs[:, i, :], diffs[:, i, :], T.Y[:, i, :], ALU.subtract).then_inc(s["diff"], 1)
                t = Tally(dve, s["chain"])
                dve.wait_ge(s["root_g"], 1)
                t.add(dve.tensor_scalar(g["floor"][:, :], g["norm"][:, :], 1e-8, None, ALU.max)); t.wait()
                t.add(dve.reciprocal(g["inv"][:, :], g["floor"][:, :])); t.wait()
                dve.tensor_scalar(guide_n[:, :], guide[:, 0:D], g["inv"][:, :], None, ALU.mult).then_inc(s["gn"], 1)
                dve.wait_ge(s["root"], 1)
                v = lambda n: m[n][:, :]
                t.add(dve.tensor_scalar(v("valid"), v("norm"), 1e-6, None, ALU.is_gt)); t.wait()
                t.add(dve.tensor_tensor(v("safe"), v("norm"), v("valid"), ALU.mult)); t.wait()
                t.add(dve.scalar_tensor_tensor(v("safe"), v("safe"), 1.0, v("valid"), ALU.add, ALU.subtract)); t.wait()
                t.add(dve.reciprocal(v("inv"), v("safe"))); t.wait()
                t.add(dve.tensor_tensor(v("inv"), v("inv"), v("valid"), ALU.mult)); t.wait()
                t.add(dve.tensor_tensor(v("a"), v("norm"), v("inv"), ALU.mult)); t.wait()
                t.add(dve.tensor_scalar(v("a"), v("a"), 1e-8, None, ALU.max)); t.wait()
                t.add(dve.reciprocal(v("ra"), v("a"))); t.wait()
                t.add(dve.tensor_tensor(v("inv2"), v("inv"), v("ra"), ALU.mult)); t.wait()
                dve.wait_ge(s["tanh"], 1)
                t.add(dve.scalar_tensor_tensor(v("c06"), v("inv"), 0.6, v("tanh"), ALU.mult, ALU.mult)); t.wait()
                t.add(dve.tensor_scalar(v("c04"), v("tanh"), 0.4, None, ALU.mult)); t.wait()
                t.add(dve.tensor_copy(weighted[:, :, D], v("tanh")))

        with phase(nc, "guided", "unit turned0 turned1 taken0 taken1 dots exp infl0 infl1 based share done") as (block, s):
            turned, taken, infl = (s["turned0"], s["turned1"]), (s["taken0"], s["taken1"]), (s["infl0"], s["infl1"])
            QUADS = TT // 4
            spot = lambda n: T.four[:, 2 + n % 2, 0:D + 1]

            @block.tensor
            def _(pe):
                for q in range(QUADS):
                    for i in range(4):
                        n = 4 * q + i
                        pe.wait_ge(s["unit"], n + 1)
                        for c in range(C):
                            if q and i == 0:
                                pe.wait_ge(taken[c], q)
                            t = pe.transpose(T.ring[c][:, i * P:(i + 1) * P], unit[:, n % 2, c * P:(c + 1) * P], K.ident)
                            t.then_inc(turned[c], 1)
                    if q >= 2:
                        pe.wait_ge(s["exp"], q - 1)
                    for c in range(C):
                        pe.wait_ge(taken[c], q + 1)
                    for c in range(C):
                        t = pe.matmul(T.four[:, q % 2, :], guide_T[:, c, :], unit_T[:, c, :], start=c == 0, stop=c == C - 1)
                    t.then_inc(s["dots"], 1)
                    pe.wait_ge(s["exp"], q + 1)
                    for i in range(4):
                        n = 4 * q + i
                        if n >= 2:
                            pe.wait_ge(s["done"], n - 1)
                        pe.matmul(spot(n), likeness[:, q % 2, i * P:(i + 1) * P], guide[:, :],
                                  start=True, stop=True).then_inc(infl[n % 2], 1)

            @block.scalar
            def _(act):
                for q in range(QUADS):
                    for c in range(C):
                        act.wait_ge(turned[c], 4 * q + 4)
                        if q:
                            act.wait_ge(s["dots"], q)
                        act.activation(unit_T[:, c, :], T.ring[c][:, :], ACT.Copy).then_inc(taken[c], 1)
                    act.wait_ge(s["dots"], q + 1)
                    if q >= 2:
                        act.wait_ge(infl[1], 2 * (q - 1))
                    act.activation(likeness[:, q % 2, :], T.four[:, q % 2, :], ACT.Exp, scale=2.0).then_inc(s["exp"], 1)

            @block.vector
            def _(dve):
                for q in range(QUADS):
                    for i in range(4):
                        n = 4 * q + i
                        if n >= 2:
                            dve.wait_ge(turned[1], n - 1)
                        dve.tensor_scalar(unit[:, n % 2, :], diffs[:, n, :], m["inv2"][:, n:n + 1], None,
                                          ALU.mult).then_inc(s["unit"], 1)
                    for i in range(4):
                        n = 4 * q + i
                        if n >= 2:
                            dve.wait_ge(s["done"], n - 1)
                        dve.tensor_scalar(base[:, n % 2, :], diffs[:, n, :], m["c06"][:, n:n + 1], None,
                                          ALU.mult).then_inc(s["based"], 1)
                        dve.wait_ge(infl[n % 2], n // 2 + 1)
                        dve.reciprocal(m["share"][:, n:n + 1], spot(n)[:, D:D + 1]).then_inc(s["share"], 1)
                        dve.wait_ge(s["share"], 2 * n + 1)
                        dve.tensor_tensor(m["share"][:, n:n + 1], m["share"][:, n:n + 1], m["c04"][:, n:n + 1],
                                          ALU.mult).then_inc(s["share"], 1)
                        dve.wait_ge(s["share"], 2 * n + 2)
                        dve.wait_ge(s["based"], n + 1)
                        dve.scalar_tensor_tensor(weighted[:, n, 0:D], spot(n)[:, 0:D], m["share"][:, n:n + 1],
                                                 base[:, n % 2, :], ALU.mult, ALU.add).then_inc(s["done"], 1)

        with phase(nc, "windows", "sum0 sum1 floor inverse added") as (block, s):
            full = (s["sum0"], s["sum1"])

            @block.tensor
            def _(pe):
                for n in range(TT):
                    if n >= 2:
                        pe.wait_ge(s["added"], n - 1)
                    first = n % TB == 0
                    t = pe.matmul(T.ring[n % 2][:, 0:D + 1], band[:, 0 if first else 1, :], weighted[:, n, :],
                                  start=True, stop=first)
                    if not first:
                        t = pe.matmul(T.ring[n % 2][:, 0:D + 1], band[:, 2, :], weighted[:, n - 1, :],
                                      start=False, stop=True)
                    t.then_inc(full[n % 2], 1)

            @block.vector
            def _(dve):
                for n in range(TT):
                    dve.wait_ge(full[n % 2], n // 2 + 1)
                    dve.tensor_scalar(winv[:, n:n + 1], T.ring[n % 2][:, D:D + 1], 1e-8, None,
                                      ALU.max).then_inc(s["floor"], 1)
                    dve.wait_ge(s["floor"], n + 1)
                    dve.reciprocal(winv[:, n:n + 1], winv[:, n:n + 1]).then_inc(s["inverse"], 1)
                    dve.wait_ge(s["inverse"], n + 1)
                    dve.scalar_tensor_tensor(T.X[:, n, :], T.ring[n % 2][:, 0:D], winv[:, n:n + 1], T.X[:, n, :],
                                             ALU.mult, ALU.add).then_inc(s["added"], 1)


def mixture_attention(nc, a, T, K):
    QC = NEXP * MHD
    with ExitStack() as stage:
        enter = stage.enter_context

        def sb(name, shape, dt=F32):
            return enter(nc.sbuf_tensor("mix_" + name, shape, dt))

        attention_tensors(nc, enter, T, "mix")
        T.values_wide = T.values[:, :, :, :, :].rearrange("p b i e d -> p (b i e d)")[:, 0:2 * S].rearrange(
            "p (u i c) -> p u i c", u=2, c=P)
        T.q_tok, T.k_tok = T.heads_out[:, 1, :].rearrange("p (i c) -> p i c", c=P), T.heads_out[:, 2, :].rearrange("p (i c) -> p i c", c=P)
        sim, sim_n = sb("sim", [P, C, NEXP]), sb("sim_n", [P, C, NEXP])
        sim_inv = sb("sim_inv", [P, NEXP])
        gates = sb("gates", [P, NEXP])
        proj = sb("w_mix_qkv", [P, 3, C, QC])
        w_o = sb("w_mix_o", [P, 8, D])
        mixed = T.probs[:, :, :, :].rearrange("p a b c -> p (a b c)")[:, 0:2 * QC].rearrange("p (u c) -> p u c", u=2)
        mixed_T = T.values_wide[:, :, :, :].rearrange("p a i c -> p a (i c)")
        n_sq, n_inv = sb("norm_sq", [P, TB]), sb("norm_inv", [P, TB])
        big = [sb(f"gate_{n}", [P, TB, NEXP]) for n in ("logits", "mask", "work", "sel", "left", "weights", "expd")]
        logits, mask, work, sel, left, weights, expd = big
        few = [sb(f"gate1_{n}", [P, TB]) for n in ("any", "max", "sum")]
        anyone, most, total = few
        order = sb("order", [P, TB, NEXP])
        share = T.turned[:, 0, 0:D]

        load(nc, "mixture_in", [(sim[:, :, :].rearrange("p c e -> p (c e)"), a["sim"]), (gates[:, :], a["gates"].partition_broadcast(P)),
                                (proj[:, :, :, :].rearrange("p a c e -> p (a c e)"), a["mix_qkv"]),
                                (w_o[:, :, :].rearrange("p c e -> p (c e)"), a["mix_o"]),
                                (order[:, :, :].rearrange("p c e -> p (c e)"), a["c_order"])])
        with phase(nc, "experts_norm", "squared summed root inverse chain") as (block, s):
            @block.vector
            def _(dve):
                t = Tally(dve, s["chain"])
                dve.tensor_tensor(work[:, 0:C, :], sim[:, :, :], sim[:, :, :], ALU.mult).then_inc(s["squared"], 1)
                dve.wait_ge(s["summed"], 1)
                t.add(dve.tensor_copy(sel[:, 0, :], T.ring[0][:, 0:NEXP])); t.wait()
                dve.wait_ge(s["root"], 1)
                t.add(dve.tensor_scalar(sim_inv[:, :], sim_inv[:, :], 1e-12, None, ALU.max)); t.wait()
                t.add(dve.reciprocal(sim_inv[:, :], sim_inv[:, :])); t.wait()
                for c in range(C):
                    dve.tensor_tensor(sim_n[:, c, :], sim[:, c, :], sim_inv[:, :], ALU.mult)

            @block.tensor
            def _(pe):
                pe.wait_ge(s["squared"], 1)
                for c in range(C):
                    t = pe.matmul(T.ring[0][:, 0:NEXP], K.ones, work[:, c, :], start=c == 0, stop=c == C - 1)
                t.then_inc(s["summed"], 1)

            @block.gpsimd
            def _(pool):
                pool.wait_ge(s["chain"], 1)
                pool.tensor_tensor(sim_inv[:, :], sel[:, 0, :], K.half[:, 0:NEXP], ALU.pow).then_inc(s["root"], 1)

            @block.scalar
            def _(act):
                act.activation(gates[:, :], gates[:, :], ACT.Sigmoid)

        with nc.Fori(0, B) as b:
            def rows(i):
                return T.X[:, bass.ds(b * TB + i, 1), :].rearrange("p o d -> p (o d)")

            normalise(nc, "mix_norm", T, K, rows, TB, T.hT, 1e-5, True)
            with phase(nc, "gate", "squared root inverse dots0 dots1 scaled chain exp gated") as (block, s):
                dots = (s["dots0"], s["dots1"])

                @block.scalar
                def _(act):
                    for i in range(TB):
                        if i:
                            act.wait_ge(s["squared"], i)
                        act.activation(share, T.normed[:, i, :], ACT.Square,
                                       accum_out=n_sq[:, i:i + 1]).then_inc(s["squared"], 1)
                    act.wait_ge(s["gated"], 1)
                    act.activation(expd[:, :, :], work[:, :, :], ACT.Exp).then_inc(s["exp"], 1)

                @block.gpsimd
                def _(pool):
                    pool.wait_ge(s["squared"], TB)
                    pool.tensor_tensor(n_inv[:, :], n_sq[:, :], K.half[:, 0:TB], ALU.pow).then_inc(s["root"], 1)

                @block.tensor
                def _(pe):
                    for i in range(TB):
                        if i >= 2:
                            pe.wait_ge(s["scaled"], i - 1)
                        for c in range(C):
                            t = pe.matmul(T.ring[i % 2][:, 0:NEXP], T.hT[:, c, i * P:(i + 1) * P], sim_n[:, c, :],
                                          start=c == 0, stop=c == C - 1)
                        t.then_inc(dots[i % 2], 1)

                @block.vector
                def _(dve):
                    t = Tally(dve, s["chain"])
                    step = lambda ins: (t.add(ins), t.wait())
                    across = lambda x: x[:, :].unsqueeze(2).to_broadcast([P, TB, NEXP])
                    f = lambda x: x[:, :, :]
                    dve.wait_ge(s["root"], 1)
                    step(dve.tensor_scalar(n_inv[:, :], n_inv[:, :], 1e-12, None, ALU.max))
                    step(dve.reciprocal(n_inv[:, :], n_inv[:, :]))
                    for i in range(TB):
                        dve.wait_ge(dots[i % 2], i // 2 + 1)
                        dve.scalar_tensor_tensor(logits[:, i, :], T.ring[i % 2][:, 0:NEXP], n_inv[:, i:i + 1],
                                                 gates[:, :], ALU.mult, ALU.subtract).then_inc(s["scaled"], 1)
                    dve.wait_ge(s["scaled"], TB)
                    step(dve.tensor_scalar(f(mask), f(logits), 0.0, None, ALU.is_gt))
                    step(dve.tensor_reduce(anyone[:, :], f(mask), AX.X, ALU.max))
                    step(dve.tensor_scalar(anyone[:, :], anyone[:, :], -1.0, 1.0, ALU.mult, ALU.add))
                    step(dve.tensor_copy(f(left), f(logits)))
                    for k in range(2):
                        step(dve.tensor_reduce(most[:, :], f(left), AX.X, ALU.max))
                        step(dve.tensor_tensor(f(sel), f(left), across(most), ALU.is_equal))
                        step(dve.tensor_tensor(f(sel), f(sel), f(order), ALU.mult))
                        step(dve.tensor_reduce(most[:, :], f(sel), AX.X, ALU.max))
                        step(dve.tensor_tensor(f(sel), f(order), across(most), ALU.is_equal))
                        step(dve.scalar_tensor_tensor(f(left), f(sel), -1e9, f(left), ALU.mult, ALU.add))
                        step(dve.tensor_tensor(f(sel), f(sel), across(anyone), ALU.mult))
                        step(dve.tensor_tensor(f(mask), f(mask), f(sel), ALU.add))
                    dve.tensor_scalar(f(work), f(logits), 0.0, None, ALU.max).then_inc(s["gated"], 1)
                    dve.wait_ge(s["exp"], 1)
                    step(dve.tensor_tensor(f(weights), f(expd), f(mask), ALU.mult))
                    step(dve.tensor_reduce(total[:, :], f(weights), AX.X, ALU.add))
                    step(dve.reciprocal(total[:, :], total[:, :]))
                    step(dve.tensor_tensor(f(weights), f(weights), across(total), ALU.mult))

            with phase(nc, "mix_project", "cleared full scaled0 scaled1 summed") as (block, s):
                @block.gpsimd
                def _(pool):
                    pool.memset(T.heads_out[:, 1:3, :], 0.0).then_inc(s["cleared"], 1)
                    pool.memset(T.values_wide[:, 0, :, MHD:P], 0.0).then_inc(s["cleared"], 1)
                    pool.wait_ge(s["cleared"], 2)
                    pool.memset(T.values_wide[:, 0, :, MHD:MHD + 1], 1.0).then_inc(s["cleared"], 1)

                jobs = [(i, x) for i in range(TB) for x in range(3)]

                @block.tensor
                def _(pe):
                    for n, (i, x) in enumerate(jobs):
                        if n >= 2:
                            pe.wait_ge(s["scaled0"], n - 1)
                        for h in range(2):
                            for c in range(C):
                                t = pe.matmul(T.scores[:, n % 2, h, :], T.hT[:, c, i * P:(i + 1) * P],
                                              proj[:, x, c, h * HALF:(h + 1) * HALF], start=c == 0, stop=c == C - 1)
                        t.then_inc(s["full"], 1)

                @block.vector
                def _(dve):
                    dve.wait_ge(s["cleared"], 3)
                    for n, (i, x) in enumerate(jobs):
                        dve.wait_ge(s["full"], n + 1)
                        if n >= 2:
                            dve.wait_ge(s["summed"], n - 1)
                        by = weights[:, i, :].unsqueeze(2).to_broadcast([P, NEXP, MHD])
                        dve.tensor_tensor(mixed[:, n % 2, :].rearrange("p (e d) -> p e d", d=MHD),
                                          T.scores[:, n % 2, :, :].rearrange("p h (e d) -> p (h e) d", d=MHD),
                                          by, ALU.mult).then_inc(s["scaled0"], 1)
                        dve.wait_ge(s["scaled0"], n + 1)
                        to = (T.q_tok[:, i, 0:MHD], T.k_tok[:, i, 0:MHD], T.values_wide[:, 0, i, 0:MHD])[x]
                        dve.tensor_reduce(to, mixed[:, n % 2, :].rearrange("p (e d) -> p d e", d=MHD), AX.X,
                                          ALU.add).then_inc(s["summed"], 1)

            w = {"q_slot_bias": K.zero4, "k_slot_bias": K.one_wide, "pick": K.one_wide[:, 0:1]}
            attention(nc, "mix", T, K, "given", None, None, w, 1, MHD, True, S, 0.125, None, 1)

            with phase(nc, "mix_out", "turned0 turned1 mixed spread0 spread1 copied out0 out1 added") as (block, s):
                turned, out = (s["turned0"], s["turned1"]), (s["out0"], s["out1"])

                def product(pe, k):
                    pe.wait_ge(s["copied"], k + 1)
                    if k >= 2:
                        pe.wait_ge(s["added"], k - 1)
                    for e in range(8):
                        t = pe.matmul((T.heads_ps, T.ring[2])[k % 2][:, 0:D], mixed_T[:, k % 2, e * P:(e + 1) * P],
                                      w_o[:, e, :], start=e == 0, stop=e == 7)
                    t.then_inc(out[k % 2], 1)

                @block.tensor
                def _(pe):
                    for i in range(TB + 1):
                        if i < TB:
                            if i >= 2:
                                pe.wait_ge(s["mixed"], i - 1)
                            pe.matmul(T.ring[i % 2][:, 0:P], T.heads_out[:, 0, i * P:(i + 1) * P], K.ident, start=True,
                                      stop=True).then_inc(turned[i % 2], 1)
                        if i:
                            k = i - 1
                            pe.wait_ge(s["mixed"], k + 1)
                            if k >= 2:
                                pe.wait_ge(s["copied"], k - 1)
                            for e in range(8):
                                t = pe.transpose(T.scores[:, k % 2, e // 4, (e % 4) * P:(e % 4 + 1) * P],
                                                 mixed[:, k % 2, e * P:(e + 1) * P], K.ident)
                            t.then_inc(s["spread0"], 1)
                        if i >= 2:
                            product(pe, i - 2)
                    product(pe, TB - 1)

                @block.scalar
                def _(act):
                    for i in range(TB):
                        act.wait_ge(s["spread0"], i + 1)
                        if i >= 2:
                            act.wait_ge(out[i % 2], i // 2)
                        act.activation(mixed_T[:, i % 2, :], T.scores[:, i % 2, :, :].rearrange("p a b -> p (a b)"),
                                       ACT.Copy).then_inc(s["copied"], 1)

                @block.vector
                def _(dve):
                    for i in range(TB + 2):
                        if i < TB:
                            dve.wait_ge(turned[i % 2], i // 2 + 1)
                            if i >= 2:
                                dve.wait_ge(s["spread0"], i - 1)
                            dve.tensor_tensor(mixed[:, i % 2, :].rearrange("p (e d) -> p e d", d=MHD),
                                              T.ring[i % 2][:, 0:MHD].unsqueeze(1).to_broadcast([P, NEXP, MHD]),
                                              weights[:, i, :].unsqueeze(2).to_broadcast([P, NEXP, MHD]),
                                              ALU.mult).then_inc(s["mixed"], 1)
                        if i >= 2:
                            k = i - 2
                            dve.wait_ge(out[k % 2], k // 2 + 1)
                            dve.tensor_tensor(rows(k), (T.heads_ps, T.ring[2])[k % 2][:, 0:D], rows(k), ALU.add).then_inc(s["added"], 1)


def level_one_attention(nc, a, T, K, cross):
    tag = "x1" if cross else "s1"
    with ExitStack() as stage:
        enter = stage.enter_context

        def sb(name, shape, dt=F32):
            return enter(nc.sbuf_tensor(tag + "_" + name, shape, dt))

        attention_tensors(nc, enter, T, tag)
        wq, wk = (sb("w1_" + n, [P, C, 4, P]) for n in "qk")
        wv, wo = sb("w1_v", [P, C, D]), sb("w1_o", [P, 4, D])
        v_bias, bias = sb("v1_bias", [P, D]), sb("qk1_bias", [P, 2, 4])
        affine = sb("affine", [P, 2, C])
        ctxT = sb("ctxT", [P, B, C, 2 * CTX])
        flat = lambda t: t[:, :, :, :].rearrange("p c g s -> p (c g s)")
        load(nc, tag + "_in", [
            (flat(wq), a[tag + "_q"]), (flat(wk), a[tag + "_k"]), (wv[:, :, :].rearrange("p c d -> p (c d)"), a[tag + "_v"]),
            (wo[:, :, :].rearrange("p g d -> p (g d)"), a[tag + "_o"]),
            (v_bias[:, :], a[tag + "_v_bias"].partition_broadcast(P)),
            (bias[:, :, :].rearrange("p g d -> p (g d)"), a[tag + "_bias"]),
            (affine[:, :, :].rearrange("p g d -> p (g d)"), a["s1_affine"]),
            (ctxT[:, :, :, :], a["ctxT"])])
        w = {"q": wq[:, :, :, :], "k": wk[:, :, :, :], "v": wv[:, :, :], "o": wo[:, :, :], "v_bias": v_bias[:, :],
             "q_slot_bias": bias[:, 0, :], "k_slot_bias": bias[:, 1, :], "pick": K.pick}
        if not cross:
            normalise(nc, "s1_outer", T, K, lambda i: T.X[:, i, :], TT, None, 1e-5, True, write=lambda i: T.Y[:, i, :])
        stream = T.X if cross else T.Y

        def tokens(b):
            return T.hT[:, :, b * S:(b + 1) * S]

        normalise(nc, tag + "_norm", T, K, lambda i: stream[:, i, :], TT, T.hT, 1e-5, True,
                  None if cross else (affine[:, 0, :], affine[:, 1, :]))
        attention(nc, tag, T, K, "plain", tokens, (lambda b: ctxT[:, b, :, :]) if cross else tokens, w, 4, HD, False,
                  CTX if cross else S, 0.25, lambda b, i: stream[:, b * TB + i, :], B)
        if not cross:
            with phase(nc, "s1_add", "added") as (block, s):
                @block.vector
                def _(dve):
                    for i in range(TT):
                        dve.tensor_tensor(T.X[:, i, :], T.X[:, i, :], T.Y[:, i, :], ALU.add)


def self_attention(nc, a, T, K):
    level_one_attention(nc, a, T, K, False)


def cross_attention(nc, a, T, K):
    level_one_attention(nc, a, T, K, True)


def gated_units(nc, tag, T, K, batches):
    names = "in0 in1 silu gated stats aggr floor rstd normed turned copied out0 out1 finished"
    with phase(nc, tag, names) as (block, s):
        full, out = (s["in0"], s["in1"]), (s["out0"], s["out1"])
        starts = [sum(len(x) for x in batches[:k]) for k in range(len(batches) + 1)]

        @block.tensor
        def _(pe):
            for k, batch in enumerate(batches):
                for n, u in enumerate(batch):
                    at = starts[k] + n
                    if at >= 2:
                        pe.wait_ge(s["gated"], at - 1)
                    for c in range(C):
                        pe.matmul(T.ring[at % 2][:, 0:2 * H1], u["x"][:, c, :], u["w12"][:, c, :], start=c == 0, stop=False)
                    pe.matmul(T.ring[at % 2][:, 0:2 * H1], K.ones_row, u["b12"], start=False,
                              stop=True).then_inc(full[at % 2], 1)
                for n, u in enumerate(batch):
                    at = starts[k] + n
                    pe.wait_ge(s["normed"], at + 1)
                    if at >= 4:
                        pe.wait_ge(s["copied"], at - 3)
                    pe.transpose(T.four[:, at % 4, 0:P], T.unit_rows[:, k % 2, n, :], K.ident).then_inc(s["turned"], 1)
                for n, u in enumerate(batch):
                    at = starts[k] + n
                    pe.wait_ge(s["copied"], at + 1)
                    if at >= 2:
                        pe.wait_ge(s["finished"], at - 1)
                    pe.matmul((T.heads_ps, T.ring[2])[at % 2][:, 0:D], T.unit_T[:, at % 4, :], u["w3"], start=True, stop=False)
                    pe.matmul((T.heads_ps, T.ring[2])[at % 2][:, 0:D], K.ones_row, u["b3"], start=False,
                              stop=True).then_inc(out[at % 2], 1)

        @block.scalar
        def _(act):
            for k, batch in enumerate(batches):
                for n, u in enumerate(batch):
                    at = starts[k] + n
                    act.wait_ge(full[at % 2], at // 2 + 1)
                    if at >= 2:
                        act.wait_ge(s["gated"], at - 1)
                    act.activation(T.unit_silu[:, at % 2, :], T.ring[at % 2][:, 0:H1], ACT.Silu).then_inc(s["silu"], 1)
                for n, u in enumerate(batch):
                    at = starts[k] + n
                    act.wait_ge(s["turned"], at + 1)
                    if at >= 4:
                        act.wait_ge(out[at % 2], (at - 4) // 2 + 1)
                    act.activation(T.unit_T[:, at % 4, :], T.four[:, at % 4, 0:P], ACT.Identity, scale=u["scale"],
                                   bias=u["shift"]).then_inc(s["copied"], 1)

        @block.gpsimd
        def _(pool):
            for k, batch in enumerate(batches):
                pool.wait_ge(s["floor"], k + 1)
                pool.tensor_tensor(T.rstd[:, 0:len(batch)], T.msq[:, 0:len(batch)], K.minus_half[:, 0:len(batch)],
                                   ALU.pow).then_inc(s["rstd"], 1)

        @block.vector
        def _(dve):
            for k, batch in enumerate(batches):
                for n, u in enumerate(batch):
                    at = starts[k] + n
                    dve.wait_ge(s["silu"], at + 1)
                    if k >= 2 and n == 0:
                        dve.wait_ge(s["turned"], starts[k - 1])
                    dve.tensor_tensor(T.unit_rows[:, k % 2, n, :], T.ring[at % 2][:, H1:2 * H1], T.unit_silu[:, at % 2, :],
                                      ALU.mult).then_inc(s["gated"], 1)
                for n, u in enumerate(batch):
                    dve.wait_ge(s["gated"], starts[k] + n + 1)
                    dve.bn_stats(T.bn[:, n, :], T.unit_rows[:, k % 2, n, :]).then_inc(s["stats"], 1)
                if k:
                    dve.wait_ge(s["normed"], starts[k])
                for n, u in enumerate(batch):
                    dve.wait_ge(s["stats"], starts[k] + n + 1)
                    dve.bn_aggr(T.mv[:, n, :], T.bn[:, n, :]).then_inc(s["aggr"], 1)
                dve.wait_ge(s["aggr"], starts[k + 1])
                dve.tensor_scalar(T.msq[:, 0:len(batch)], T.mv[:, 0:len(batch), 1], 1e-5, None, ALU.add).then_inc(s["floor"], 1)
                dve.wait_ge(s["rstd"], k + 1)
                for n, u in enumerate(batch):
                    dve.tensor_scalar(T.unit_rows[:, k % 2, n, :], T.unit_rows[:, k % 2, n, :], T.mv[:, n, 0:1],
                                      T.rstd[:, n:n + 1], ALU.subtract, ALU.mult).then_inc(s["normed"], 1)
                for n, u in enumerate(batch):
                    at = starts[k] + n
                    dve.wait_ge(out[at % 2], at // 2 + 1)
                    if at:
                        dve.wait_ge(s["finished"], at)
                    u["finish"](dve, (T.heads_ps, T.ring[2])[at % 2][:, 0:D]).then_inc(s["finished"], 1)


def expert_ffn(nc, a, T, K):
    with ExitStack() as stage:
        enter = stage.enter_context

        def sb(name, shape, dt=F32):
            return enter(nc.sbuf_tensor("moe_" + name, shape, dt))

        w12, b12 = sb("e_w12", [P, C, E1 + 1, 2 * H1]), sb("e_b12", [1, E1 + 1, 2 * H1])
        w3, b3 = sb("e_w3", [P, E1 + 1, D]), sb("e_b3", [1, E1 + 1, D])
        norms = sb("e_norms", [P, 4])
        wg, bg = sb("e_gate", [P, C, E1 + 1]), sb("e_gate_bias", [1, E1 + 1])
        exp_bias, order = sb("exp_bias", [P, E1]), sb("e_order", [P, NEXP])
        at_i, at_f = sb("at_int", [P, 2, M1], I32), sb("at_float", [P, 2, M1])
        col_i, col_f = sb("col_int", [P, 2, MT], I32), sb("col_float", [P, 2, MT])
        place = sb("token_number", [P, B * S])
        one_hot = sb("one_hot", [P, 2, B * S // 2])
        shared = sb("shared_rows", [P, TT, D])
        picked = sb("picked_T", [P, C, M1])
        values = sb("picked_values", [P, MT, D + 1])
        T.normed = sb("normed", [P, TB, D])
        T.unit_rows, T.unit_T, T.unit_silu = sb("unit_rows", [P, 2, 8, H1]), sb("unit_T", [P, 4, P]), sb("unit_silu", [P, 2, H1])
        score = sb("e_score", [P, MT, E1 + 1])
        names = "biased pick tmp mix expd".split()
        e = {n: sb("e_" + n, [P, MT, E1 + 1]) for n in names}
        one = {n: sb("e1_" + n, [P, MT]) for n in ("top", "sum")}
        count, keep = sb("count", [P, TT]), sb("keep", [P, TT])
        number = sb("number_by_tile", [P, TT])
        flat4 = lambda t: t[:, :, :, :].rearrange("p c e h -> p (c e h)")
        flat3 = lambda t: t[:, :, :].rearrange("p e h -> p (e h)")

        load(nc, "experts_in", [
            (flat4(w12), a["e_w12"]), (flat3(w3), a["e_w3"]), (flat3(b12), a["e_b12"]), (flat3(b3), a["e_b3"]),
            (norms[:, :], a["e_norms"]), (flat3(wg), a["e_gate"]), (bg[:, :], a["e_gate_bias"]),
            (exp_bias[:, :], a["e_bias"].partition_broadcast(P)), (order[:, :], a["c_order"][:, 0:NEXP]),
            (at_i[:, 0, :], a["index_b"].partition_broadcast(P)), (at_i[:, 1, :], a["index_t"].partition_broadcast(P)),
            (col_i[:, :, :], a["index_cols"]),
            (place[:, :], a["c_place"].partition_broadcast(P)), (number[:, :], a["c_number"])])
        normalise(nc, "experts_norm_all", T, K, lambda i: T.X[:, i, :], TT, None, 1e-5, True,
                  write=lambda i: T.Y[:, i, :])
        with phase(nc, "experts_gather", "chain hot gathered taken gates scored sig exped onecol") as (block, s):
            @block.vector
            def _(dve):
                t = Tally(dve, s["chain"])
                step = lambda ins: (t.add(ins), t.wait())
                for i, f in ((at_i, at_f), (col_i, col_f)):
                    step(dve.tensor_copy(f[:, :, :], i[:, :, :]))
                    step(dve.scalar_tensor_tensor(f[:, 0, :], f[:, 0, :], float(S), f[:, 1, :], ALU.mult, ALU.add))
                for n in range(TT):
                    if n >= 2:
                        dve.wait_ge(s["gathered"], n - 1)
                    dve.tensor_scalar(one_hot[:, n % 2, 0:M1], at_f[:, 0, :], number[:, n:n + 1], None,
                                      ALU.is_equal).then_inc(s["hot"], 1)
                dve.wait_ge(s["sig"], MT)
                f = lambda n: e[n][:, :, 0:E1]
                across = lambda x: x[:, :].unsqueeze(2).to_broadcast([P, MT, E1])
                order_all = order[:, 0:E1].unsqueeze(1).to_broadcast([P, MT, E1])
                step(dve.tensor_tensor(f("biased"), score[:, :, 0:E1], exp_bias[:, :].unsqueeze(1).to_broadcast([P, MT, E1]), ALU.add))
                step(dve.tensor_reduce(one["top"][:, :], f("biased"), AX.X, ALU.max))
                step(dve.tensor_tensor(f("pick"), f("biased"), across(one["top"]), ALU.is_equal))
                step(dve.tensor_tensor(f("pick"), f("pick"), order_all, ALU.mult))
                step(dve.tensor_reduce(one["top"][:, :], f("pick"), AX.X, ALU.max))
                step(dve.tensor_tensor(f("pick"), order_all, across(one["top"]), ALU.is_equal))
                step(dve.tensor_tensor(f("tmp"), f("pick"), score[:, :, 0:E1], ALU.mult))
                step(dve.tensor_reduce(e["mix"][:, :, 0], f("tmp"), AX.X, ALU.add))
                step(dve.tensor_copy(e["mix"][:, :, 1], score[:, :, E1]))
                dve.wait_ge(s["exped"], 1)
                step(dve.tensor_reduce(one["sum"][:, :], e["expd"][:, :, 0:2], AX.X, ALU.add))
                step(dve.reciprocal(one["sum"][:, :], one["sum"][:, :]))
                step(dve.tensor_tensor(e["mix"][:, :, 0:2], e["expd"][:, :, 0:2],
                                       one["sum"][:, :].unsqueeze(2).to_broadcast([P, MT, 2]), ALU.mult))
                step(dve.tensor_tensor(f("pick"), f("pick"), e["mix"][:, :, 0:1].to_broadcast([P, MT, E1]), ALU.mult))

            @block.tensor
            def _(pe):
                for n in range(TT):
                    pe.wait_ge(s["hot"], n + 1)
                    for c in range(C):
                        m = pe.matmul(T.four[:, c, :], T.Y[:, n, c * P:(c + 1) * P], one_hot[:, n % 2, 0:M1],
                                      start=n == 0, stop=n == TT - 1)
                    m.then_inc(s["gathered"], 1)
                pe.wait_ge(s["taken"], C)
                for n in range(MT):
                    for c in range(C):
                        pe.matmul(T.ring[0][:, n * 16:n * 16 + E1 + 1], picked[:, c, n * P:(n + 1) * P], wg[:, c, :],
                                  start=c == 0, stop=False)
                    pe.matmul(T.ring[0][:, n * 16:n * 16 + E1 + 1], K.ones_row, bg[:, :], start=False,
                              stop=True).then_inc(s["scored"], 1)

            @block.scalar
            def _(act):
                act.wait_ge(s["gathered"], TT)
                for c in range(C):
                    act.activation(picked[:, c, :], T.four[:, c, :], ACT.Copy).then_inc(s["taken"], 1)
                act.wait_ge(s["scored"], MT)
                for n in range(MT):
                    act.activation(score[:, n, :], T.ring[0][:, n * 16:n * 16 + E1 + 1], ACT.Sigmoid).then_inc(s["sig"], 1)
                act.wait_ge(s["chain"], 4 + 9)
                act.activation(e["expd"][:, :, 0:2], e["mix"][:, :, 0:2], ACT.Exp).then_inc(s["exped"], 1)

            @block.gpsimd
            def _(pool):
                pool.memset(values[:, :, D:D + 1], 1.0)

        def unit(k, x, finish):
            n = 0 if k == E1 else 2
            return {"x": x, "w12": w12[:, :, k, :], "b12": b12[:, k, :], "scale": norms[:, n:n + 1],
                    "shift": norms[:, n + 1:n + 2], "w3": w3[:, k, :], "b3": b3[:, k, :], "finish": finish}

        with nc.Fori(0, B) as b:
            def rows(i):
                return T.Y[:, bass.ds(b * TB + i, 1), :].rearrange("p o d -> p (o d)")

            def keep_shared(i):
                return lambda dve, ps: dve.tensor_copy(
                    shared[:, bass.ds(b * TB + i, 1), :].rearrange("p o d -> p (o d)"), ps)

            transposed(nc, "experts_turn", T, K, rows)
            gated_units(nc, "shared_net", T, K, [[unit(E1, T.hT[:, :, i * P:(i + 1) * P], keep_shared(i)) for i in range(TB)]])

        def first(n):
            return lambda dve, ps: dve.tensor_scalar(values[:, n, 0:D], ps, e["mix"][:, n, 1:2], None, ALU.mult)

        def more(n, k):
            return lambda dve, ps: dve.scalar_tensor_tensor(values[:, n, 0:D], ps, e["pick"][:, n, k:k + 1],
                                                            values[:, n, 0:D], ALU.mult, ALU.add)

        x_of = lambda n: picked[:, :, n * P:(n + 1) * P]
        gated_units(nc, "expert_nets", T, K, [[unit(E1, x_of(n), first(n)) for n in range(MT)]] +
                    [[unit(k, x_of(n), more(n, k)) for k in range(E1)] for n in range(MT)])
        with phase(nc, "experts_back", "hot back0 back1 counted kept scaled done") as (block, s):
            back = (s["back0"], s["back1"])

            def finish(dve, n):
                dve.wait_ge(back[n % 2], n // 2 + 1)
                ps = T.ring[n % 2]
                dve.tensor_scalar(count[:, n:n + 1], ps[:, D:D + 1], 1.0, None, ALU.max).then_inc(s["counted"], 1)
                dve.tensor_scalar(keep[:, n:n + 1], ps[:, D:D + 1], 1.0, -1.0, ALU.min, ALU.mult).then_inc(s["counted"], 1)
                dve.wait_ge(s["counted"], 2 * n + 2)
                dve.reciprocal(count[:, n:n + 1], count[:, n:n + 1]).then_inc(s["kept"], 1)
                dve.scalar_tensor_tensor(shared[:, n, :], shared[:, n, :], keep[:, n:n + 1], shared[:, n, :],
                                         ALU.mult, ALU.add).then_inc(s["kept"], 1)
                dve.wait_ge(s["kept"], 2 * n + 2)
                dve.scalar_tensor_tensor(shared[:, n, :], ps[:, 0:D], count[:, n:n + 1], shared[:, n, :], ALU.mult,
                                         ALU.add).then_inc(s["scaled"], 1)
                dve.wait_ge(s["scaled"], n + 1)
                dve.tensor_tensor(T.X[:, n, :], T.X[:, n, :], shared[:, n, :], ALU.add).then_inc(s["done"], 1)

            @block.vector
            def _(dve):
                for n in range(TT):
                    if n >= 2:
                        dve.wait_ge(back[n % 2], n // 2)
                    for m in range(MT):
                        dve.tensor_scalar(one_hot[:, n % 2, m * P:(m + 1) * P], place[:, n * P:(n + 1) * P],
                                          col_f[:, 0, m:m + 1], None, ALU.is_equal).then_inc(s["hot"], 1)
                    if n:
                        finish(dve, n - 1)
                finish(dve, TT - 1)

            @block.tensor
            def _(pe):
                for n in range(TT):
                    pe.wait_ge(s["hot"], MT * (n + 1))
                    if n >= 2:
                        pe.wait_ge(s["scaled"], n - 1)
                    for m in range(MT):
                        t = pe.matmul(T.ring[n % 2][:, 0:D + 1], one_hot[:, n % 2, m * P:(m + 1) * P], values[:, m, :],
                                      start=m == 0, stop=m == MT - 1)
                    t.then_inc(back[n % 2], 1)


def transposed(nc, tag, T, K, rows):
    with phase(nc, tag, "staged turned0 turned1 taken0 taken1") as (block, s):
        turned, taken = (s["turned0"], s["turned1"]), (s["taken0"], s["taken1"])

        @block.vector
        def _(dve):
            for i in range(TB):
                dve.tensor_copy(T.normed[:, i, :], rows(i)).then_inc(s["staged"], 1)

        @block.tensor
        def _(pe):
            for q in range(NH):
                pe.wait_ge(s["staged"], 4 * q + 4)
                for c in range(C):
                    if q:
                        pe.wait_ge(taken[c], q)
                    for i in range(4):
                        m = pe.transpose(T.ring[c][:, i * P:(i + 1) * P], T.normed[:, 4 * q + i, c * P:(c + 1) * P], K.ident)
                    m.then_inc(turned[c], 1)

        @block.scalar
        def _(act):
            for q in range(NH):
                for c in range(C):
                    act.wait_ge(turned[c], q + 1)
                    act.activation(T.hT[:, c, q * HALF:(q + 1) * HALF], T.ring[c][:, :], ACT.Copy).then_inc(taken[c], 1)


def program(nc, a, out, stages):
    with ExitStack() as ctx:
        K = constants(nc, ctx.enter_context, a)
        T = tensors(nc, ctx.enter_context)
        load(nc, "x_in", [(T.X[:, b * TB:(b + 1) * TB, :], a["x"][b].rearrange("(t p) d -> p t d", p=P)) for b in range(B)])
        if "traj" in stages:
            trajectories(nc, a, T, K)
        if "decoder" in stages:
            decoder(nc, a, T, K)
        if "mixture" in stages:
            mixture_attention(nc, a, T, K)
        if "self" in stages:
            self_attention(nc, a, T, K)
        if "cross" in stages:
            cross_attention(nc, a, T, K)
        if "moe" in stages:
            expert_ffn(nc, a, T, K)
        with phase(nc, "x_out", "stored") as (block, s):
            @block.sync
            def _(sync):
                for b in range(B):
                    sync.dma_start(out[b].rearrange("(t p) d -> p t d", p=P),
                                   T.X[:, b * TB:(b + 1) * TB, :]).then_inc(s["stored"], 16)
                sync.wait_ge(s["stored"], 16 * B)


def _chunks(w):
    return np.ascontiguousarray(w.reshape(-1, P, w.shape[1]).transpose(1, 0, 2).reshape(P, -1))


def _slots(w, turned=False):
    o = np.zeros((HEADS, 32) + w.shape[1:], w.dtype)
    r = w.reshape((HEADS, HD) + w.shape[1:])
    o[:, 0:HD] = r
    if turned:
        o[:, HD:HD + 8], o[:, HD + 8:2 * HD] = r[:, 8:16], r[:, 0:8]
    return o.reshape((4 * P,) + w.shape[1:])


def _w_slots(w, turned=False):
    return _chunks(_slots(w, turned).T)


def _out_slots(w, bias=None):
    o = _slots(w)
    if bias is not None:
        o[HD] = bias
    return np.ascontiguousarray(o.reshape(4, P, D).transpose(1, 0, 2).reshape(P, 4 * D))


def _columns(bias, turned=False):
    return np.ascontiguousarray(_slots(bias, turned).reshape(4, P).T)


def _by_feature(v):
    return np.ascontiguousarray(v.reshape(C, P).T)


def _tables():
    f = np.float32
    ident = np.eye(P, dtype=f)
    fold = np.zeros((P, P), f)
    trig, cols = np.zeros((P, S), f), np.zeros((P, 18), f)
    inv = (1.0 / f(10000.0) ** (np.arange(0, HD, 2, dtype=f) / f(HD))).astype(f)
    angle = np.arange(S, dtype=f)[:, None] * inv[None, :]
    cos, sin = np.cos(angle), np.sin(angle)
    for j in range(4):
        for d in range(HD):
            fold[32 * j + d, 32 * j + d] = fold[32 * j + HD + d, 32 * j + d] = 1
            trig[32 * j + d] = cos[:, d % 8]
            trig[32 * j + HD + d] = sin[:, d % 8] * (-1 if d < 8 else 1)
        cols[32 * j + HD, 4:8] = 1
    cols[MHD, 8:12] = 1
    for j in range(4):
        cols[32 * j + HD, 14 + j] = 1
    cols[:, 12], cols[:, 13] = np.arange(P), np.arange(P) + LOOKBACK
    q, k = np.arange(P)[:, None], np.arange(P)[None, :]
    mask = np.stack([np.where(k > q, f(MASKED), f(0)), np.where(q > k, f(MASKED), f(0))], 1).astype(f)
    band = np.zeros((P, 3, P), f)
    for pos in range(2 * P):
        n = min(pos, WINDOW)
        for j in range(n):
            idx = pos - n + j
            v = f(0.1) + f(0.9) * f(j) / f(max(n - 1, 1)) if n > 1 else f(0.1)
            if pos < P:
                band[idx, 0, pos] = v
            elif idx >= P:
                band[idx - P, 1, pos - P] = v
            else:
                band[idx, 2, pos - P] = v
    order = np.tile(np.arange(NEXP, 0, -1, dtype=f), (P, TB))
    place = np.arange(B * S, dtype=f)
    return {"c_place": place, "c_number": np.ascontiguousarray(place.reshape(TT, P).T), "c_band": band, "c_order": order, "c_ident": ident, "c_fold": fold, "c_trig": trig,
            "c_mask": mask, "c_cols": cols}


def layouts(i):
    g = {k: np.asarray(v) for k, v in i.items()}
    a = dict(_tables())
    a["x"] = g["x"]
    ctx = g["ctx_1024"].reshape(B, CTX, C, P).transpose(3, 0, 2, 1)
    a["ctxT"] = np.concatenate([ctx, ctx], -1)
    a["seg"] = g["itok_BxS_0_255"].reshape(B * S)
    n = "L0_xattn_"
    qkv, bqkv = g[n + "Wqkv"], g[n + "bqkv"]
    kv = g[n + "Wkv_c"]
    a["nf"] = g[n + "nf"]
    a["w_slots"] = np.stack([np.concatenate([
        _w_slots(qkv[l, 0:D], True), _w_slots(qkv[l, D:2 * D], True),
        _w_slots(g[n + "Wq_c"][l]), _w_slots(kv[l, 0:D])], 1) for l in range(LAYERS)])
    a["w_v"] = np.stack([np.concatenate([_chunks(qkv[l, 2 * D:].T), _chunks(kv[l, D:].T)], 1) for l in range(LAYERS)])
    a["w_outs"] = np.stack([np.concatenate([_out_slots(g[n + "Wo"][l].T, g[n + "bo"][l]),
                                            _out_slots(g[n + "Wo_c"][l].T)], 1) for l in range(LAYERS)])
    a["v_bias"] = bqkv[:, 2 * D:]
    a["qk_bias"] = np.stack([np.concatenate([_columns(bqkv[l, 0:D], True), _columns(bqkv[l, D:2 * D], True)], 1)
                             for l in range(LAYERS)])
    a["norm_scales"] = np.stack([np.concatenate([_by_feature(g[n + m][l]) for m in ("n1", "n2", "n3")], 1)
                                 for l in range(LAYERS)])
    for name in ("w_slots", "w_v", "w_outs", "v_bias", "qk_bias", "norm_scales"):
        a[name] = np.concatenate([a[name], a[name][0:1]])
    a["w_gate"] = np.stack([_chunks(g[n + "Wg"][l].T) for l in range(LAYERS)])
    a["w_up"] = np.stack([_chunks(g[n + "Wu"][l].T) for l in range(LAYERS)])
    a["w_down"] = np.stack([_chunks(g[n + "Wd"][l].T) for l in range(LAYERS)])
    a["guide"] = g["L0_attn_guidance_trajectories"]
    n = "L0_ffn_"
    a["sim"], a["gates"] = _chunks(g[n + "sim_matrix"]), g[n + "gates"]
    wide = lambda w: _chunks(w.transpose(1, 0, 2).reshape(D, NEXP * MHD))
    a["mix_qkv"] = np.concatenate([wide(g[n + m]) for m in ("q_proj", "k_proj", "v_proj")], 1)
    a["mix_o"] = _chunks(g[n + "o_proj"].reshape(NEXP * MHD, D))
    n = "L1_attn_"
    wt, bias = g[n + "w_qkv"].T, g[n + "b_qkv"]
    parts = {"s1": (wt[0:D], wt[D:2 * D], wt[2 * D:], g[n + "w_out"], bias[0:D], bias[D:2 * D], bias[2 * D:], g[n + "b_out"])}
    a["s1_affine"] = np.concatenate([_by_feature(g[n + "ln_gamma"]), _by_feature(g[n + "ln_beta"])], 1)
    n = "L1_xattn_"
    parts["x1"] = (g[n + "Wq"].T, g[n + "Wk"].T, g[n + "Wv"].T, g[n + "Wo"], g[n + "b_q"], g[n + "b_k"], g[n + "b_v"],
                   g[n + "b_o"])
    for tag, (q, k, v, o, bq, bk, bv, bo) in parts.items():
        a[tag + "_q"], a[tag + "_k"], a[tag + "_v"] = _w_slots(q), _w_slots(k), _chunks(v.T)
        a[tag + "_o"], a[tag + "_v_bias"] = _out_slots(o, bo), bv
        k_cols = _columns(bk)
        if tag == "x1":
            k_cols[HD::32] = 1
        a[tag + "_bias"] = np.concatenate([_columns(bq), k_cols], 1)
    n = "L1_ffn_"
    both = lambda w1, w2: np.concatenate([w1, w2], -2).transpose(0, 2, 1)
    w12 = np.concatenate([both(g[n + "ew1"], g[n + "ew2"]), both(g[n + "sw1"][None], g[n + "sw2"][None])], 0)
    a["e_w12"] = w12.reshape(E1 + 1, C, P, 2 * H1).transpose(2, 1, 0, 3).reshape(P, -1)
    a["e_b12"] = np.concatenate([np.concatenate([g[n + "eb1"], g[n + "eb2"]], 1).reshape(-1), g[n + "sb1"], g[n + "sb2"]])[None]
    a["e_w3"] = np.concatenate([g[n + "ew3"], g[n + "sw3"][None]], 0).transpose(2, 0, 1).reshape(P, -1)
    a["e_b3"] = np.concatenate([g[n + "eb3"].reshape(-1), g[n + "sb3"]])[None]
    a["e_norms"] = np.stack([g[n + m] for m in ("s_ln_g", "s_ln_b", "sel_ln_g", "sel_ln_b")], 1)
    a["e_gate"] = _chunks(np.concatenate([g[n + "eg_w"], g[n + "sg_w"]], 0).T)
    a["e_gate_bias"] = np.concatenate([g[n + "eg_b"], g[n + "sg_b"]])[None]
    a["e_bias"] = g[n + "exp_bias"]
    a["index_b"], a["index_t"] = g[n + "index_b"], g[n + "index_t"]
    a["index_cols"] = np.stack([g[n + m].reshape(MT, P).T for m in ("index_b", "index_t")], 1)
    return a


STAGES = ("traj", "decoder", "mixture", "self", "cross", "moe")


def declare(nc, arrays, stages=STAGES):
    args = {k: nc.dram_tensor(f"in_{k}", v.shape, mybir.dt.from_np(v.dtype), kind="ExternalInput").ap()
            for k, v in arrays.items()}
    args["parked"] = nc.dram_tensor("parked", (P, TT * D), F32, kind="Internal").ap()
    out = nc.dram_tensor("out", (B, S, D), F32, kind="ExternalOutput").ap()
    program(nc, args, out, stages)


def kernel(**inputs):
    import concourse.bacc as bacc
    from concourse.bass_utils import run_bass_kernel_spmd

    arrays = {k: np.ascontiguousarray(v) for k, v in layouts(inputs).items()}
    nc = bacc.Bacc("TRN2", target_bir_lowering=False, num_devices=1)
    declare(nc, arrays)
    r = run_bass_kernel_spmd(nc, [{f"in_{k}": v for k, v in arrays.items()}], core_ids=[0])
    return r.results[0]["out"]
```
